# Optimizing a Trainium2 kernel written in Bass

```python
import numpy as np
import jax
import jax.numpy as jnp

def _softmax(x, axis=-1):
    return jax.nn.softmax(x, axis=axis)

def _gelu(x):
    return jax.nn.gelu(x, approximate=True)

def _silu(x):
    return jax.nn.silu(x)

def _sigmoid(x):
    return jax.nn.sigmoid(x)

def _layernorm(x, axis=-1, eps=1e-05):
    m = jnp.mean(x, axis=axis, keepdims=True)
    v = jnp.var(x, axis=axis, keepdims=True)
    return (x - m) / jnp.sqrt(v + eps)

def _scatter_add(tgt, idx, src, axis=0):
    return tgt.at[idx].add(src)

def _segment_sum(src, seg, n):
    return jax.ops.segment_sum(src, seg, n)
kernel_name = 'mk_gnn_preln_d2_gnn_r32_1cb998'

def setup_inputs(seed: int=0):
    np.random.seed(seed)
    _w = jnp.asarray

    def _rec_inputs():
        import jax
        import jax.numpy as jnp
        _gk = jax.random.key(seed)
        x = -0.000202 + 1 * jax.random.normal(jax.random.fold_in(_gk, 1), (50000, 64), jnp.float32)
        src = jax.random.randint(jax.random.fold_in(_gk, 2), (50000,), 0, 50000, jnp.int32)
        dst = jax.random.randint(jax.random.fold_in(_gk, 3), (50000,), 0, 50000, jnp.int32)
        _o = jnp.argsort(dst, stable=True)
        src = src[_o]
        dst = dst[_o]
        edge_attr_16 = 0.000254156 + 0.999948 * jax.random.normal(jax.random.fold_in(_gk, 11), (50000, 16), jnp.float32)
        edge_weight = jax.random.uniform(jax.random.fold_in(_gk, 13), (50000,), jnp.float32, 0.0, 1)
        return (x, src, dst, edge_attr_16, edge_weight)
    x, src, dst, edge_attr_16, edge_weight = _rec_inputs()

    def _L0_gnn_setup():
        import jax, jax.numpy as jnp
        import numpy as np
        NUM_LAYERS = 3
        key = jax.random.key(seed)
        k1, k2, k3 = jax.random.split(key, 3)
        N, D, E = (3125, 64, 1250000)
        emb = jax.random.normal(k1, (N, D), dtype=jnp.float32)
        edge_attr = jax.random.uniform(k2, (E,), dtype=jnp.float32)
        edge_index = jax.random.randint(k3, (2, E), 0, N, dtype=jnp.int64)
        return {'emb': emb, 'edge_attr': edge_attr, 'edge_index': edge_index}
    _L0_gnn_all = _L0_gnn_setup()
    _L0_gnn_in = {k: v for k, v in _L0_gnn_all.items() if k in ()}
    del _L0_gnn_all

    def _L1_gnn_setup():
        import jax, jax.numpy as jnp
        import numpy as np
        N, E, D, ED = (50000, 25000, 64, 16)
        H1 = 2 * D + ED

        def _forward(x, edge_weights, W_att1, b_att1, W_att2, b_att2, W_lin, b_lin, W_ih, b_ih, W_hh, b_hh, edge_idx):
            num_nodes = x.shape[0]
            src = edge_idx[0]
            dst = edge_idx[1]
            lin_x = x @ W_lin.T + b_lin
            feat = jnp.concatenate([x[src], edge_weights, x[dst]], axis=1)
            h = jax.nn.relu(feat @ W_att1.T + b_att1)
            scores = (h @ W_att2.T + b_att2)[:, 0]
            m = jax.ops.segment_max(scores, src, num_segments=num_nodes)
            e = jnp.exp(scores - m[src])
            denom = jax.ops.segment_sum(e, src, num_segments=num_nodes)
            alpha = e / denom[src]
            msg = jax.ops.segment_sum(alpha[:, None] * lin_x[dst], src, num_segments=num_nodes)
            gi = x @ W_ih.T + b_ih
            gh = msg @ W_hh.T + b_hh
            i_r, i_z, i_n = jnp.split(gi, 3, axis=1)
            h_r, h_z, h_n = jnp.split(gh, 3, axis=1)
            r = jax.nn.sigmoid(i_r + h_r)
            z = jax.nn.sigmoid(i_z + h_z)
            n = jnp.tanh(i_n + r * h_n)
            new_h = (1.0 - z) * n + z * msg
            deg = jax.ops.segment_sum(jnp.ones_like(scores), src, num_segments=num_nodes)
            return jnp.where(deg[:, None] > 0, new_h, x)
        key = jax.random.key(seed)
        ks = jax.random.split(key, 16)
        s = 0.05
        inp = {'x': jax.random.normal(ks[0], (N, D), jnp.float32), 'edge_idx': jax.random.randint(ks[1], (2, E), 0, N, jnp.int64), 'edge_weights': jax.random.normal(ks[2], (E, ED), jnp.float32), 'W_att1': jax.random.normal(ks[3], (H1, H1), jnp.float32) * s, 'b_att1': jnp.zeros((H1,), jnp.float32), 'W_att2': jax.random.normal(ks[4], (1, H1), jnp.float32) * s, 'b_att2': jnp.zeros((1,), jnp.float32), 'W_lin': jax.random.normal(ks[5], (D, D), jnp.float32) * s, 'b_lin': jnp.zeros((D,), jnp.float32), 'W_ih': jax.random.normal(ks[6], (3 * D, D), jnp.float32) * s, 'b_ih': jnp.zeros((3 * D,), jnp.float32), 'W_hh': jax.random.normal(ks[7], (3 * D, D), jnp.float32) * s, 'b_hh': jnp.zeros((3 * D,), jnp.float32)}
        return inp
    _L1_gnn_all = _L1_gnn_setup()
    _L1_gnn_in = {k: v for k, v in _L1_gnn_all.items() if k in ('W_att1', 'b_att1', 'W_att2', 'b_att2', 'W_lin', 'b_lin', 'W_ih', 'b_ih', 'W_hh', 'b_hh')}
    del _L1_gnn_all
    return {'x': x, 'src': src, 'dst': dst, 'edge_attr_16': edge_attr_16, 'edge_weight': edge_weight, 'L1_gnn_W_att1': _L1_gnn_in['W_att1'], 'L1_gnn_b_att1': _L1_gnn_in['b_att1'], 'L1_gnn_W_att2': _L1_gnn_in['W_att2'], 'L1_gnn_b_att2': _L1_gnn_in['b_att2'], 'L1_gnn_W_lin': _L1_gnn_in['W_lin'], 'L1_gnn_b_lin': _L1_gnn_in['b_lin'], 'L1_gnn_W_ih': _L1_gnn_in['W_ih'], 'L1_gnn_b_ih': _L1_gnn_in['b_ih'], 'L1_gnn_W_hh': _L1_gnn_in['W_hh'], 'L1_gnn_b_hh': _L1_gnn_in['b_hh']}

def reference(x, src, dst, edge_attr_16, edge_weight, L1_gnn_W_att1, L1_gnn_b_att1, L1_gnn_W_att2, L1_gnn_b_att2, L1_gnn_W_lin, L1_gnn_b_lin, L1_gnn_W_ih, L1_gnn_b_ih, L1_gnn_W_hh, L1_gnn_b_hh):
    import jax
    import jax.numpy as jnp

    def _L0_gnn_ref(emb, edge_attr, edge_index):
        import jax, jax.numpy as jnp
        import numpy as np
        NUM_LAYERS = 3
        N = emb.shape[0]
        src, dst = (edge_index[0], edge_index[1])
        deg = jax.ops.segment_sum(edge_attr, dst, num_segments=N)
        dinv = jnp.where(deg > 0, jax.lax.rsqrt(deg), 0.0)
        w = dinv[src] * edge_attr * dinv[dst]
        alpha = jnp.float32(1.0 / (NUM_LAYERS + 1))
        x = emb
        out = x * alpha
        for _ in range(NUM_LAYERS):
            msgs = x[src] * w[:, None]
            x = jax.ops.segment_sum(msgs, dst, num_segments=N)
            out = out + x * alpha
        return out

    def _L1_gnn_ref(x, edge_idx, edge_weights, W_att1, b_att1, W_att2, b_att2, W_lin, b_lin, W_ih, b_ih, W_hh, b_hh):
        import jax, jax.numpy as jnp
        import numpy as np
        N, E, D, ED = (50000, 25000, 64, 16)
        H1 = 2 * D + ED

        def _forward(x, edge_weights, W_att1, b_att1, W_att2, b_att2, W_lin, b_lin, W_ih, b_ih, W_hh, b_hh, edge_idx):
            num_nodes = x.shape[0]
            src = edge_idx[0]
            dst = edge_idx[1]
            lin_x = x @ W_lin.T + b_lin
            feat = jnp.concatenate([x[src], edge_weights, x[dst]], axis=1)
            h = jax.nn.relu(feat @ W_att1.T + b_att1)
            scores = (h @ W_att2.T + b_att2)[:, 0]
            m = jax.ops.segment_max(scores, src, num_segments=num_nodes)
            e = jnp.exp(scores - m[src])
            denom = jax.ops.segment_sum(e, src, num_segments=num_nodes)
            alpha = e / denom[src]
            msg = jax.ops.segment_sum(alpha[:, None] * lin_x[dst], src, num_segments=num_nodes)
            gi = x @ W_ih.T + b_ih
            gh = msg @ W_hh.T + b_hh
            i_r, i_z, i_n = jnp.split(gi, 3, axis=1)
            h_r, h_z, h_n = jnp.split(gh, 3, axis=1)
            r = jax.nn.sigmoid(i_r + h_r)
            z = jax.nn.sigmoid(i_z + h_z)
            n = jnp.tanh(i_n + r * h_n)
            new_h = (1.0 - z) * n + z * msg
            deg = jax.ops.segment_sum(jnp.ones_like(scores), src, num_segments=num_nodes)
            return jnp.where(deg[:, None] > 0, new_h, x)
        return _forward(x, edge_weights, W_att1, b_att1, W_att2, b_att2, W_lin, b_lin, W_ih, b_ih, W_hh, b_hh, edge_idx)
    edge_index = jnp.stack([src, dst])
    h = jnp.maximum(_layernorm(x, axis=-1), 0.0)
    x = x + _L0_gnn_ref(h, edge_weight, edge_index)
    h = jnp.maximum(_layernorm(x, axis=-1), 0.0)
    x = x + _L1_gnn_ref(h, edge_index, edge_attr_16, L1_gnn_W_att1, L1_gnn_b_att1, L1_gnn_W_att2, L1_gnn_b_att2, L1_gnn_W_lin, L1_gnn_b_lin, L1_gnn_W_ih, L1_gnn_b_ih, L1_gnn_W_hh, L1_gnn_b_hh)
    return x

_drawn_inputs = setup_inputs


def setup_inputs(seed=0):
    import zlib

    import numpy as np

    out = dict(_drawn_inputs(seed))
    spreads = {'L1_gnn_b_att1': (0.0, 0.8),
     'L1_gnn_b_lin': (0.0, 0.285),
     'L1_gnn_b_ih': (0.0, 0.297),
     'L1_gnn_b_hh': (0.0, 0.573)}
    factors = {'edge_attr_16': 8.0, 'L1_gnn_W_att1': 8.0, 'L1_gnn_W_att2': 8.0, 'L1_gnn_W_hh': 3.42}
    for name, (base, spread) in spreads.items():
        noise = np.random.default_rng([zlib.crc32(name.encode()), seed]).standard_normal(out[name].shape)
        drawn = base * np.exp(spread * noise) if base else spread * noise
        out[name] = jnp.asarray(drawn.astype(out[name].dtype))
    for name, factor in factors.items():
        out[name] = (out[name] * factor).astype(out[name].dtype)
    return out
```

```python
from contextlib import ExitStack

import concourse.bass as bass
from concourse import mybir

F32 = mybir.dt.float32
I32 = mybir.dt.int32
U32 = mybir.dt.uint32
ALU = mybir.AluOpType
ACT = mybir.ActivationFunctionType
AX = mybir.AxisListType

P = 128
N = 50000
E = 50000
D = 64
ED = 16
H1 = 2 * D + ED
J = 392
NP = P * J
B = 7
NB = J // B
IT = NB // 2
FULL = N // J
REST = N - FULL * J
ROW_FIX = NP
ROW_ZERO = NP + P
ROWS = NP + 2 * P
PAD_KEY = 60000
OOB = 1000000.0
BIG = 1.0e30
TINY = 2.0 ** -116
EXP_MIN = -200.0
EPS = 1e-5
SORT = P * 512
SORT0 = SORT - NP


def build(nc, x, src, dst, edge_attr, edge_weight, W_att1, b_att1, W_att2, b_att2, W_lin, b_lin,
          W_ih, b_ih, W_hh, b_hh, out):
    with ExitStack() as ctx:
        def sb(name, shape, dt=F32):
            return ctx.enter_context(nc.sbuf_tensor(name, shape, dt))

        def sem(name):
            return ctx.enter_context(nc.semaphore(name))

        def dram(name, shape, dt=F32):
            return nc.dram_tensor(name, shape, dt, kind="Internal").ap()

        t_place = dram("t_place", [NP, 2])
        t_h = dram("t_h", [NP, D + 2])
        t_xa = dram("t_xa", [NP, D])
        t_u = [dram(f"t_u{k}", [ROWS, D]) for k in range(3)]
        t_sorted = dram("t_sorted", [SORT, 1], I32)
        t_edge = dram("t_edge", [NP, ED + 1])
        t_x2 = dram("t_x2", [NP, D])
        t_h2 = dram("t_h2", [NP, D])
        t_msg = dram("t_msg", [NP, D + 1])
        t_last = dram("t_last", [1, J * D])

        def rows(t):
            return t[0:NP, :].rearrange("(p j) f -> p (j f)", j=J)

        big = sb("big", [P, J * D])
        edge_s = sb("edge_s", [P, J * (ED + 1)])
        key_d = sb("key_d", [P, J + 2], I32)
        key_s = key_d
        src_i = sb("src_i", [P, J + 2 * B], I32)
        ew = sb("ew", [P, J])
        keep_d = sb("keep_d", [P, J])
        end_d = sb("end_d", [P, J])
        dinv = sb("dinv", [P, J])
        w_e = sb("w_e", [P, J])
        row_i = sb("row_i", [P, J + 2 * B], I32)
        place_v = sb("place_v", [P, J * 2])
        node_v = place_v
        node_i = src_i
        start_s = sb("start_s", [P, J])
        end_s = sb("end_s", [P, J])
        srcs_i = sb("srcs_i", [P, J + 2 * B], I32)
        dsts_i = sb("dsts_i", [P, J + 2 * B], I32)
        place_i = dsts_i
        perm_i = sb("perm_i", [P, J + 2 * B], I32)
        scat_i = sb("scat_i", [P, J + 2 * B], I32)
        m_all = sb("m_all", [P, 1 + J])
        tile_a = sb("tile_a", [P, J + 2])
        tile_b = sb("tile_b", [P, J + 2])
        tile_c = sb("tile_c", [P, J + 2])
        tile_d = sb("tile_d", [P, J + 2])
        rstd = w_e
        shift = m_all
        work = sb("work", [P, 6 * 512])
        sx = [work[:, k * 512:(k + 1) * 512] for k in range(2)]
        kx = work[:, 1024:1536].bitcast(I32)
        mask = work[:, 1536:2048].bitcast(U32)
        gray = work[:, 2048:2560].bitcast(U32)
        lin_i = work[:, 2560:3072].bitcast(U32)
        stats = edge_s[:, 0:6 * J]
        ident = sb("ident", [P, P])
        ones = sb("ones", [P, P])
        cols = sb("cols", [P, 40])
        pos = m_all[:, 0:J]
        fixrow = sb("fixrow", [P, 1])
        fix_i = sb("fix_i", [P, 1], I32)
        st = [sb(f"st{h}", [P, 2 * B], I32) for h in range(2)]
        sst = [sb(f"sst{h}", [P, B], I32) for h in range(2)]
        ea7 = [work[:, 1792 + h * B * ED:1792 + (h + 1) * B * ED] for h in range(2)]
        eaT = [work[0:B * ED, 2016 + h * P:2016 + (h + 1) * P] for h in range(2)]
        ftS = [work[:, h * B * P:(h + 1) * B * P] for h in range(2)]
        q14 = [sb(f"q14_{h}", [P, 2 * B]) for h in range(2)]
        e14 = [sb(f"e14_{h}", [P, 2 * B]) for h in range(2)]
        score = [sb(f"score{h}", [P, B]) for h in range(2)]
        sv = [sb(f"sv{h}", [P, 2 * B]) for h in range(2)]
        G = [sb(f"G{h}", [P, B * 128]) for h in range(2)]
        V = [sb(f"V{h}", [P, B * (D + 1)]) for h in range(2)]
        zrow = V[1][:, :]
        R = [sb(f"R{h}", [P, B * (D + 1)]) for h in range(2)]
        O = [sb(f"O{h}", [P, B * (D + 2)]) for h in range(2)]
        O2 = [sb(f"O2{h}", [P, B * D]) for h in range(2)]
        F = sb("F", [P, D + 1])
        q7 = [[sb(f"q7_{h}_{k}", [P, B]) for k in range(6)] for h in range(2)]
        st6 = [sb(f"st6_{h}", [P, B * 6]) for h in range(2)]
        row1 = sb("row1", [1, 3 * (P + 1)])
        row2 = sb("row2", [1, 2 * P])
        cT = sb("cT", [D + 1, P])
        co = sb("co", [D + 1, P + 1])
        fixr = sb("fixr", [P, D + 1])
        cbc = sb("cbc", [P, D + 1])
        wcat = G[1][:, 0:256].rearrange("p (k w) -> p k w", k=2)
        wea = G[1][:, 256:288].rearrange("p (k w) -> p k w", k=2)
        wih = G[1][:, 288:416].rearrange("p (k w) -> p k w", k=2)
        whh = G[1][:, 416:544].rearrange("p (k w) -> p k w", k=2)
        wlin = G[1][0:D, 544:672]
        whhT = G[1][0:D, 672:864]
        bcol = sb("bcol", [D, 1])
        rhs1 = sb("rhs1", [P, H1])
        rhs_e = sb("rhs_e", [B * ED, B * H1])
        w1e = sb("w1e", [ED, H1])
        b1row = sb("b1row", [1, H1])
        w2bc = sb("w2bc", [P, H1])
        bias_n = sb("bias_n", [P, 5 * D])
        brow = O2[1][0:1, :]
        nrow = O2[0][0:1, 0:5 * D]
        rowt = O[0][0:1, 3 * D:3 * D + H1]
        hrow = O[0][0:1, 0:3 * D]
        rhs_n = sb("rhs_n", [P, 5 * D])
        hh = [[big[:, (h * B + i) * H1:(h * B + i + 1) * H1] for i in range(B)] for h in range(2)]
        b2c = sb("b2c", [P, 1])

        ps = [ctx.enter_context(nc.psum_tensor(f"ps{k}", [P, 512], F32)) for k in range(8)]
        psT, psH, psE, psC = ps[0:2], ps[2:5], ps[5], ps[6]

        pads = sem("pads")
        pool_pads = sem("pool_pads")
        consts = sem("consts")
        ld_dst, ld_src, ld_ew, ld_x = sem("ld_dst"), sem("ld_src"), sem("ld_ew"), sem("ld_x")
        ld_ea, ld_key, ld_w, ld_node, ld_sorted = sem("ld_ea"), sem("ld_key"), sem("ld_w"), sem("ld_node"), sem("ld_sorted")
        zeroed = sem("zeroed")
        place_set = sem("place_set")
        place_pads = sem("place_pads")
        edge_ready = sem("edge_ready")
        edge_stored = sem("edge_stored")
        dv = sem("dv")
        ask = sem("ask")
        given = sem("given")
        sq_ask, sq_given = sem("sq_ask"), sem("sq_given")
        place_ready = sem("place_ready")
        sort_done = sem("sort_done")
        order_s = sem("order_s")
        node_ready = sem("node_ready")
        fix_ready = [sem(f"fix_ready{k}") for k in range(4)]
        fix_stored = [sem(f"fix_stored{k}") for k in range(4)]
        w_step = sem("w_step")
        w_copied = sem("w_copied")
        w_bias = sem("w_bias")
        w_done = sem("w_done")
        zset = sem("zset")
        nodes_listed = sem("nodes_listed")
        rhs_zero, e_placed = sem("rhs_zero"), sem("e_placed")
        bn = sem("bn")
        order_sp = sem("order_sp")
        order = sem("order")
        ps_staged, ps_s = sem("ps_staged"), [sem(f"ps_s{h}") for h in range(2)]
        tw_h, tw_p, tw_x, tw_s = sem("tw_h"), sem("tw_p"), sem("tw_x"), [sem(f"tw_s{h}") for h in range(2)]
        ed_staged, ed_g, ed_c = sem("ed_staged"), [sem(f"ed_g{h}") for h in range(2)], sem("ed_c")

        class Sweep:
            def __init__(self, name):
                self.staged = sem(name + "_staged")
                self.g = [sem(f"{name}_g{h}") for h in range(2)]
                self.v = sem(name + "_v")
                self.r = sem(name + "_r")
                self.f = sem(name + "_f")
                self.x = sem(name + "_x")
                self.s = [sem(f"{name}_s{h}") for h in range(2)]

        SW = [Sweep(f"l{k}") for k in range(3)]
        sw_small = sem("sw_small")
        sw_sq = sem("sw_sq")
        sw_w = sem("sw_w")
        nu_staged, nu_g, nu_l = sem("nu_staged"), [sem(f"nu_g{h}") for h in range(2)], [sem(f"nu_l{h}") for h in range(2)]
        nu_d, nu_q, nu_h, nu_s = sem("nu_d"), sem("nu_q"), sem("nu_h"), [sem(f"nu_s{h}") for h in range(2)]
        at_staged, at_g = sem("at_staged"), [sem(f"at_g{h}") for h in range(2)]
        at_ea, at_t, at_c, at_h, at_sc = sem("at_ea"), sem("at_t"), sem("at_c"), sem("at_h"), sem("at_sc")
        at_d, at_e, at_v, at_r, at_f, at_s = sem("at_d"), sem("at_e"), sem("at_v"), sem("at_r"), sem("at_f"), [sem(f"at_s{h}") for h in range(2)]
        gr_l, gr_d, gr_u, gr_t, gr_c, gr_m = [sem(f"gr_l{h}") for h in range(2)], sem("gr_d"), sem("gr_u"), sem("gr_t"), sem("gr_c"), sem("gr_m")
        gr_p, gr_a, gr_s = sem("gr_p"), sem("gr_a"), [sem(f"gr_s{h}") for h in range(2)]
        at_ss, gr_x, gr_o = sem("at_ss"), sem("gr_x"), sem("gr_o")
        last_out = sem("last_out")

        C_C, C_IN, C_DEND, C_G0S, C_CS, C_NBC, C_NBG, C_MCI, C_MCO, C_ME, C_X0, C_X1, C_T0, C_T1, C_T2, C_T3, C_E0 = range(17)

        def col(k):
            return cols[:, k:k + 1]

        def at(tile, b, w=1, n=B):
            return tile[:, bass.ds(b * (n * w), n * w)]

        gates = [big[:, h * B * 5 * D:(h + 1) * B * 5 * D].rearrange("p (i w) -> p i w", w=5 * D) for h in range(2)]
        banks = [psH[0], psH[1], psH[2], psE]
        ED_PARTS = [(0, 14), (28, 5), (38, 4), (46, 5)]

        block = ctx.enter_context(nc.Block())

        @block.sync
        def _(sp):
            def load(tile, c0, src_flat, w, s):
                for a, b in ((0, 112), (112, FULL)):
                    sp.dma_start(tile[a:b, c0:c0 + J * w],
                                 src_flat[a * J * w:b * J * w].rearrange("(p j) -> p j", j=J * w)).then_inc(s, 16)
                sp.dma_start(tile[FULL:P, c0:c0 + REST * w],
                             src_flat[FULL * J * w:].rearrange("(p j) -> p j", j=REST * w)).then_inc(s, 16)

            sp.wait_ge(pads, 4)
            load(key_d, 1, dst, 1, ld_dst)
            sp.dma_start(key_d[1:P, 0:1], dst[J - 1:FULL * J:J].rearrange("(p a) -> p a", a=1), allow_slow_non_contiguous=True).then_inc(ld_dst, 16)
            sp.dma_start(key_d[0:FULL, J + 1:J + 2], dst[J:FULL * J + 1:J].rearrange("(p a) -> p a", a=1), allow_slow_non_contiguous=True).then_inc(ld_dst, 16)
            load(ew, 0, edge_weight, 1, ld_ew)
            load(src_i, 0, src, 1, ld_src)
            sp.dma_start(kx[0:96, :], src[0:96 * 512].rearrange("(p j) -> p j", j=512)).then_inc(ld_key, 16)
            sp.dma_start(kx[96:97, :], src[96 * 512:97 * 512].rearrange("(p j) -> p j", j=512)).then_inc(ld_key, 16)
            sp.dma_start(kx[97:98, 0:E - 97 * 512], src[97 * 512:].rearrange("(p j) -> p j", j=E - 97 * 512)).then_inc(ld_key, 16)
            sp.wait_ge(place_pads, 1)
            sp.dma_start(rows(t_place), place_v[:, :]).then_inc(place_set, 16)
            sp.wait_ge(pool_pads, 2)
            load(big, 0, x.rearrange("n f -> (n f)"), D, ld_x)
            er = edge_s[:, :].rearrange("p (j w) -> p j w", w=ED + 1)
            for a, b, n in ((0, 112, J), (112, FULL, J), (FULL, P, REST)):
                sp.dma_start(er[a:b, 0:n, 0:ED],
                             edge_attr[a * J:a * J + (b - a) * n, :].rearrange("(p j) f -> p j f", j=n)).then_inc(ld_ea, 16)
            sp.wait_ge(zset, 2)
            for k, (a, b) in enumerate(((0, P), (P, H1))):
                sp.dma_start(wcat[0:b - a, k, 0:D], W_att1[a:b, 0:D]).then_inc(ld_w, 16)
                sp.dma_start(wcat[0:b - a, k, D:P], W_att1[a:b, D + ED:H1]).then_inc(ld_w, 16)
                sp.dma_start(wea[0:b - a, k, :], W_att1[a:b, D:D + ED]).then_inc(ld_w, 16)
            for k, (a, b) in enumerate(((0, P), (P, 3 * D))):
                sp.dma_start(wih[0:b - a, k, :], W_ih[a:b, :]).then_inc(ld_w, 16)
                sp.dma_start(whh[0:b - a, k, :], W_hh[a:b, :]).then_inc(ld_w, 16)
            sp.dma_start(wlin[:, D:P], W_lin).then_inc(ld_w, 16)
            sp.dma_start(bcol[:, :], b_lin.rearrange("(p a) -> p a", a=1)).then_inc(ld_w, 16)
            for t, c, v, n in ((brow, 0, b_ih, 3 * D), (brow, 3 * D, b_hh, 3 * D), (brow, 6 * D, b_lin, D),
                               (b1row, 0, b_att1, H1), (rowt, 0, W_att2.rearrange("a b -> (a b)"), H1),
                               (row2, 2 * P - 1, b_att2, 1)):
                sp.dma_start(t[0:1, c:c + n], v.rearrange("(a n) -> a n", a=1)).then_inc(ld_w, 16)
            for k in range(3):
                sp.dma_start(t_u[k][ROW_ZERO:ROWS, :], zrow[:, 0:D]).then_inc(zeroed, 16)
            msg_rows = rows(t_msg)
            with sp.Fori(0, NB) as b:
                sp.dma_start(at(msg_rows, b, D + 1), zrow[:, :]).then_inc(zeroed, 16)
            sp.wait_ge(edge_ready, 1)
            sp.dma_start(rows(t_edge), edge_s[:, :]).then_inc(edge_stored, 16)
            sp.wait_ge(sort_done, 1)
            flat = t_sorted.rearrange("n a -> (n a)")
            sp.dma_start(flat.rearrange("(p j) -> p j", j=512), sx[0][:, :].bitcast(I32)).then_inc(ld_sorted, 16)
            sp.wait_ge(ld_sorted, 16)
            sp.dma_start(key_s[:, 1:J + 1], flat[SORT0:].rearrange("(p j) -> p j", j=J)).then_inc(ld_sorted, 16)
            sp.dma_start(key_s[1:P, 0:1], t_sorted[SORT0 + J - 1:SORT - 1:J, :], allow_slow_non_contiguous=True).then_inc(ld_sorted, 16)
            sp.dma_start(key_s[0:P - 1, J + 1:J + 2], t_sorted[SORT0 + J:SORT:J, :], allow_slow_non_contiguous=True).then_inc(ld_sorted, 16)
            sp.wait_ge(w_copied, 3)
            sp.wait_ge(rhs_zero, 1)
            for i in range(B):
                sp.dma_start(rhs_e[i * ED:(i + 1) * ED, i * H1:(i + 1) * H1], w1e[:, :]).then_inc(e_placed, 16)
            for h in range(2):
                sp.wait_ge(ps_s[h], 16 * B * IT)
            sp.dma_start(node_v[:, :], rows(t_place)).then_inc(ld_node, 16)
            h_rows, xa_rows = rows(t_h), rows(t_xa)
            with sp.Fori(0, IT) as t:
                for h in range(2):
                    sp.wait_ge(tw_h, 14 * t + 7 * h + 7)
                    sp.sem_inc(order_sp, 1)
                    sp.wait_ge(tw_p, 2 * t + h + 1)
                    sp.sem_inc(order_sp, 1)
                    sp.dma_start(at(h_rows, 2 * t + h, D + 2), O[h][:, :]).then_inc(tw_s[h], 16)
                    sp.wait_ge(tw_x, 2 * t + h + 1)
                    sp.sem_inc(order_sp, 1)
                    sp.dma_start(at(xa_rows, 2 * t + h, D), O2[h][:, :]).then_inc(tw_s[h], 16)
            for k in range(3):
                s, u_rows = SW[k], rows(t_u[k])
                with sp.Fori(0, IT) as t:
                    for h in range(2):
                        sp.wait_ge(s.x, 14 + 14 * t + 7 * h + 7)
                        sp.sem_inc(order_sp, 1)
                        sp.dma_start(at(u_rows, 2 * t + h, D), O[h][:, 0:B * D]).then_inc(s.s[h], 16)
                sp.wait_ge(fix_ready[k], 1)
                sp.dma_start(t_u[k][ROW_FIX:ROW_FIX + P, :], fixr[:, 0:D]).then_inc(fix_stored[k], 16)
            x2_rows, h2_rows = rows(t_x2), rows(t_h2)
            for h in range(2):
                sp.dma_start(O2[h][:, :], xa_rows[:, h * B * D:(h + 1) * B * D]).then_inc(nu_l[h], 16)

            def nu_store(b, h, last):
                sp.wait_ge(nu_h, 7 * b + 21)
                sp.sem_inc(order_sp, 1)
                sp.dma_start(at(x2_rows, b, D), V[h][:, 0:B * D]).then_inc(nu_s[h], 16)
                sp.dma_start(at(h2_rows, b, D), R[h][:, 0:B * D]).then_inc(nu_s[h], 16)
                if not last:
                    sp.dma_start(O2[h][:, :], at(xa_rows, b + 2, D)).then_inc(nu_l[h], 16)

            with sp.Fori(0, IT - 1) as t:
                for h in range(2):
                    nu_store(2 * t + h, h, False)
            for h in range(2):
                nu_store(NB - 2 + h, h, True)
            for h in range(2):
                sp.wait_ge(at_s[h], 16 * B * IT)
            sp.wait_ge(fix_stored[3], 16)
            cat = [G[h][:, :].rearrange("p (j w) -> p j w", w=P)[:, :, 0:D] for h in range(2)]

            def gr_load(b, h):
                sp.dma_start(V[h][:, :], at(msg_rows, b, D + 1)).then_inc(gr_l[h], 16)
                sp.dma_start(cat[h], at(h2_rows, b, D).rearrange("p (j w) -> p j w", w=D)).then_inc(gr_l[h], 16)
                sp.dma_start(O2[h][:, :], at(x2_rows, b, D)).then_inc(gr_l[h], 16)

            out_rows = out[0:FULL * J, :].rearrange("(p j) f -> p (j f)", j=J)

            def gr_out(b, h):
                sp.wait_ge(gr_o, b + 1)
                sp.sem_inc(order_sp, 1)
                sp.dma_start(at(out_rows[0:112, :], b, D), O[h][0:112, 0:B * D]).then_inc(gr_s[h], 16)
                sp.dma_start(at(out_rows[112:FULL, :], b, D), O[h][112:FULL, 0:B * D]).then_inc(gr_s[h], 16)
                sp.dma_start(at(t_last, b, D), O[h][FULL:P, 0:B * D]).then_inc(gr_s[h], 16)

            for h in range(2):
                gr_load(h, h)
            with sp.Fori(0, IT - 1) as t:
                for h in range(2):
                    gr_out(2 * t + h, h)
                    gr_load(2 * t + h + 2, h)
            for h in range(2):
                gr_out(NB - 2 + h, h)
            for h in range(2):
                sp.wait_ge(gr_s[h], 48 * IT)
            sp.dma_start(out[FULL * J:N, :].rearrange("(a j) f -> a (j f)", a=1), t_last[:, 0:REST * D]).then_inc(last_out, 16)
            sp.wait_ge(last_out, 16)

        @block.gpsimd
        def _(pool):
            def gather(dst_ap, table, idx, bound, s):
                pool.indirect_dma_start(out=dst_ap, out_offset=None, in_=table,
                                        in_offset=bass.IndirectOffsetOnAxis(ap=idx, axis=0),
                                        bounds_check=bound, oob_is_err=False).then_inc(s, 16)

            def scatter(table, src_ap, idx, bound, s):
                pool.indirect_dma_start(out=table, out_offset=bass.IndirectOffsetOnAxis(ap=idx, axis=0), in_=src_ap,
                                        in_offset=None, bounds_check=bound, oob_is_err=False).then_inc(s, 16)

            pool.memset(ident[:, :], 0.0).then_inc(consts, 1)
            pool.iota(lin_i[:, :], pattern=[[1, 512]], base=0, channel_multiplier=512).then_inc(consts, 1)
            pool.iota(pos[:, :], pattern=[[1, J]], base=0, channel_multiplier=J,
                      allow_small_or_imprecise_dtypes=True).then_inc(consts, 1)
            pool.iota(fixrow[:, :], pattern=[[0, 1]], base=ROW_FIX, channel_multiplier=1,
                      allow_small_or_imprecise_dtypes=True).then_inc(consts, 1)
            pool.memset(ones[:, :], 1.0).then_inc(consts, 1)
            pool.wait_ge(consts, 5)
            pool.affine_select(out=ident[:, :], in_=ident[:, :], compare_op=ALU.not_equal, fill=1.0, base=0,
                               pattern=[[-1, P]], channel_multiplier=1).then_inc(consts, 1)
            pool.wait_ge(consts, 6)
            pool.memset(big[96:P, REST * D:J * D], 0.0).then_inc(pool_pads, 1)
            pool.wait_ge(pool_pads, 1)
            pool.memset(edge_s[96:P, REST * (ED + 1):J * (ED + 1)], 0.0).then_inc(pool_pads, 1)

            pool.wait_ge(pool_pads, 2)
            pool.wait_ge(place_set, 16)
            with pool.Fori(0, IT) as t:
                for h in range(2):
                    pool.wait_ge(ps_staged, 2 * (2 * t + h) + 2)
                    pool.sem_inc(order, 1)
                    for i in range(B):
                        scatter(t_place, sv[h][:, 2 * i:2 * i + 2], st[h][:, i:i + 1], NP - 1, ps_s[h])

            def edge_part(k):
                b0, n = ED_PARTS[k]
                with pool.Fori(0, n) as t:
                    for h in range(2):
                        pool.wait_ge(ed_staged, b0 + 2 * t + h + 1)
                        pool.sem_inc(order, 1)
                        for i in range(B):
                            w = ED + 1
                            gather(G[h][:, w * i:w * i + w], t_edge, st[h][:, i:i + 1], NP - 1, ed_g[h])

            pool.wait_ge(ld_w, 16 * 18)
            pool.partition_broadcast(w2bc[:, :], rowt[0:1, :]).then_inc(w_done, 1)
            pool.partition_broadcast(b2c[:, :], row2[0:1, 2 * P - 1:2 * P]).then_inc(w_done, 1)
            pool.wait_ge(w_bias, 1)
            pool.partition_broadcast(bias_n[:, :], nrow[0:1, :]).then_inc(w_done, 1)
            pool.wait_ge(edge_stored, 16)
            pool.wait_ge(w_copied, 9)
            edge_part(0)
            for h in range(2):
                pool.wait_ge(tw_s[h], 32 * IT)
            for k in range(3):
                s = SW[k]
                w = D + 2 if k == 0 else D
                if k:
                    for h in range(2):
                        pool.wait_ge(SW[k - 1].s[h], 16 * IT)
                    pool.wait_ge(fix_stored[k - 1], 16)
                with pool.Fori(0, IT) as t:
                    for h in range(2):
                        pool.wait_ge(s.staged, 2 * t + h + 1)
                        pool.sem_inc(order, 1)
                        for i in range(B):
                            if k == 0:
                                gather(G[h][:, w * i:w * i + w], t_h, st[h][:, i:i + 1], NP - 1, s.g[h])
                            else:
                                gather(G[h][:, w * i:w * i + w], t_u[k - 1], st[h][:, i:i + 1], ROWS - 1, s.g[h])
                edge_part(k + 1)
            for h in range(2):
                pool.wait_ge(SW[2].s[h], 16 * IT)
            pool.wait_ge(fix_stored[2], 16)
            with pool.Fori(0, IT) as t:
                for h in range(2):
                    pool.wait_ge(nu_staged, 2 * t + h + 1)
                    pool.sem_inc(order, 1)
                    for i in range(B):
                        gather(G[h][:, D * i:D * i + D], t_u[2], st[h][:, i:i + 1], ROWS - 1, nu_g[h])

            for h in range(2):
                pool.wait_ge(nu_s[h], 32 * IT)
            pool.wait_ge(zeroed, 16 * (NB + 3))

            def at_gather(b, h):
                pool.wait_ge(at_staged, 2 * b + 2)
                pool.sem_inc(order, 1)
                for i in range(B):
                    gather(G[h][:, P * i:P * i + D], t_h2, st[h][:, i:i + 1], NP - 1, at_g[h])
                    gather(G[h][:, P * i + D:P * i + P], t_h2, st[h][:, B + i:B + i + 1], NP - 1, at_g[h])

            def at_scatter(b, h):
                w = D + 1
                pool.wait_ge(at_ss, b + 1)
                pool.wait_ge(at_r, 7 * b + 8)
                pool.sem_inc(order, 1)
                for i in range(B):
                    scatter(t_msg, R[h][:, w * i:w * i + w], sst[h][:, i:i + 1], NP - 1, at_s[h])

            at_gather(0, 0)
            with pool.Fori(0, IT - 1) as t:
                at_gather(2 * t + 1, 1)
                at_scatter(2 * t, 0)
                at_gather(2 * t + 2, 0)
                at_scatter(2 * t + 1, 1)
            at_gather(NB - 1, 1)
            at_scatter(NB - 2, 0)
            at_scatter(NB - 1, 1)
            pool.wait_ge(fix_ready[3], 2)
            scatter(t_msg, fixr[:, :], fix_i[:, :], NP - 1, fix_stored[3])

        @block.scalar
        def _(act):
            S = nc.scalar

            def stage(b, h, lists, s):
                for k, lst in enumerate(lists):
                    S.copy(st[h][:, k * B:k * B + B], at(lst, b)).then_inc(s, 1)

            act.wait_ge(sq_ask, 1)
            S.activation(tile_d[:, 0:J], tile_b[:, 0:J], ACT.Sqrt).then_inc(sq_given, 1)
            act.wait_ge(place_ready, 1)
            with act.Fori(0, IT) as t:
                for h in range(2):
                    act.wait_ge(ps_s[h], 16 * B * t)
                    S.copy(st[h][:, 0:B], at(dsts_i, 2 * t + h)).then_inc(ps_staged, 1)
                    S.copy(sv[h][:, :], at(place_v, 2 * t + h, 2)).then_inc(ps_staged, 1)
            act.wait_ge(sq_ask, 2)
            S.activation(tile_d[:, 0:J], tile_b[:, 0:J], ACT.Sqrt).then_inc(sq_given, 1)

            act.wait_ge(w_step, 1)
            S.copy(rhs1[:, 0:P], psH[0][:, 0:P]).then_inc(w_copied, 1)
            S.copy(rhs1[:, P:H1], psH[0][:, P:H1]).then_inc(w_copied, 1)
            S.copy(w1e[:, :], psH[1][0:ED, 0:H1]).then_inc(w_copied, 1)
            S.copy(whhT[:, :], psH[2][0:D, 0:3 * D]).then_inc(w_copied, 1)
            S.copy(rhs_n[0:D, 0:3 * D], psE[0:D, 0:3 * D]).then_inc(w_copied, 1)
            act.wait_ge(w_step, 2)
            S.copy(rhs_n[D:P, 0:2 * D], psH[0][D:P, 0:2 * D]).then_inc(w_copied, 1)
            S.copy(rhs_n[D:P, 3 * D:4 * D], psH[0][D:P, 2 * D:3 * D]).then_inc(w_copied, 1)
            S.copy(rhs_n[D:P, 4 * D:5 * D], psH[1][D:P, 0:D]).then_inc(w_copied, 1)
            S.copy(hrow[0:1, :], psH[2][0:1, 0:3 * D]).then_inc(w_copied, 1)

            act.wait_ge(node_ready, 1)
            with act.Fori(0, IT) as t:
                for h in range(2):
                    act.wait_ge(tw_s[h], 32 * t)
                    for i in range(B):
                        c = (2 * t + h) * B + i
                        S.activation(O[h][:, i * (D + 2):i * (D + 2) + D], big[:, bass.ds(c * D, D)], ACT.Relu,
                                     bias=shift[:, bass.ds(c, 1)], scale=rstd[:, bass.ds(c, 1)]).then_inc(tw_h, 1)

            def edge_part(k):
                b0, n = ED_PARTS[k]
                for h in range(2):
                    S.copy(st[h][:, 0:B], perm_i[:, (b0 + h) * B:(b0 + h + 1) * B]).then_inc(ed_staged, 1)

                def take(b, h, more):
                    act.wait_ge(ed_g[h], 8 * B * (b + 2 - h))
                    S.copy(at(edge_s, b, ED + 1), G[h][:, 0:B * (ED + 1)]).then_inc(ed_c, 1)
                    if more:
                        act.wait_ge(ed_c, b + 1)
                        S.copy(st[h][:, 0:B], at(perm_i, b + 2)).then_inc(ed_staged, 1)

                with act.Fori(0, n - 1) as t:
                    for h in range(2):
                        take(b0 + 2 * t + h, h, True)
                for h in range(2):
                    take(b0 + 2 * n - 2 + h, h, False)

            for k in range(3):
                s = SW[k]
                lst = src_i if k == 0 else row_i
                w = D + 2 if k == 0 else D
                if k == 0:
                    for h in range(2):
                        act.wait_ge(ed_g[h], 16 * B * ED_PARTS[0][1])
                    act.wait_ge(ed_c, 2 * ED_PARTS[0][1])
                    act.wait_ge(tw_x, NB)
                    act.wait_ge(ld_src, 48)
                S.copy(st[0][:, 0:B], lst[:, 0:B]).then_inc(s.staged, 1)
                S.copy(st[1][:, 0:B], lst[:, B:2 * B]).then_inc(s.staged, 1)
                act.sem_inc(s.x, 14)
                with act.Fori(0, IT) as t:
                    for h in range(2):
                        b = 2 * t + h
                        if k == 0:
                            act.wait_ge(sw_small, 4 * b + 1)
                            S.activation(q7[h][1][:, :], q7[h][0][:, :], ACT.Sqrt).then_inc(sw_sq, 1)
                            act.wait_ge(sw_w, b + 1)
                            for i in range(B):
                                c = b * B + i
                                S.activation(big[:, bass.ds(c * D, D)], G[h][:, w * i:w * i + D], ACT.Copy,
                                             scale=w_e[:, bass.ds(c, 1)]).then_inc(s.v, 1)
                        act.wait_ge(s.v, 7 * b + 7)
                        act.wait_ge(s.g[h], 16 * B * (t + 1))
                        S.copy(st[h][:, 0:B], at(lst, b + 2)).then_inc(s.staged, 1)
                        act.wait_ge(s.s[h], 16 * t)
                        for i in range(B):
                            c = b * B + i
                            act.wait_ge(s.r, 7 * b + i + 2)
                            S.activation(O[h][:, D * i:D * i + D], R[h][:, D * i:D * i + D], ACT.Copy,
                                         scale=dinv[:, bass.ds(c, 1)]).then_inc(s.x, 1)
                act.wait_ge(s.staged, NB + 2)
                edge_part(k + 1)

            act.wait_ge(nodes_listed, 1)
            S.copy(st[0][:, 0:B], node_i[:, 0:B]).then_inc(nu_staged, 1)
            S.copy(st[1][:, 0:B], node_i[:, B:2 * B]).then_inc(nu_staged, 1)
            with act.Fori(0, IT) as t:
                for h in range(2):
                    b = 2 * t + h
                    act.wait_ge(nu_d, 16 * b + 1)
                    act.wait_ge(nu_g[h], 16 * B * (t + 1))
                    S.copy(st[h][:, 0:B], at(node_i, b + 2)).then_inc(nu_staged, 1)
                    act.wait_ge(nu_d, 16 * b + 14)
                    S.activation(q7[h][5][:, :], q7[h][4][:, :], ACT.Sqrt).then_inc(nu_q, 1)
                    act.wait_ge(nu_d, 16 * b + 16)
                    act.wait_ge(nu_s[h], 32 * t)
                    for i in range(B):
                        S.activation(R[h][:, D * i:D * i + D], V[h][:, D * i:D * i + D], ACT.Relu,
                                     bias=q7[h][1][:, i:i + 1], scale=q7[h][0][:, i:i + 1]).then_inc(nu_h, 1)

            def stage_at(b, h):
                for k, lst in enumerate((srcs_i, dsts_i)):
                    S.copy(st[h][:, k * B:k * B + B], at(lst, b)).then_inc(at_staged, 1)

            act.wait_ge(at_d, 1)
            act.wait_ge(nu_staged, NB + 2)
            for h in range(2):
                act.wait_ge(nu_g[h], 16 * B * IT)
                stage_at(h, h)
            with act.Fori(0, IT) as t:
                for h in range(2):
                    b = 2 * t + h
                    ea = at(edge_s, b, ED + 1).rearrange("p (j w) -> p j w", w=ED + 1)[:, :, 0:ED]
                    S.copy(ea7[h][:, :].rearrange("p (j w) -> p j w", w=ED), ea).then_inc(at_ea, 1)
                    act.wait_ge(at_t, 3 * b + 1)
                    S.copy(ftS[h][:, 0:512], psT[0][:, :]).then_inc(at_c, 1)
                    act.wait_ge(at_t, 3 * b + 2)
                    S.copy(ftS[h][:, 512:B * P], psT[1][:, 0:B * P - 512]).then_inc(at_c, 1)
                    act.wait_ge(at_t, 3 * b + 3)
                    S.copy(eaT[h][:, :], psE[0:B * ED, 0:P]).then_inc(at_c, 1)
                    act.wait_ge(at_d, 7 * b + 7)
                    S.activation(e14[h][:, :], q14[h][:, :], ACT.Exp).then_inc(at_e, 1)
                    act.wait_ge(at_e, b + 1)
                    for i in range(B):
                        S.activation(V[h][:, i * (D + 1):i * (D + 1) + D], G[h][:, i * P + D:i * P + P], ACT.Copy,
                                     scale=e14[h][:, B + i:B + i + 1]).then_inc(at_v, 1)
                    act.wait_ge(at_s[h], 16 * B * t)
                    S.copy(sst[h][:, :], at(scat_i, b)).then_inc(at_ss, 1)
                    act.wait_ge(at_v, 7 * b + 7)
                    act.wait_ge(at_g[h], 32 * B * (t + 1))
                    stage_at(b + 2, h)
            act.wait_ge(sq_ask, 3)
            S.activation(cols[:, C_E0:C_E0 + 4], cols[:, C_T0:C_T0 + 4], ACT.Exp).then_inc(sq_given, 1)

            with act.Fori(0, IT) as t:
                for h in range(2):
                    b = 2 * t + h
                    act.wait_ge(gr_d, 10 * b + 3)
                    for i in range(B):
                        S.activation(G[h][:, i * P + D:i * P + P], V[h][:, i * (D + 1):i * (D + 1) + D], ACT.Copy,
                                     scale=q7[h][1][:, i:i + 1]).then_inc(gr_u, 1)
                    act.wait_ge(gr_t, 2 * b + 1)
                    S.copy(ftS[h][:, 0:512], psT[0][:, :]).then_inc(gr_c, 1)
                    act.wait_ge(gr_t, 2 * b + 2)
                    S.copy(ftS[h][:, 512:B * P], psT[1][:, 0:B * P - 512]).then_inc(gr_c, 1)
                    pre = gates[h]
                    act.wait_ge(gr_p, 7 * b + 14)
                    S.activation(pre[:, :, 0:2 * D], pre[:, :, 0:2 * D], ACT.Sigmoid).then_inc(gr_a, 1)
                    act.wait_ge(gr_d, 10 * b + 5)
                    S.activation(pre[:, :, 2 * D:3 * D], pre[:, :, 2 * D:3 * D], ACT.Tanh).then_inc(gr_a, 1)

        @block.tensor
        def _(pe):
            T = nc.tensor
            turn = [0]

            def asked():
                turn[0] += 1
                pe.wait_ge(ask, turn[0])

            pe.wait_ge(consts, 6)
            asked()
            T.transpose(psC[0:1, 0:P], tile_d[:, J - 1:J], ident[:, :])
            T.transpose(psC[0:1, P:2 * P], col(C_C), ident[:, :]).then_inc(given, 1)
            asked()
            T.transpose(psC[:, 2 * P:2 * P + 1], row1[0:1, 0:P], ident[0:1, 0:1]).then_inc(given, 1)
            asked()
            T.transpose(psC[0:D + 1, 0:P], cbc[:, :], ident[:, :]).then_inc(given, 1)
            for k in range(14):
                asked()
                for c in range(4):
                    mm = T.transpose(psC[:, c * P:(c + 1) * P], sx[k % 2][:, c * P:(c + 1) * P], ident[:, :])
                mm.then_inc(given, 1)

            pe.wait_ge(ld_w, 16 * 18)
            pe.wait_ge(pads, 5)
            T.transpose(psH[0][:, 0:P], wcat[:, 0, :], ident[:, :])
            T.transpose(psH[0][:, P:H1], wcat[0:H1 - P, 1, :], ident[0:H1 - P, 0:H1 - P])
            T.transpose(psH[1][0:ED, 0:P], wea[:, 0, :], ident[:, :])
            T.transpose(psH[1][0:ED, P:H1], wea[0:H1 - P, 1, :], ident[0:H1 - P, 0:H1 - P])
            T.transpose(psH[2][0:D, 0:P], whh[:, 0, :], ident[:, :])
            T.transpose(psH[2][0:D, P:3 * D], whh[0:D, 1, :], ident[0:D, 0:D])
            T.transpose(psE[0:D, 0:P], wih[:, 0, :], ident[:, :])
            T.transpose(psE[0:D, P:3 * D], wih[0:D, 1, :], ident[0:D, 0:D]).then_inc(w_step, 1)
            pe.wait_ge(w_copied, 5)
            T.matmul(psH[0][:, 0:3 * D], wlin[:, :], whhT[:, :], start=True, stop=True)
            T.matmul(psH[1][:, 0:D], wlin[:, :], ident[0:D, 0:D], start=True, stop=True)
            T.matmul(psH[2][0:1, 0:3 * D], bcol[:, :], whhT[:, :], start=True, stop=True).then_inc(w_step, 1)

            for k in range(3):
                asked()
                T.transpose(psC[0:D, 0:P], R[1][:, (B - 1) * D:B * D], ident[:, :]).then_inc(given, 1)
                asked()
                T.transpose(psC[:, P:P + D], co[0:D, 0:P], ident[0:D, 0:D]).then_inc(given, 1)

            pe.wait_ge(w_copied, 9)
            pe.wait_ge(e_placed, 16 * B)
            with pe.Fori(0, IT) as t:
                for h in range(2):
                    b = 2 * t + h
                    pe.wait_ge(at_g[h], 32 * B * (t + 1))
                    pe.wait_ge(at_c, 3 * b)
                    for i in range(B):
                        mm = T.transpose(psT[i // 4][:, (i % 4) * P:(i % 4 + 1) * P], G[h][:, i * P:(i + 1) * P],
                                         ident[:, :])
                        if i in (3, B - 1):
                            mm.then_inc(at_t, 1)
                    pe.wait_ge(at_ea, b + 1)
                    T.transpose(psE[0:B * ED, 0:P], ea7[h][:, :], ident[:, :]).then_inc(at_t, 1)
                    pe.wait_ge(at_c, 3 * b + 3)
                    for i in range(B):
                        o = psH[i // 3][:, (i % 3) * H1:(i % 3 + 1) * H1]
                        if i % 3 == 0:
                            pe.wait_ge(at_sc, 7 * b + min(i + 3, B))
                        T.matmul(o, ftS[h][:, i * P:(i + 1) * P], rhs1[:, :], start=True, stop=False)
                        T.matmul(o, eaT[h][:, :], rhs_e[:, i * H1:(i + 1) * H1], start=False, stop=False)
                        T.matmul(o, ones[0:1, :], b1row[:, :], start=False, stop=True).then_inc(at_h, 1)
            asked()
            T.transpose(psC[0:1, 0:P], m_all[:, J:J + 1], ident[:, :])
            T.transpose(psC[0:1, P:2 * P], col(C_NBC), ident[:, :]).then_inc(given, 1)
            asked()
            T.transpose(psC[:, 2 * P:2 * P + 1], row1[0:1, 0:P], ident[0:1, 0:1])
            T.transpose(psC[:, 2 * P + 1:2 * P + 2], row1[0:1, 1:P + 1], ident[0:1, 0:1]).then_inc(given, 1)
            asked()
            T.transpose(psC[0:D + 1, 0:P], V[0][:, 0:D + 1], ident[:, :])
            T.transpose(psC[0:D + 1, P:2 * P], cbc[:, :], ident[:, :]).then_inc(given, 1)
            asked()
            T.transpose(psC[:, 2 * P:2 * P + D + 1], co[:, 0:P], ident[0:D + 1, 0:D + 1]).then_inc(given, 1)

            with pe.Fori(0, IT) as t:
                for h in range(2):
                    b = 2 * t + h
                    pe.wait_ge(gr_l[h], 48 * (t + 1))
                    pe.wait_ge(gr_u, 7 * b + 7)
                    pe.wait_ge(gr_c, 2 * b)
                    for i in range(B):
                        mm = T.transpose(psT[i // 4][:, (i % 4) * P:(i % 4 + 1) * P], G[h][:, i * P:(i + 1) * P],
                                         ident[:, :])
                        if i in (3, B - 1):
                            mm.then_inc(gr_t, 1)
                    for i in range(B):
                        if i in (0, 4):
                            pe.wait_ge(gr_c, 2 * b + 1 + i // 4)
                        pe.wait_ge(gr_p, 7 * b + (i + 4 if i >= 4 else i + 5 if i < 3 else 4))
                        T.matmul(banks[i % 4][:, 0:5 * D], ftS[h][:, i * P:(i + 1) * P], rhs_n[:, :],
                                 start=True, stop=True).then_inc(gr_m, 1)

        @block.vector
        def _(dve):
            v = nc.vector
            steps = [0]
            turn = [0]

            def link(ins):
                steps[0] += 1
                ins.then_inc(dv, 1)
                dve.wait_ge(dv, steps[0])

            def exchange():
                turn[0] += 1
                dve.sem_inc(ask, 1)
                dve.wait_ge(given, turn[0])

            ta, tb, tc, td = tile_a[:, 0:J], tile_b[:, 0:J], tile_c[:, 0:J], tile_d[:, 0:J]

            v.memset(key_d[:, :], PAD_KEY).then_inc(pads, 1)
            v.memset(ew[:, :], 0.0).then_inc(pads, 1)
            v.memset(src_i[:, :], 0).then_inc(pads, 1)
            v.memset(kx[:, :], PAD_KEY).then_inc(pads, 1)
            pl = place_v[:, :].rearrange("p (j w) -> p j w", w=2)
            link(v.memset(pl[:, :, 1:2], 0.0))
            v.memset(pl[:, :, 0:1], float(ROW_ZERO)).then_inc(place_pads, 1)
            v.memset(zrow[:, :], 0.0).then_inc(zset, 1)
            v.memset(wlin[:, :], 0.0).then_inc(zset, 1)
            link(v.memset(rhs_n[:, :], 0.0))
            v.memset(rhs_e[:, :], 0.0).then_inc(rhs_zero, 1)
            for lst in (row_i, srcs_i, dsts_i, perm_i, scat_i):
                link(v.memset(lst[:, J:J + 2 * B], 0))
            link(v.memset(row1[:, 0:1], 0.0))
            link(v.memset(co[:, 0:1], 0.0))
            dve.sem_inc(pads, 1)

            def runs(key, end):
                link(v.tensor_tensor(ta, key[:, 1:J + 1], key[:, 0:J], ALU.not_equal))
                link(v.tensor_tensor(tb, key[:, 1:J + 1], key[:, 2:J + 2], ALU.not_equal))
                link(v.tensor_copy(tc[:, 1:J], ta[:, 1:J]))
                link(v.memset(tc[:, 0:1], 0.0))
                link(v.tensor_tensor_scan(td, tc, tc, 0.0, ALU.max, ALU.max))
                link(v.tensor_scalar(tc, td, -1.0, 1.0, ALU.mult, ALU.add))
                link(v.tensor_tensor(end, tc, tb, ALU.mult))

            dve.wait_ge(ld_dst, 80)
            dve.wait_ge(consts, 6)
            runs(key_d, end_d[:, :])
            link(v.tensor_scalar(keep_d[:, :], ta, -1.0, 1.0, ALU.mult, ALU.add))
            link(v.tensor_tensor(col(C_C), tc[:, J - 1:J], keep_d[:, 0:1], ALU.mult))
            link(v.tensor_scalar(td, tb, -OOB, OOB, ALU.mult, ALU.add))
            link(v.tensor_tensor(place_i[:, 0:J], td, key_d[:, 1:J + 1], ALU.add))
            dve.wait_ge(place_set, 16)
            link(v.tensor_scalar(td, pos[:, :], fixrow[:, 0:1], None, ALU.subtract))
            link(v.tensor_tensor(td, td, end_d[:, :], ALU.mult))
            link(v.tensor_tensor(pl[:, :, 0], pos[:, :], td, ALU.subtract))
            dve.wait_ge(ld_ew, 48)
            link(v.tensor_tensor_scan(td, keep_d[:, :], ew[:, :], 0.0, ALU.mult, ALU.add))
            exchange()
            link(v.tensor_copy(row2[0:1, 0:P], psC[0:1, P:2 * P]))
            link(v.tensor_tensor_scan(row1[:, 1:P + 1], row2[0:1, 0:P], psC[0:1, 0:P], 0.0, ALU.mult, ALU.add))
            exchange()
            link(v.tensor_tensor(col(C_IN), psC[:, 2 * P:2 * P + 1], keep_d[:, 0:1], ALU.mult))
            link(v.scalar_tensor_tensor(out=pl[:, :, 1], in0=tc, scalar=col(C_IN), in1=td, op0=ALU.mult, op1=ALU.add))
            dve.sem_inc(place_ready, 1)
            link(v.tensor_scalar(tb, pl[:, :, 1], TINY, None, ALU.max))
            dve.sem_inc(sq_ask, 1)
            link(v.tensor_scalar(cbc[:, :], ones[:, 0:D + 1], col(C_C), None, ALU.mult))
            exchange()
            link(v.tensor_copy(cT[:, :], psC[0:D + 1, 0:P]))
            dve.wait_ge(sq_given, 1)
            link(v.reciprocal(ta, td))
            link(v.scalar_tensor_tensor(out=dinv[:, :], in0=pl[:, :, 1], scalar=0.0, in1=ta, op0=ALU.is_gt, op1=ALU.mult))
            link(v.scalar_tensor_tensor(out=ta, in0=end_d[:, :], scalar=1.0, in1=dinv[:, :], op0=ALU.mult, op1=ALU.mult,
                                        accum_out=col(C_DEND)))

            er = edge_s[:, :].rearrange("p (j w) -> p j w", w=ED + 1)
            dve.wait_ge(ld_ea, 48)
            dve.wait_ge(pool_pads, 2)
            link(v.tensor_copy(er[:, :, ED], key_d[:, 1:J + 1]))
            dve.sem_inc(edge_ready, 1)

            cur = [0]
            lin, u0, u1 = lin_i[:, :], sx[0][:, :].bitcast(U32), sx[1][:, :].bitcast(U32)
            dve.wait_ge(ld_key, 48)
            link(v.tensor_scalar(sx[1][:, :].bitcast(I32), kx[:, :], 32512.0, 256.0, ALU.is_ge, ALU.mult))
            link(v.scalar_tensor_tensor(out=sx[0][:, :].bitcast(I32), in0=kx[:, :], scalar=128.0,
                                        in1=sx[1][:, :].bitcast(I32), op0=ALU.add, op1=ALU.add))
            link(v.tensor_scalar(u1, u0, 16, None, ALU.logical_shift_left))
            link(v.tensor_tensor(u0, u1, lin, ALU.bitwise_or))
            link(v.tensor_scalar(mask[:, :], lin, 1, None, ALU.logical_shift_right))
            link(v.tensor_tensor(gray[:, :], lin, mask[:, :], ALU.bitwise_xor))

            def flip(k):
                s, d = (sx[cur[0]][:, :].bitcast(U32), sx[1 - cur[0]][:, :].bitcast(U32))
                link(v.tensor_scalar(mask[:, :], (gray if k else lin_i)[:, :], 31 - max(k, 1), 0x80000000,
                                     ALU.logical_shift_left, ALU.bitwise_and))
                link(v.tensor_tensor(d, s, mask[:, :], ALU.bitwise_xor))
                cur[0] ^= 1

            def compare(bit):
                a = sx[cur[0]][:, :].rearrange("p (a t s) -> p a t s", t=2, s=1 << bit)
                o = sx[1 - cur[0]][:, :].rearrange("p (a t s) -> p a t s", t=2, s=1 << bit)
                steps[0] += 2
                v.tensor_tensor(o[:, :, 0, :], a[:, :, 0, :], a[:, :, 1, :], ALU.min).then_inc(dv, 1)
                v.tensor_tensor(o[:, :, 1, :], a[:, :, 0, :], a[:, :, 1, :], ALU.max).then_inc(dv, 1)
                dve.wait_ge(dv, steps[0])
                cur[0] ^= 1

            swaps = [0]

            def swap():
                k = swaps[0] % 2
                if cur[0] != k:
                    link(v.tensor_copy(sx[k][:, :], sx[1 - k][:, :]))
                    cur[0] = k
                exchange()
                link(v.tensor_copy(sx[1 - k][:, :], psC[:, :]))
                cur[0] ^= 1
                swaps[0] += 1

            flip(0)
            for k in range(1, 17):
                low = k - 1
                if k >= 10:
                    swap()
                    for bit in range(k - 1, 6, -1):
                        compare(bit - 9 if bit >= 9 else bit)
                    swap()
                    low = 6
                for bit in range(low, -1, -1):
                    compare(bit)
                if k < 16:
                    flip(k)
            if cur[0]:
                link(v.tensor_copy(sx[0][:, :], sx[1][:, :]))
            link(v.memset(key_s[:, :], 0))
            dve.sem_inc(sort_done, 1)
            dve.wait_ge(ld_sorted, 64)
            packed = key_s[:, :].bitcast(U32)
            hi, lo = tile_a[:, :].bitcast(U32), tile_b[:, :].bitcast(U32)
            link(v.tensor_scalar(hi, packed, 16, None, ALU.logical_shift_right))
            link(v.tensor_scalar(lo, packed, 0xFFFF, None, ALU.bitwise_and))
            link(v.tensor_scalar(perm_i[:, 0:J], lo[:, 1:J + 1], float(E), None, ALU.min))
            link(v.tensor_scalar(tile_c[:, :], hi, 32768.0, -256.0, ALU.is_ge, ALU.mult))
            link(v.scalar_tensor_tensor(out=key_s[:, :], in0=hi, scalar=-128.0, in1=tile_c[:, :], op0=ALU.add, op1=ALU.add))
            link(v.tensor_scalar(srcs_i[:, 0:J], key_s[:, 1:J + 1], float(NP - 1), None, ALU.min))
            runs(key_s, end_s[:, :])
            link(v.tensor_scalar(start_s[:, :], ta, -BIG, None, ALU.mult))
            link(v.tensor_scalar(col(C_G0S), ta[:, 0:1], -1.0, 1.0, ALU.mult, ALU.add))
            link(v.tensor_tensor(col(C_CS), tc[:, J - 1:J], col(C_G0S), ALU.mult))
            link(v.tensor_scalar(col(C_NBC), col(C_CS), BIG, -BIG, ALU.mult, ALU.add))
            link(v.tensor_scalar(col(C_NBG), col(C_G0S), BIG, -BIG, ALU.mult, ALU.add))
            link(v.tensor_tensor(tb, tb, end_s[:, :], ALU.subtract))
            link(v.tensor_scalar(td, tb, -OOB, OOB, ALU.mult, ALU.add))
            link(v.tensor_tensor(scat_i[:, 0:J], td, key_s[:, 1:J + 1], ALU.add))
            link(v.scalar_tensor_tensor(out=ta, in0=end_s[:, :], scalar=1.0, in1=key_s[:, 1:J + 1], op0=ALU.mult,
                                        op1=ALU.mult, accum_out=col(C_X0)))
            link(v.scalar_tensor_tensor(out=ta, in0=end_s[:, :], scalar=1.0, in1=end_s[:, :], op0=ALU.mult,
                                        op1=ALU.mult, accum_out=col(C_X1)))
            link(v.tensor_scalar(col(C_X1), col(C_X1), -OOB, OOB, ALU.mult, ALU.add))
            link(v.tensor_tensor(fix_i[:, :], col(C_X0), col(C_X1), ALU.add))

            dve.wait_ge(ld_x, 48)
            with dve.Fori(0, NB) as b:
                for i in range(B):
                    c = b * B + i
                    v.bn_stats(stats[:, bass.ds(c * 6, 6)], big[:, bass.ds(c * D, D)]).then_inc(bn, 1)
            dve.wait_ge(bn, J)

            def norm(s6, s, d, q, var, between):
                between(v.tensor_tensor(s, s6[:, :, 1], s6[:, :, 4], ALU.add))
                between(v.tensor_tensor(d, s6[:, :, 1], s6[:, :, 4], ALU.subtract))
                between(v.tensor_tensor(q, s6[:, :, 2], s6[:, :, 5], ALU.add))
                between(v.tensor_tensor(d, d, d, ALU.mult))
                between(v.tensor_scalar(q, q, 1.0 / D, EPS, ALU.mult, ALU.add))
                between(v.scalar_tensor_tensor(out=var, in0=d, scalar=0.25, in1=q, op0=ALU.mult, op1=ALU.add))

            norm(stats.rearrange("p (j w) -> p j w", w=6), ta, tb, tc, tb, link)
            dve.sem_inc(sq_ask, 1)
            dve.wait_ge(sq_given, 2)
            link(v.reciprocal(rstd[:, :], td))
            link(v.scalar_tensor_tensor(out=shift[:, 0:J], in0=ta, scalar=-0.5, in1=rstd[:, :], op0=ALU.mult, op1=ALU.mult))

            dve.wait_ge(w_copied, 9)
            for i in range(B):
                pass
            link(v.tensor_tensor(nrow[0:1, 0:3 * D], brow[0:1, 0:3 * D], brow[0:1, 0:3 * D], ALU.max))
            link(v.tensor_tensor(hrow[0:1, :], hrow[0:1, :], brow[0:1, 3 * D:6 * D], ALU.add))
            link(v.tensor_tensor(nrow[0:1, 0:2 * D], nrow[0:1, 0:2 * D], hrow[0:1, 0:2 * D], ALU.add))
            link(v.tensor_copy(nrow[0:1, 3 * D:4 * D], hrow[0:1, 2 * D:3 * D]))
            link(v.tensor_copy(nrow[0:1, 4 * D:5 * D], brow[0:1, 6 * D:7 * D]))
            dve.sem_inc(w_bias, 1)

            dve.wait_ge(ld_node, 16)
            dve.wait_ge(w_done, 3)
            dve.sem_inc(node_ready, 1)

            def node_row(t, h):
                b = 2 * t + h
                rows_h = O[h][:, :].rearrange("p (i w) -> p i w", w=D + 2)
                dve.wait_ge(tw_s[h], 32 * t)
                v.tensor_copy(rows_h[:, :, D:D + 2], at(node_v, b, 2).rearrange("p (i w) -> p i w", w=2)).then_inc(tw_p, 1)
                dve.wait_ge(tw_h, 7 * b + 7)
                v.scalar_tensor_tensor(out=O2[h][:, :].rearrange("p (i w) -> p i w", w=D), in0=rows_h[:, :, 0:D],
                                       scalar=0.25, in1=at(big, b, D).rearrange("p (i w) -> p i w", w=D),
                                       op0=ALU.mult, op1=ALU.add).then_inc(tw_x, 1)

            def edge_row(b, h, more):
                dve.wait_ge(ed_g[h], 8 * B * (b + 2 - h))
                v.tensor_copy(at(edge_s, b, ED + 1), G[h][:, 0:B * (ED + 1)]).then_inc(ed_c, 1)
                if more:
                    dve.wait_ge(ed_c, b + 1)
                    v.tensor_copy(st[h][:, 0:B], at(perm_i, b + 2)).then_inc(ed_staged, 1)

            n0 = ED_PARTS[0][1]
            for h in range(2):
                v.tensor_copy(st[h][:, 0:B], perm_i[:, h * B:(h + 1) * B]).then_inc(ed_staged, 1)
            with dve.Fori(0, n0 - 1) as t:
                for e in range(2):
                    for h in range(2):
                        node_row(2 * t + e, h)
                    edge_row(2 * t + e, e, True)
            for e in range(2):
                for h in range(2):
                    node_row(2 * n0 - 2 + e, h)
                edge_row(2 * n0 - 2 + e, e, False)

            for k in range(3):
                s = SW[k]
                w = D + 2 if k == 0 else D
                if k == 1:
                    dve.wait_ge(zeroed, 16 * (NB + 3))
                if k:
                    dve.wait_ge(SW[k - 1].x, 14 + J)
                else:
                    dve.wait_ge(tw_x, NB)
                v.memset(R[1][:, (B - 1) * D:B * D], 0.0).then_inc(s.r, 1)
                v.memset(F[:, :], 0.0).then_inc(s.f, 1)
                with dve.Fori(0, IT) as t:
                    for h in range(2):
                        b = 2 * t + h
                        dve.wait_ge(s.g[h], 16 * B * (t + 1))
                        if k == 0:
                            gv = G[h][:, 0:B * w].rearrange("p (i w) -> p i w", w=w)
                            v.tensor_scalar(q7[h][0][:, :], gv[:, :, D + 1], TINY, None, ALU.max).then_inc(sw_small, 1)
                            v.tensor_copy(at(row_i, b), gv[:, :, D]).then_inc(sw_small, 1)
                            v.scalar_tensor_tensor(out=q7[h][2][:, :], in0=gv[:, :, D + 1], scalar=0.0, in1=at(ew, b),
                                                   op0=ALU.is_gt, op1=ALU.mult).then_inc(sw_small, 1)
                            dve.wait_ge(sw_sq, b + 1)
                            v.reciprocal(q7[h][3][:, :], q7[h][1][:, :]).then_inc(sw_small, 1)
                            dve.wait_ge(sw_small, 4 * b + 4)
                            v.tensor_tensor(at(w_e, b), q7[h][2][:, :], q7[h][3][:, :], ALU.mult).then_inc(sw_w, 1)
                        else:
                            wb = at(w_e, b).unsqueeze(2).to_broadcast([P, B, D])
                            vv = V[h][:, 0:B * D].rearrange("p (i w) -> p i w", w=D)
                            v.tensor_tensor(vv, G[h][:, 0:B * D].rearrange("p (i w) -> p i w", w=D), wb,
                                            ALU.mult).then_inc(sw_small, 1)
                            dve.wait_ge(sw_small, 4 * NB + (k - 1) * NB + b + 1)
                            v.tensor_tensor(V[h][:, 0:B * D], V[h][:, 0:B * D], at(big, b, D), ALU.add).then_inc(s.v, B)
                        dve.wait_ge(s.x, 14 * t + 7 * h + 7)

                        def finish(i):
                            c = b * B + i
                            dve.wait_ge(s.r, c + 2)
                            dve.wait_ge(s.f, c + 1)
                            v.scalar_tensor_tensor(out=F[:, 0:D], in0=R[h][:, i * D:(i + 1) * D],
                                                   scalar=end_d[:, bass.ds(c, 1)], in1=F[:, 0:D], op0=ALU.mult,
                                                   op1=ALU.add).then_inc(s.f, 1)

                        for i in range(B):
                            c = b * B + i
                            prev = R[h][:, (i - 1) * D:i * D] if i else R[1 - h][:, (B - 1) * D:B * D]
                            new = V[h][:, i * D:(i + 1) * D] if k else big[:, bass.ds(c * D, D)]
                            dve.wait_ge(s.v, c + 1 if k == 0 else 7 * b + 7)
                            dve.wait_ge(s.r, c + 1)
                            v.scalar_tensor_tensor(out=R[h][:, i * D:(i + 1) * D], in0=prev,
                                                   scalar=keep_d[:, bass.ds(c, 1)], in1=new, op0=ALU.mult,
                                                   op1=ALU.add).then_inc(s.r, 1)
                            if i:
                                finish(i - 1)
                        finish(B - 1)
                dve.wait_ge(s.r, J + 1)
                dve.wait_ge(s.f, J + 1)
                exchange()
                link(v.tensor_tensor_scan(co[0:D, 1:P + 1], cT[0:D, :], psC[0:D, 0:P], 0.0, ALU.mult, ALU.add))
                exchange()
                if k:
                    dve.wait_ge(fix_stored[k - 1], 16)
                link(v.scalar_tensor_tensor(out=fixr[:, 0:D], in0=psC[:, P:P + D], scalar=keep_d[:, 0:1], in1=F[:, 0:D],
                                            op0=ALU.mult, op1=ALU.add))
                link(v.tensor_scalar(fixr[:, 0:D], fixr[:, 0:D], col(C_DEND), None, ALU.mult))
                dve.sem_inc(fix_ready[k], 1)

            dve.wait_ge(SW[2].x, 14 + J)
            nv = node_v[:, :].rearrange("p (j w) -> p j w", w=2)
            link(v.tensor_copy(node_i[:, 0:J], nv[:, :, 0]))
            dve.sem_inc(nodes_listed, 1)
            dve.sem_inc(nu_h, 14)
            with dve.Fori(0, IT) as t:
                for h in range(2):
                    b = 2 * t + h
                    dve.wait_ge(nu_g[h], 16 * B * (t + 1))
                    dve.wait_ge(nu_l[h], 16 * (t + 1))
                    dve.wait_ge(nu_s[h], 32 * t)
                    dve.wait_ge(nu_h, 14 * t + 7 * h + 7)
                    count = [0]

                    def step(ins):
                        count[0] += 1
                        ins.then_inc(nu_d, 1)
                        dve.wait_ge(nu_d, 16 * b + count[0])

                    step(v.scalar_tensor_tensor(out=V[h][:, 0:B * D], in0=G[h][:, 0:B * D], scalar=0.25,
                                                in1=O2[h][:, :], op0=ALU.mult, op1=ALU.add))
                    for i in range(B):
                        v.bn_stats(st6[h][:, i * 6:(i + 1) * 6], V[h][:, i * D:(i + 1) * D]).then_inc(nu_d, 1)
                    count[0] += B
                    dve.wait_ge(nu_d, 16 * b + count[0])
                    q = q7[h]
                    norm(st6[h][:, :].rearrange("p (i w) -> p i w", w=6), q[2][:, :], q[3][:, :], q[0][:, :], q[4][:, :], step)
                    dve.wait_ge(nu_q, b + 1)
                    step(v.reciprocal(q[0][:, :], q[5][:, :]))
                    step(v.scalar_tensor_tensor(out=q[1][:, :], in0=q[2][:, :], scalar=-0.5, in1=q[0][:, :],
                                                op0=ALU.mult, op1=ALU.mult))

            dve.wait_ge(ed_c, NB)
            dve.wait_ge(nu_h, 14 + J)
            for h in range(2):
                dve.wait_ge(nu_s[h], 32 * IT)
            link(v.memset(F[:, :], 0.0))
            link(v.memset(m_all[:, 0:1], -BIG))
            v.memset(R[1][:, (B - 1) * (D + 1):B * (D + 1)], 0.0).then_inc(at_r, 1)
            v.tensor_scalar(dsts_i[:, 0:J], er[:, :, ED], float(NP - 1), None, ALU.min).then_inc(at_d, 1)
            dve.sem_inc(at_sc, 7)
            dve.wait_ge(w_done, 2)
            dve.wait_ge(pads, 5)
            with dve.Fori(0, IT) as t:
                for h in range(2):
                    b = 2 * t + h
                    w = D + 1
                    for i in range(B):
                        if i % 3 == 0:
                            dve.wait_ge(at_h, 7 * b + min(i + 3, B))
                        v.scalar_tensor_tensor(out=hh[h][i], in0=psH[i // 3][:, (i % 3) * H1:(i % 3 + 1) * H1],
                                               scalar=0.0, in1=w2bc[:, :], op0=ALU.max, op1=ALU.mult,
                                               accum_out=score[h][:, i:i + 1]).then_inc(at_sc, 1)
                    dve.wait_ge(at_sc, 7 * b + 14)
                    count = [1]

                    def step(ins):
                        count[0] += 1
                        ins.then_inc(at_d, 1)
                        dve.wait_ge(at_d, 7 * b + count[0])

                    sc, mp = q7[h][0][:, :], q7[h][1][:, :]
                    m_new, m_old = m_all[:, bass.ds(b * B + 1, B)], at(m_all, b)
                    step(v.tensor_scalar(sc, score[h][:, :], b2c[:, 0:1], None, ALU.add))
                    step(v.tensor_tensor_scan(m_new, at(start_s, b), sc, m_all[:, bass.ds(b * B, 1)], ALU.add, ALU.max))
                    step(v.tensor_tensor(mp, at(start_s, b), m_old, ALU.add))
                    step(v.tensor_tensor(q14[h][:, 0:B], mp, m_new, ALU.subtract))
                    step(v.tensor_tensor(q14[h][:, B:2 * B], sc, m_new, ALU.subtract))
                    step(v.tensor_scalar(q14[h][:, :], q14[h][:, :], EXP_MIN, None, ALU.max))
                    dve.wait_ge(at_e, b + 1)
                    vv = V[h][:, :].rearrange("p (i w) -> p i w", w=w)
                    step(v.tensor_copy(vv[:, :, D], e14[h][:, B:2 * B]))
                    dve.wait_ge(at_s[h], 16 * B * t)

                    def finish(i):
                        c = b * B + i
                        dve.wait_ge(at_r, c + 2)
                        dve.wait_ge(at_f, c)
                        v.scalar_tensor_tensor(out=F[:, :], in0=R[h][:, i * w:(i + 1) * w],
                                               scalar=end_s[:, bass.ds(c, 1)], in1=F[:, :], op0=ALU.mult,
                                               op1=ALU.add).then_inc(at_f, 1)

                    for i in range(B):
                        c = b * B + i
                        prev = R[h][:, (i - 1) * w:i * w] if i else R[1 - h][:, (B - 1) * w:B * w]
                        dve.wait_ge(at_v, c + 1)
                        dve.wait_ge(at_r, c + 1)
                        v.scalar_tensor_tensor(out=R[h][:, i * w:(i + 1) * w], in0=prev, scalar=e14[h][:, i:i + 1],
                                               in1=V[h][:, i * w:(i + 1) * w], op0=ALU.mult,
                                               op1=ALU.add).then_inc(at_r, 1)
                        if i:
                            finish(i - 1)
                    finish(B - 1)
            dve.wait_ge(at_r, J + 1)
            dve.wait_ge(at_f, J)
            link(v.memset(row1[:, 0:1], -BIG))
            exchange()
            link(v.tensor_copy(row2[0:1, 0:P], psC[0:1, P:2 * P]))
            link(v.tensor_tensor_scan(row1[:, 1:P + 1], row2[0:1, 0:P], psC[0:1, 0:P], -BIG, ALU.add, ALU.max))
            exchange()
            link(v.tensor_copy(cols[:, C_MCI:C_MCI + 2], psC[:, 2 * P:2 * P + 2]))
            link(v.scalar_tensor_tensor(out=ta, in0=end_s[:, :], scalar=1.0, in1=m_all[:, 1:J + 1], op0=ALU.mult,
                                        op1=ALU.mult, accum_out=col(C_ME)))
            link(v.tensor_tensor(col(C_X0), col(C_MCI), col(C_NBG), ALU.add))
            link(v.tensor_tensor(col(C_X1), col(C_ME), col(C_X0), ALU.max))
            link(v.tensor_tensor(col(C_T0), col(C_MCI), col(C_MCO), ALU.subtract))
            link(v.tensor_tensor(col(C_T1), m_all[:, J:J + 1], col(C_MCO), ALU.subtract))
            link(v.tensor_tensor(col(C_T2), col(C_X0), col(C_X1), ALU.subtract))
            link(v.tensor_tensor(col(C_T3), col(C_ME), col(C_X1), ALU.subtract))
            link(v.tensor_scalar(cols[:, C_T0:C_T0 + 4], cols[:, C_T0:C_T0 + 4], EXP_MIN, 0.0, ALU.max, ALU.min))
            dve.sem_inc(sq_ask, 1)
            dve.wait_ge(sq_given, 3)
            link(v.tensor_tensor(col(C_X0), col(C_CS), col(C_E0), ALU.mult))
            link(v.tensor_scalar(cbc[:, :], ones[:, 0:D + 1], col(C_X0), None, ALU.mult))
            link(v.tensor_scalar(V[0][:, 0:D + 1], R[1][:, (B - 1) * (D + 1):B * (D + 1)], col(C_E0 + 1), None, ALU.mult))
            exchange()
            link(v.tensor_copy(cT[:, :], psC[0:D + 1, P:2 * P]))
            link(v.tensor_tensor_scan(co[:, 1:P + 1], cT[:, :], psC[0:D + 1, 0:P], 0.0, ALU.mult, ALU.add))
            exchange()
            dve.wait_ge(fix_stored[2], 16)
            link(v.tensor_scalar(F[:, :], F[:, :], col(C_E0 + 3), None, ALU.mult))
            v.scalar_tensor_tensor(out=fixr[:, :], in0=psC[:, 2 * P:2 * P + D + 1], scalar=col(C_E0 + 2), in1=F[:, :],
                                   op0=ALU.mult, op1=ALU.add).then_inc(fix_ready[3], 2)

            dve.wait_ge(w_done, 3)
            dve.sem_inc(gr_p, 7)
            with dve.Fori(0, IT) as t:
                for h in range(2):
                    b = 2 * t + h
                    q = q7[h]
                    dve.wait_ge(gr_l[h], 48 * (t + 1))
                    count = [0]

                    def step(ins):
                        count[0] += 1
                        ins.then_inc(gr_d, 1)
                        dve.wait_ge(gr_d, 10 * b + count[0])

                    den = V[h][:, :].rearrange("p (i w) -> p i w", w=D + 1)[:, :, D]
                    step(v.tensor_scalar(q[0][:, :], den, 0.5, None, ALU.max))
                    step(v.tensor_scalar(q[2][:, :], den, 0.0, None, ALU.is_gt))
                    step(v.reciprocal(q[1][:, :], q[0][:, :]))
                    g = gates[h]
                    for i in range(B):
                        dve.wait_ge(gr_m, 7 * b + i + 1)
                        v.tensor_tensor(g[:, i, :], banks[i % 4][:, 0:5 * D], bias_n[:, :], ALU.add).then_inc(gr_p, 1)
                    dve.wait_ge(gr_a, 2 * b + 1)
                    r, z, n, hn, m = (g[:, :, k * D:(k + 1) * D] for k in range(5))
                    step(v.tensor_tensor(hn, hn, r, ALU.mult))
                    step(v.tensor_tensor(n, n, hn, ALU.add))
                    dve.wait_ge(gr_a, 2 * b + 2)
                    h2 = G[h][:, :].rearrange("p (i w) -> p i w", w=P)[:, :, 0:D]
                    step(v.tensor_tensor(m, m, n, ALU.subtract))
                    step(v.tensor_tensor(m, m, z, ALU.mult))
                    step(v.tensor_tensor(n, n, h2, ALU.subtract))
                    step(v.tensor_tensor(m, m, n, ALU.add))
                    step(v.tensor_tensor(m, m, q[2][:, :].unsqueeze(2).to_broadcast([P, B, D]), ALU.mult))
                    dve.wait_ge(gr_s[h], 48 * t)
                    o = O[h][:, 0:B * D].rearrange("p (i w) -> p i w", w=D)
                    v.tensor_tensor(o, m, h2, ALU.add).then_inc(gr_x, 1)
                    dve.wait_ge(gr_x, b + 1)
                    v.tensor_tensor(O[h][:, 0:B * D], O[h][:, 0:B * D], O2[h][:, :], ALU.add).then_inc(gr_o, 1)


_INS = ["x", "src", "dst", "edge_attr_16", "edge_weight", "L1_gnn_W_att1", "L1_gnn_b_att1", "L1_gnn_W_att2",
        "L1_gnn_b_att2", "L1_gnn_W_lin", "L1_gnn_b_lin", "L1_gnn_W_ih", "L1_gnn_b_ih", "L1_gnn_W_hh", "L1_gnn_b_hh"]


def kernel(**inputs):
    import numpy as _np
    import concourse.bacc as _bacc
    from concourse import mybir as _mybir
    from concourse.bass_utils import run_bass_kernel_spmd as _run

    nc = _bacc.Bacc("TRN2", target_bir_lowering=False, num_devices=1)
    arrays, args = {}, []
    for name in _INS:
        a = _np.ascontiguousarray(inputs[name])
        arrays[f"in_{name}_dram"] = a
        args.append(nc.dram_tensor(f"in_{name}_dram", a.shape, _mybir.dt.from_np(a.dtype), kind="ExternalInput").ap())
    out = nc.dram_tensor("out_0_dram", (N, D), F32, kind="ExternalOutput").ap()
    build(nc, *args, out)
    r = _run(nc, [arrays], core_ids=[0])
    return r.results[0]["out_0_dram"]
```

```python
from contextlib import ExitStack

import concourse.bass as bass
from concourse import mybir

F32 = mybir.dt.float32
I32 = mybir.dt.int32
U32 = mybir.dt.uint32
ALU = mybir.AluOpType
ACT = mybir.ActivationFunctionType
AX = mybir.AxisListType

P = 128
N = 50000
E = 50000
D = 64
ED = 16
H1 = 2 * D + ED
J = 392
NP = P * J
B = 7
NB = J // B
IT = NB // 2
FULL = N // J
REST = N - FULL * J
ROW_FIX = NP
ROW_ZERO = NP + P
ROWS = NP + 2 * P
PAD_KEY = 60000
OOB = 1000000.0
BIG = 1.0e30
TINY = 2.0 ** -116
EXP_MIN = -200.0
EPS = 1e-5
SORT = P * 512
SORT0 = SORT - NP


def build(nc, x, src, dst, edge_attr, edge_weight, W_att1, b_att1, W_att2, b_att2, W_lin, b_lin,
          W_ih, b_ih, W_hh, b_hh, out):
    with ExitStack() as ctx:
        def sb(name, shape, dt=F32):
            return ctx.enter_context(nc.sbuf_tensor(name, shape, dt))

        def sem(name):
            return ctx.enter_context(nc.semaphore(name))

        def dram(name, shape, dt=F32):
            return nc.dram_tensor(name, shape, dt, kind="Internal").ap()

        t_place = dram("t_place", [NP, 2])
        t_h = dram("t_h", [NP, D + 2])
        t_xa = dram("t_xa", [NP, D])
        t_u = [dram(f"t_u{k}", [ROWS, D]) for k in range(3)]
        t_sorted = dram("t_sorted", [SORT, 1], I32)
        t_edge = dram("t_edge", [NP, ED + 1])
        t_x2 = dram("t_x2", [NP, D])
        t_h2 = dram("t_h2", [NP, D])
        t_msg = dram("t_msg", [NP, D + 1])
        t_last = dram("t_last", [1, J * D])

        def rows(t):
            return t[0:NP, :].rearrange("(p j) f -> p (j f)", j=J)

        big = sb("big", [P, J * D])
        edge_s = sb("edge_s", [P, J * (ED + 1)])
        key_d = sb("key_d", [P, J + 2], I32)
        key_s = key_d
        src_i = sb("src_i", [P, J + 2 * B], I32)
        ew = sb("ew", [P, J])
        keep_d = sb("keep_d", [P, J])
        end_d = sb("end_d", [P, J])
        dinv = sb("dinv", [P, J])
        w_e = sb("w_e", [P, J])
        row_i = sb("row_i", [P, J + 2 * B], I32)
        place_v = sb("place_v", [P, J * 2])
        node_v = place_v
        node_i = src_i
        start_s = sb("start_s", [P, J])
        end_s = sb("end_s", [P, J])
        srcs_i = sb("srcs_i", [P, J + 2 * B], I32)
        dsts_i = sb("dsts_i", [P, J + 2 * B], I32)
        place_i = dsts_i
        perm_i = sb("perm_i", [P, J + 2 * B], I32)
        scat_i = sb("scat_i", [P, J + 2 * B], I32)
        m_all = sb("m_all", [P, 1 + J])
        tile_a = sb("tile_a", [P, J + 2])
        tile_b = sb("tile_b", [P, J + 2])
        tile_c = sb("tile_c", [P, J + 2])
        tile_d = sb("tile_d", [P, J + 2])
        rstd = w_e
        shift = m_all
        work = sb("work", [P, 6 * 512])
        sx = [work[:, k * 512:(k + 1) * 512] for k in range(2)]
        kx = work[:, 1024:1536].bitcast(I32)
        mask = work[:, 1536:2048].bitcast(U32)
        gray = work[:, 2048:2560].bitcast(U32)
        lin_i = work[:, 2560:3072].bitcast(U32)
        stats = edge_s[:, 0:6 * J]
        ident = sb("ident", [P, P])
        ones = sb("ones", [P, P])
        cols = sb("cols", [P, 40])
        pos = m_all[:, 0:J]
        fixrow = sb("fixrow", [P, 1])
        fix_i = sb("fix_i", [P, 1], I32)
        st = [sb(f"st{h}", [P, 2 * B], I32) for h in range(2)]
        sst = [sb(f"sst{h}", [P, B], I32) for h in range(2)]
        ea7 = [work[:, 1792 + h * B * ED:1792 + (h + 1) * B * ED] for h in range(2)]
        eaT = [work[0:B * ED, 2016 + h * P:2016 + (h + 1) * P] for h in range(2)]
        ftS = [work[:, h * B * P:(h + 1) * B * P] for h in range(2)]
        q14 = [sb(f"q14_{h}", [P, 2 * B]) for h in range(2)]
        e14 = [sb(f"e14_{h}", [P, 2 * B]) for h in range(2)]
        score = [sb(f"score{h}", [P, B]) for h in range(2)]
        sv = [sb(f"sv{h}", [P, 2 * B]) for h in range(2)]
        G = [sb(f"G{h}", [P, B * 128]) for h in range(2)]
        V = [sb(f"V{h}", [P, B * (D + 1)]) for h in range(2)]
        zrow = V[1][:, :]
        R = [sb(f"R{h}", [P, B * (D + 1)]) for h in range(2)]
        O = [sb(f"O{h}", [P, B * (D + 2)]) for h in range(2)]
        O2 = [sb(f"O2{h}", [P, B * D]) for h in range(2)]
        F = sb("F", [P, D + 1])
        q7 = [[sb(f"q7_{h}_{k}", [P, B]) for k in range(6)] for h in range(2)]
        st6 = [sb(f"st6_{h}", [P, B * 6]) for h in range(2)]
        row1 = sb("row1", [1, 3 * (P + 1)])
        row2 = sb("row2", [1, 2 * P])
        cT = sb("cT", [D + 1, P])
        co = sb("co", [D + 1, P + 1])
        fixr = sb("fixr", [P, D + 1])
        cbc = sb("cbc", [P, D + 1])
        wcat = G[1][:, 0:256].rearrange("p (k w) -> p k w", k=2)
        wea = G[1][:, 256:288].rearrange("p (k w) -> p k w", k=2)
        wih = G[1][:, 288:416].rearrange("p (k w) -> p k w", k=2)
        whh = G[1][:, 416:544].rearrange("p (k w) -> p k w", k=2)
        wlin = G[1][0:D, 544:672]
        whhT = G[1][0:D, 672:864]
        bcol = sb("bcol", [D, 1])
        rhs1 = sb("rhs1", [P, H1])
        rhs_e = sb("rhs_e", [B * ED, B * H1])
        w1e = sb("w1e", [ED, H1])
        b1row = sb("b1row", [1, H1])
        w2bc = sb("w2bc", [P, H1])
        bias_n = sb("bias_n", [P, 5 * D])
        brow = O2[1][0:1, :]
        nrow = O2[0][0:1, 0:5 * D]
        rowt = O[0][0:1, 3 * D:3 * D + H1]
        hrow = O[0][0:1, 0:3 * D]
        rhs_n = sb("rhs_n", [P, 5 * D])
        hh = [[big[:, (h * B + i) * H1:(h * B + i + 1) * H1] for i in range(B)] for h in range(2)]
        b2c = sb("b2c", [P, 1])

        ps = [ctx.enter_context(nc.psum_tensor(f"ps{k}", [P, 512], F32)) for k in range(8)]
        psT, psH, psE, psC = ps[0:2], ps[2:5], ps[5], ps[6]

        pads = sem("pads")
        pool_pads = sem("pool_pads")
        consts = sem("consts")
        ld_dst, ld_src, ld_ew, ld_x = sem("ld_dst"), sem("ld_src"), sem("ld_ew"), sem("ld_x")
        ld_ea, ld_key, ld_w, ld_node, ld_sorted = sem("ld_ea"), sem("ld_key"), sem("ld_w"), sem("ld_node"), sem("ld_sorted")
        zeroed = sem("zeroed")
        place_set = sem("place_set")
        place_pads = sem("place_pads")
        edge_ready = sem("edge_ready")
        edge_stored = sem("edge_stored")
        dv = sem("dv")
        ask = sem("ask")
        given = sem("given")
        sq_ask, sq_given = sem("sq_ask"), sem("sq_given")
        place_ready = sem("place_ready")
        sort_done = sem("sort_done")
        order_s = sem("order_s")
        node_ready = sem("node_ready")
        fix_ready = [sem(f"fix_ready{k}") for k in range(4)]
        fix_stored = [sem(f"fix_stored{k}") for k in range(4)]
        w_step = sem("w_step")
        w_copied = sem("w_copied")
        w_bias = sem("w_bias")
        w_done = sem("w_done")
        zset = sem("zset")
        nodes_listed = sem("nodes_listed")
        rhs_zero, e_placed = sem("rhs_zero"), sem("e_placed")
        bn = sem("bn")
        order_sp = sem("order_sp")
        order = sem("order")
        ps_staged, ps_s = sem("ps_staged"), [sem(f"ps_s{h}") for h in range(2)]
        tw_h, tw_p, tw_x, tw_s = sem("tw_h"), sem("tw_p"), sem("tw_x"), [sem(f"tw_s{h}") for h in range(2)]
        ed_staged, ed_g, ed_c = sem("ed_staged"), [sem(f"ed_g{h}") for h in range(2)], sem("ed_c")

        class Sweep:
            def __init__(self, name):
                self.staged = sem(name + "_staged")
                self.g = [sem(f"{name}_g{h}") for h in range(2)]
                self.v = sem(name + "_v")
                self.r = sem(name + "_r")
                self.f = sem(name + "_f")
                self.x = sem(name + "_x")
                self.s = [sem(f"{name}_s{h}") for h in range(2)]

        SW = [Sweep(f"l{k}") for k in range(3)]
        sw_small = sem("sw_small")
        sw_sq = sem("sw_sq")
        sw_w = sem("sw_w")
        nu_staged, nu_g, nu_l = sem("nu_staged"), [sem(f"nu_g{h}") for h in range(2)], [sem(f"nu_l{h}") for h in range(2)]
        nu_d, nu_q, nu_h, nu_s = sem("nu_d"), sem("nu_q"), sem("nu_h"), [sem(f"nu_s{h}") for h in range(2)]
        at_staged, at_g = sem("at_staged"), [sem(f"at_g{h}") for h in range(2)]
        at_ea, at_t, at_c, at_h, at_sc = sem("at_ea"), sem("at_t"), sem("at_c"), sem("at_h"), sem("at_sc")
        at_d, at_e, at_v, at_r, at_f, at_s = sem("at_d"), sem("at_e"), sem("at_v"), sem("at_r"), sem("at_f"), [sem(f"at_s{h}") for h in range(2)]
        gr_lv, gr_lc = [sem(f"gr_lv{k}") for k in range(4)], [sem(f"gr_lc{k}") for k in range(4)]
        gr_den = sem("gr_den")
        gr_u = sem("gr_u")
        gr_t, gr_c = sem("gr_t"), sem("gr_c")
        gr_m, gr_p = sem("gr_m"), sem("gr_p")
        gr_sig, gr_n, gr_tanh = sem("gr_sig"), sem("gr_n"), sem("gr_tanh")
        gr_base, gr_nh, gr_mix = sem("gr_base"), sem("gr_nh"), sem("gr_mix")
        gr_o = sem("gr_o")
        gr_s = [sem(f"gr_s{h}") for h in range(2)]
        at_ss = sem("at_ss")
        last_out = sem("last_out")

        C_C, C_IN, C_DEND, C_G0S, C_CS, C_NBC, C_NBG, C_MCI, C_MCO, C_ME, C_X0, C_X1, C_T0, C_T1, C_T2, C_T3, C_E0 = range(17)

        def col(k):
            return cols[:, k:k + 1]

        def at(tile, b, w=1, n=B):
            return tile[:, bass.ds(b * (n * w), n * w)]

        def ring(start, n):
            return [big[:, start + k * n:start + (k + 1) * n] for k in range(4)]

        cat = ring(0, B * P)
        h2_g = [cat[k].rearrange("p (i w) -> p i w", w=P)[:, :, 0:D] for k in range(4)]
        msg_g = ring(4 * B * P, B * (D + 1))
        x2_g = ring(4 * B * (P + D + 1), B * D)
        gates = [g.rearrange("p (i w) -> p i w", w=5 * D) for g in ring(4 * B * (P + 2 * D + 1), B * 5 * D)]
        recip = ring(4 * B * (P + 7 * D + 1), B)
        flag = ring(4 * B * (P + 7 * D + 2), B)
        banks = [psH[0], psH[1], psH[2], psE, psC, ps[7]]

        def parts(k):
            return [gates[k][:, :, g * D:(g + 1) * D] for g in range(5)]

        def ahead(q, k, d):
            return q + (k + d) // 4, (k + d) % 4

        def last_load(q, k, d):
            return isinstance(q, int) and 4 * q + k + d >= NB

        def gru_loop(engine, step):
            for s in range(4):
                step(0, s, s == 0, 0)
            with engine.Fori(1, NB // 4 - 1) as t:
                for k in range(4):
                    step(t, k, False, 0)
            for s in range(NB - 4, NB + 1):
                step(s // 4, s % 4, False, max(0, s + 3 - NB))

        ED_PARTS = [(0, 14), (28, 5), (38, 4), (46, 5)]

        block = ctx.enter_context(nc.Block())

        @block.sync
        def _(sp):
            def load(tile, c0, src_flat, w, s):
                for a, b in ((0, 112), (112, FULL)):
                    sp.dma_start(tile[a:b, c0:c0 + J * w],
                                 src_flat[a * J * w:b * J * w].rearrange("(p j) -> p j", j=J * w)).then_inc(s, 16)
                sp.dma_start(tile[FULL:P, c0:c0 + REST * w],
                             src_flat[FULL * J * w:].rearrange("(p j) -> p j", j=REST * w)).then_inc(s, 16)

            sp.wait_ge(pads, 4)
            load(key_d, 1, dst, 1, ld_dst)
            sp.dma_start(key_d[1:P, 0:1], dst[J - 1:FULL * J:J].rearrange("(p a) -> p a", a=1), allow_slow_non_contiguous=True).then_inc(ld_dst, 16)
            sp.dma_start(key_d[0:FULL, J + 1:J + 2], dst[J:FULL * J + 1:J].rearrange("(p a) -> p a", a=1), allow_slow_non_contiguous=True).then_inc(ld_dst, 16)
            load(ew, 0, edge_weight, 1, ld_ew)
            load(src_i, 0, src, 1, ld_src)
            sp.dma_start(kx[0:96, :], src[0:96 * 512].rearrange("(p j) -> p j", j=512)).then_inc(ld_key, 16)
            sp.dma_start(kx[96:97, :], src[96 * 512:97 * 512].rearrange("(p j) -> p j", j=512)).then_inc(ld_key, 16)
            sp.dma_start(kx[97:98, 0:E - 97 * 512], src[97 * 512:].rearrange("(p j) -> p j", j=E - 97 * 512)).then_inc(ld_key, 16)
            sp.wait_ge(place_pads, 1)
            sp.dma_start(rows(t_place), place_v[:, :]).then_inc(place_set, 16)
            sp.wait_ge(pool_pads, 2)
            load(big, 0, x.rearrange("n f -> (n f)"), D, ld_x)
            er = edge_s[:, :].rearrange("p (j w) -> p j w", w=ED + 1)
            for a, b, n in ((0, 112, J), (112, FULL, J), (FULL, P, REST)):
                sp.dma_start(er[a:b, 0:n, 0:ED],
                             edge_attr[a * J:a * J + (b - a) * n, :].rearrange("(p j) f -> p j f", j=n)).then_inc(ld_ea, 16)
            sp.wait_ge(zset, 2)
            for k, (a, b) in enumerate(((0, P), (P, H1))):
                sp.dma_start(wcat[0:b - a, k, 0:D], W_att1[a:b, 0:D]).then_inc(ld_w, 16)
                sp.dma_start(wcat[0:b - a, k, D:P], W_att1[a:b, D + ED:H1]).then_inc(ld_w, 16)
                sp.dma_start(wea[0:b - a, k, :], W_att1[a:b, D:D + ED]).then_inc(ld_w, 16)
            for k, (a, b) in enumerate(((0, P), (P, 3 * D))):
                sp.dma_start(wih[0:b - a, k, :], W_ih[a:b, :]).then_inc(ld_w, 16)
                sp.dma_start(whh[0:b - a, k, :], W_hh[a:b, :]).then_inc(ld_w, 16)
            sp.dma_start(wlin[:, D:P], W_lin).then_inc(ld_w, 16)
            sp.dma_start(bcol[:, :], b_lin.rearrange("(p a) -> p a", a=1)).then_inc(ld_w, 16)
            for t, c, v, n in ((brow, 0, b_ih, 3 * D), (brow, 3 * D, b_hh, 3 * D), (brow, 6 * D, b_lin, D),
                               (b1row, 0, b_att1, H1), (rowt, 0, W_att2.rearrange("a b -> (a b)"), H1),
                               (row2, 2 * P - 1, b_att2, 1)):
                sp.dma_start(t[0:1, c:c + n], v.rearrange("(a n) -> a n", a=1)).then_inc(ld_w, 16)
            for k in range(3):
                sp.dma_start(t_u[k][ROW_ZERO:ROWS, :], zrow[:, 0:D]).then_inc(zeroed, 16)
            msg_rows = rows(t_msg)
            with sp.Fori(0, NB) as b:
                sp.dma_start(at(msg_rows, b, D + 1), zrow[:, :]).then_inc(zeroed, 16)
            sp.wait_ge(edge_ready, 1)
            sp.dma_start(rows(t_edge), edge_s[:, :]).then_inc(edge_stored, 16)
            sp.wait_ge(sort_done, 1)
            flat = t_sorted.rearrange("n a -> (n a)")
            sp.dma_start(flat.rearrange("(p j) -> p j", j=512), sx[0][:, :].bitcast(I32)).then_inc(ld_sorted, 16)
            sp.wait_ge(ld_sorted, 16)
            sp.dma_start(key_s[:, 1:J + 1], flat[SORT0:].rearrange("(p j) -> p j", j=J)).then_inc(ld_sorted, 16)
            sp.dma_start(key_s[1:P, 0:1], t_sorted[SORT0 + J - 1:SORT - 1:J, :], allow_slow_non_contiguous=True).then_inc(ld_sorted, 16)
            sp.dma_start(key_s[0:P - 1, J + 1:J + 2], t_sorted[SORT0 + J:SORT:J, :], allow_slow_non_contiguous=True).then_inc(ld_sorted, 16)
            sp.wait_ge(w_copied, 3)
            sp.wait_ge(rhs_zero, 1)
            for i in range(B):
                sp.dma_start(rhs_e[i * ED:(i + 1) * ED, i * H1:(i + 1) * H1], w1e[:, :]).then_inc(e_placed, 16)
            for h in range(2):
                sp.wait_ge(ps_s[h], 16 * B * IT)
            sp.dma_start(node_v[:, :], rows(t_place)).then_inc(ld_node, 16)
            h_rows, xa_rows = rows(t_h), rows(t_xa)
            with sp.Fori(0, IT) as t:
                for h in range(2):
                    sp.wait_ge(tw_h, 14 * t + 7 * h + 7)
                    sp.sem_inc(order_sp, 1)
                    sp.wait_ge(tw_p, 2 * t + h + 1)
                    sp.sem_inc(order_sp, 1)
                    sp.dma_start(at(h_rows, 2 * t + h, D + 2), O[h][:, :]).then_inc(tw_s[h], 16)
                    sp.wait_ge(tw_x, 2 * t + h + 1)
                    sp.sem_inc(order_sp, 1)
                    sp.dma_start(at(xa_rows, 2 * t + h, D), O2[h][:, :]).then_inc(tw_s[h], 16)
            for k in range(3):
                s, u_rows = SW[k], rows(t_u[k])
                with sp.Fori(0, IT) as t:
                    for h in range(2):
                        sp.wait_ge(s.x, 14 + 14 * t + 7 * h + 7)
                        sp.sem_inc(order_sp, 1)
                        sp.dma_start(at(u_rows, 2 * t + h, D), O[h][:, 0:B * D]).then_inc(s.s[h], 16)
                sp.wait_ge(fix_ready[k], 1)
                sp.dma_start(t_u[k][ROW_FIX:ROW_FIX + P, :], fixr[:, 0:D]).then_inc(fix_stored[k], 16)
            x2_rows, h2_rows = rows(t_x2), rows(t_h2)
            for h in range(2):
                sp.dma_start(O2[h][:, :], xa_rows[:, h * B * D:(h + 1) * B * D]).then_inc(nu_l[h], 16)

            def nu_store(b, h, last):
                sp.wait_ge(nu_h, 7 * b + 21)
                sp.sem_inc(order_sp, 1)
                sp.dma_start(at(x2_rows, b, D), V[h][:, 0:B * D]).then_inc(nu_s[h], 16)
                sp.dma_start(at(h2_rows, b, D), R[h][:, 0:B * D]).then_inc(nu_s[h], 16)
                if not last:
                    sp.dma_start(O2[h][:, :], at(xa_rows, b + 2, D)).then_inc(nu_l[h], 16)

            with sp.Fori(0, IT - 1) as t:
                for h in range(2):
                    nu_store(2 * t + h, h, False)
            for h in range(2):
                nu_store(NB - 2 + h, h, True)
            for h in range(2):
                sp.wait_ge(at_s[h], 16 * B * IT)
            sp.wait_ge(fix_stored[3], 16)
            out_rows = out[0:FULL * J, :].rearrange("(p j) f -> p (j f)", j=J)

            def load_msg(q, k, d):
                q, k = ahead(q, k, d)
                sp.dma_start(msg_g[k], at(msg_rows, 4 * q + k, D + 1)).then_inc(gr_lv[k], 16)

            def load_rows(q, k, d):
                q, k = ahead(q, k, d)
                b = 4 * q + k
                sp.dma_start(h2_g[k], at(h2_rows, b, D).rearrange("p (j w) -> p j w", w=D)).then_inc(gr_lc[k], 16)
                sp.dma_start(x2_g[k], at(x2_rows, b, D)).then_inc(gr_lc[k], 16)

            def gru_step(q, k, first, last):
                if last < 1:
                    if not last_load(q, k, 4):
                        sp.wait_ge(gr_u, 7 * (4 * q + k) + 7)
                        sp.sem_inc(order_sp, 1)
                        load_msg(q, k, 4)
                if not first:
                    q1, k1 = ahead(q, k, -1)
                    b, h = 4 * q1 + k1, k1 % 2
                    sp.wait_ge(gr_o, b + 1)
                    sp.sem_inc(order_sp, 1)
                    sp.dma_start(at(out_rows[0:112, :], b, D), O[h][0:112, 0:B * D]).then_inc(gr_s[h], 16)
                    sp.dma_start(at(out_rows[112:FULL, :], b, D), O[h][112:FULL, 0:B * D]).then_inc(gr_s[h], 16)
                    sp.dma_start(at(t_last, b, D), O[h][FULL:P, 0:B * D]).then_inc(gr_s[h], 16)
                    if not last_load(q1, k1, 4):
                        load_rows(q1, k1, 4)

            for k in range(4):
                load_msg(0, k, 0)
                load_rows(0, k, 0)
            gru_loop(sp, gru_step)
            for h in range(2):
                sp.wait_ge(gr_s[h], 48 * IT)
            sp.dma_start(out[FULL * J:N, :].rearrange("(a j) f -> a (j f)", a=1), t_last[:, 0:REST * D]).then_inc(last_out, 16)
            sp.wait_ge(last_out, 16)

        @block.gpsimd
        def _(pool):
            def gather(dst_ap, table, idx, bound, s):
                pool.indirect_dma_start(out=dst_ap, out_offset=None, in_=table,
                                        in_offset=bass.IndirectOffsetOnAxis(ap=idx, axis=0),
                                        bounds_check=bound, oob_is_err=False).then_inc(s, 16)

            def scatter(table, src_ap, idx, bound, s):
                pool.indirect_dma_start(out=table, out_offset=bass.IndirectOffsetOnAxis(ap=idx, axis=0), in_=src_ap,
                                        in_offset=None, bounds_check=bound, oob_is_err=False).then_inc(s, 16)

            pool.memset(ident[:, :], 0.0).then_inc(consts, 1)
            pool.iota(lin_i[:, :], pattern=[[1, 512]], base=0, channel_multiplier=512).then_inc(consts, 1)
            pool.iota(pos[:, :], pattern=[[1, J]], base=0, channel_multiplier=J,
                      allow_small_or_imprecise_dtypes=True).then_inc(consts, 1)
            pool.iota(fixrow[:, :], pattern=[[0, 1]], base=ROW_FIX, channel_multiplier=1,
                      allow_small_or_imprecise_dtypes=True).then_inc(consts, 1)
            pool.memset(ones[:, :], 1.0).then_inc(consts, 1)
            pool.wait_ge(consts, 5)
            pool.affine_select(out=ident[:, :], in_=ident[:, :], compare_op=ALU.not_equal, fill=1.0, base=0,
                               pattern=[[-1, P]], channel_multiplier=1).then_inc(consts, 1)
            pool.wait_ge(consts, 6)
            pool.memset(big[96:P, REST * D:J * D], 0.0).then_inc(pool_pads, 1)
            pool.wait_ge(pool_pads, 1)
            pool.memset(edge_s[96:P, REST * (ED + 1):J * (ED + 1)], 0.0).then_inc(pool_pads, 1)

            pool.wait_ge(pool_pads, 2)
            pool.wait_ge(place_set, 16)
            with pool.Fori(0, IT) as t:
                for h in range(2):
                    pool.wait_ge(ps_staged, 2 * (2 * t + h) + 2)
                    pool.sem_inc(order, 1)
                    for i in range(B):
                        scatter(t_place, sv[h][:, 2 * i:2 * i + 2], st[h][:, i:i + 1], NP - 1, ps_s[h])

            def edge_part(k):
                b0, n = ED_PARTS[k]
                with pool.Fori(0, n) as t:
                    for h in range(2):
                        pool.wait_ge(ed_staged, b0 + 2 * t + h + 1)
                        pool.sem_inc(order, 1)
                        for i in range(B):
                            w = ED + 1
                            gather(G[h][:, w * i:w * i + w], t_edge, st[h][:, i:i + 1], NP - 1, ed_g[h])

            pool.wait_ge(ld_w, 16 * 18)
            pool.partition_broadcast(w2bc[:, :], rowt[0:1, :]).then_inc(w_done, 1)
            pool.partition_broadcast(b2c[:, :], row2[0:1, 2 * P - 1:2 * P]).then_inc(w_done, 1)
            pool.wait_ge(w_bias, 1)
            pool.partition_broadcast(bias_n[:, :], nrow[0:1, :]).then_inc(w_done, 1)
            pool.wait_ge(edge_stored, 16)
            pool.wait_ge(w_copied, 9)
            edge_part(0)
            for h in range(2):
                pool.wait_ge(tw_s[h], 32 * IT)
            for k in range(3):
                s = SW[k]
                w = D + 2 if k == 0 else D
                if k:
                    for h in range(2):
                        pool.wait_ge(SW[k - 1].s[h], 16 * IT)
                    pool.wait_ge(fix_stored[k - 1], 16)
                with pool.Fori(0, IT) as t:
                    for h in range(2):
                        pool.wait_ge(s.staged, 2 * t + h + 1)
                        pool.sem_inc(order, 1)
                        for i in range(B):
                            if k == 0:
                                gather(G[h][:, w * i:w * i + w], t_h, st[h][:, i:i + 1], NP - 1, s.g[h])
                            else:
                                gather(G[h][:, w * i:w * i + w], t_u[k - 1], st[h][:, i:i + 1], ROWS - 1, s.g[h])
                edge_part(k + 1)
            for h in range(2):
                pool.wait_ge(SW[2].s[h], 16 * IT)
            pool.wait_ge(fix_stored[2], 16)
            with pool.Fori(0, IT) as t:
                for h in range(2):
                    pool.wait_ge(nu_staged, 2 * t + h + 1)
                    pool.sem_inc(order, 1)
                    for i in range(B):
                        gather(G[h][:, D * i:D * i + D], t_u[2], st[h][:, i:i + 1], ROWS - 1, nu_g[h])

            for h in range(2):
                pool.wait_ge(nu_s[h], 32 * IT)
            pool.wait_ge(zeroed, 16 * (NB + 3))

            def at_gather(b, h):
                pool.wait_ge(at_staged, 2 * b + 2)
                pool.sem_inc(order, 1)
                for i in range(B):
                    gather(G[h][:, P * i:P * i + D], t_h2, st[h][:, i:i + 1], NP - 1, at_g[h])
                    gather(G[h][:, P * i + D:P * i + P], t_h2, st[h][:, B + i:B + i + 1], NP - 1, at_g[h])

            def at_scatter(b, h):
                w = D + 1
                pool.wait_ge(at_ss, b + 1)
                pool.wait_ge(at_r, 7 * b + 8)
                pool.sem_inc(order, 1)
                for i in range(B):
                    scatter(t_msg, R[h][:, w * i:w * i + w], sst[h][:, i:i + 1], NP - 1, at_s[h])

            at_gather(0, 0)
            with pool.Fori(0, IT - 1) as t:
                at_gather(2 * t + 1, 1)
                at_scatter(2 * t, 0)
                at_gather(2 * t + 2, 0)
                at_scatter(2 * t + 1, 1)
            at_gather(NB - 1, 1)
            at_scatter(NB - 2, 0)
            at_scatter(NB - 1, 1)
            pool.wait_ge(fix_ready[3], 2)
            scatter(t_msg, fixr[:, :], fix_i[:, :], NP - 1, fix_stored[3])

            def add_x2(q, k, d):
                q, k = ahead(q, k, d)
                pool.wait_ge(gr_lc[k], 32 * (q + 1))
                pool.sem_inc(order, 1)
                pool.tensor_tensor(x2_g[k].rearrange("p (i w) -> p i w", w=D), x2_g[k].rearrange("p (i w) -> p i w", w=D),
                                   h2_g[k], ALU.add).then_inc(gr_base, 1)

            def gru_step(q, k, first, last):
                if last < 2:
                    add_x2(q, k, 1)
                if not first:
                    q1, k1 = ahead(q, k, -1)
                    b, h = 4 * q1 + k1, k1 % 2
                    r, z, n, hn, m = parts(k1)
                    pool.wait_ge(gr_tanh, b + 1)
                    pool.sem_inc(order, 1)
                    pool.tensor_tensor(hn, n, h2_g[k1], ALU.subtract).then_inc(gr_nh, 1)
                    if not (isinstance(b, int) and b < 2):
                        pool.wait_ge(gr_s[h], 48 * (2 * q1 + k1 // 2))
                        pool.sem_inc(order, 1)
                    pool.wait_ge(gr_mix, 4 * b + 4)
                    pool.sem_inc(order, 1)
                    pool.wait_ge(gr_base, b + 1)
                    pool.sem_inc(order, 1)
                    pool.tensor_tensor(O[h][:, 0:B * D].rearrange("p (i w) -> p i w", w=D), m,
                                       x2_g[k1].rearrange("p (i w) -> p i w", w=D), ALU.add).then_inc(gr_o, 1)

            add_x2(0, 0, 0)
            gru_loop(pool, gru_step)

        @block.scalar
        def _(act):
            S = nc.scalar

            def stage(b, h, lists, s):
                for k, lst in enumerate(lists):
                    S.copy(st[h][:, k * B:k * B + B], at(lst, b)).then_inc(s, 1)

            act.wait_ge(sq_ask, 1)
            S.activation(tile_d[:, 0:J], tile_b[:, 0:J], ACT.Sqrt).then_inc(sq_given, 1)
            act.wait_ge(place_ready, 1)
            with act.Fori(0, IT) as t:
                for h in range(2):
                    act.wait_ge(ps_s[h], 16 * B * t)
                    S.copy(st[h][:, 0:B], at(dsts_i, 2 * t + h)).then_inc(ps_staged, 1)
                    S.copy(sv[h][:, :], at(place_v, 2 * t + h, 2)).then_inc(ps_staged, 1)
            act.wait_ge(sq_ask, 2)
            S.activation(tile_d[:, 0:J], tile_b[:, 0:J], ACT.Sqrt).then_inc(sq_given, 1)

            act.wait_ge(w_step, 1)
            S.copy(rhs1[:, 0:P], psH[0][:, 0:P]).then_inc(w_copied, 1)
            S.copy(rhs1[:, P:H1], psH[0][:, P:H1]).then_inc(w_copied, 1)
            S.copy(w1e[:, :], psH[1][0:ED, 0:H1]).then_inc(w_copied, 1)
            S.copy(whhT[:, :], psH[2][0:D, 0:3 * D]).then_inc(w_copied, 1)
            S.copy(rhs_n[0:D, 0:3 * D], psE[0:D, 0:3 * D]).then_inc(w_copied, 1)
            act.wait_ge(w_step, 2)
            S.copy(rhs_n[D:P, 0:2 * D], psH[0][D:P, 0:2 * D]).then_inc(w_copied, 1)
            S.copy(rhs_n[D:P, 3 * D:4 * D], psH[0][D:P, 2 * D:3 * D]).then_inc(w_copied, 1)
            S.copy(rhs_n[D:P, 4 * D:5 * D], psH[1][D:P, 0:D]).then_inc(w_copied, 1)
            S.copy(hrow[0:1, :], psH[2][0:1, 0:3 * D]).then_inc(w_copied, 1)

            act.wait_ge(node_ready, 1)
            with act.Fori(0, IT) as t:
                for h in range(2):
                    act.wait_ge(tw_s[h], 32 * t)
                    for i in range(B):
                        c = (2 * t + h) * B + i
                        S.activation(O[h][:, i * (D + 2):i * (D + 2) + D], big[:, bass.ds(c * D, D)], ACT.Relu,
                                     bias=shift[:, bass.ds(c, 1)], scale=rstd[:, bass.ds(c, 1)]).then_inc(tw_h, 1)

            def edge_part(k):
                b0, n = ED_PARTS[k]
                for h in range(2):
                    S.copy(st[h][:, 0:B], perm_i[:, (b0 + h) * B:(b0 + h + 1) * B]).then_inc(ed_staged, 1)

                def take(b, h, more):
                    act.wait_ge(ed_g[h], 8 * B * (b + 2 - h))
                    S.copy(at(edge_s, b, ED + 1), G[h][:, 0:B * (ED + 1)]).then_inc(ed_c, 1)
                    if more:
                        act.wait_ge(ed_c, b + 1)
                        S.copy(st[h][:, 0:B], at(perm_i, b + 2)).then_inc(ed_staged, 1)

                with act.Fori(0, n - 1) as t:
                    for h in range(2):
                        take(b0 + 2 * t + h, h, True)
                for h in range(2):
                    take(b0 + 2 * n - 2 + h, h, False)

            for k in range(3):
                s = SW[k]
                lst = src_i if k == 0 else row_i
                w = D + 2 if k == 0 else D
                if k == 0:
                    for h in range(2):
                        act.wait_ge(ed_g[h], 16 * B * ED_PARTS[0][1])
                    act.wait_ge(ed_c, 2 * ED_PARTS[0][1])
                    act.wait_ge(tw_x, NB)
                    act.wait_ge(ld_src, 48)
                S.copy(st[0][:, 0:B], lst[:, 0:B]).then_inc(s.staged, 1)
                S.copy(st[1][:, 0:B], lst[:, B:2 * B]).then_inc(s.staged, 1)
                act.sem_inc(s.x, 14)
                with act.Fori(0, IT) as t:
                    for h in range(2):
                        b = 2 * t + h
                        if k == 0:
                            act.wait_ge(sw_small, 4 * b + 1)
                            S.activation(q7[h][1][:, :], q7[h][0][:, :], ACT.Sqrt).then_inc(sw_sq, 1)
                            act.wait_ge(sw_w, b + 1)
                            for i in range(B):
                                c = b * B + i
                                S.activation(big[:, bass.ds(c * D, D)], G[h][:, w * i:w * i + D], ACT.Copy,
                                             scale=w_e[:, bass.ds(c, 1)]).then_inc(s.v, 1)
                        act.wait_ge(s.v, 7 * b + 7)
                        act.wait_ge(s.g[h], 16 * B * (t + 1))
                        S.copy(st[h][:, 0:B], at(lst, b + 2)).then_inc(s.staged, 1)
                        act.wait_ge(s.s[h], 16 * t)
                        for i in range(B):
                            c = b * B + i
                            act.wait_ge(s.r, 7 * b + i + 2)
                            S.activation(O[h][:, D * i:D * i + D], R[h][:, D * i:D * i + D], ACT.Copy,
                                         scale=dinv[:, bass.ds(c, 1)]).then_inc(s.x, 1)
                act.wait_ge(s.staged, NB + 2)
                edge_part(k + 1)

            act.wait_ge(nodes_listed, 1)
            S.copy(st[0][:, 0:B], node_i[:, 0:B]).then_inc(nu_staged, 1)
            S.copy(st[1][:, 0:B], node_i[:, B:2 * B]).then_inc(nu_staged, 1)
            with act.Fori(0, IT) as t:
                for h in range(2):
                    b = 2 * t + h
                    act.wait_ge(nu_d, 16 * b + 1)
                    act.wait_ge(nu_g[h], 16 * B * (t + 1))
                    S.copy(st[h][:, 0:B], at(node_i, b + 2)).then_inc(nu_staged, 1)
                    act.wait_ge(nu_d, 16 * b + 14)
                    S.activation(q7[h][5][:, :], q7[h][4][:, :], ACT.Sqrt).then_inc(nu_q, 1)
                    act.wait_ge(nu_d, 16 * b + 16)
                    act.wait_ge(nu_s[h], 32 * t)
                    for i in range(B):
                        S.activation(R[h][:, D * i:D * i + D], V[h][:, D * i:D * i + D], ACT.Relu,
                                     bias=q7[h][1][:, i:i + 1], scale=q7[h][0][:, i:i + 1]).then_inc(nu_h, 1)

            def stage_at(b, h):
                for k, lst in enumerate((srcs_i, dsts_i)):
                    S.copy(st[h][:, k * B:k * B + B], at(lst, b)).then_inc(at_staged, 1)

            act.wait_ge(at_d, 1)
            act.wait_ge(nu_staged, NB + 2)
            for h in range(2):
                act.wait_ge(nu_g[h], 16 * B * IT)
                stage_at(h, h)
            with act.Fori(0, IT) as t:
                for h in range(2):
                    b = 2 * t + h
                    ea = at(edge_s, b, ED + 1).rearrange("p (j w) -> p j w", w=ED + 1)[:, :, 0:ED]
                    S.copy(ea7[h][:, :].rearrange("p (j w) -> p j w", w=ED), ea).then_inc(at_ea, 1)
                    act.wait_ge(at_t, 3 * b + 1)
                    S.copy(ftS[h][:, 0:512], psT[0][:, :]).then_inc(at_c, 1)
                    act.wait_ge(at_t, 3 * b + 2)
                    S.copy(ftS[h][:, 512:B * P], psT[1][:, 0:B * P - 512]).then_inc(at_c, 1)
                    act.wait_ge(at_t, 3 * b + 3)
                    S.copy(eaT[h][:, :], psE[0:B * ED, 0:P]).then_inc(at_c, 1)
                    act.wait_ge(at_d, 7 * b + 7)
                    S.activation(e14[h][:, :], q14[h][:, :], ACT.Exp).then_inc(at_e, 1)
                    act.wait_ge(at_e, b + 1)
                    for i in range(B):
                        S.activation(V[h][:, i * (D + 1):i * (D + 1) + D], G[h][:, i * P + D:i * P + P], ACT.Copy,
                                     scale=e14[h][:, B + i:B + i + 1]).then_inc(at_v, 1)
                    act.wait_ge(at_s[h], 16 * B * t)
                    S.copy(sst[h][:, :], at(scat_i, b)).then_inc(at_ss, 1)
                    act.wait_ge(at_v, 7 * b + 7)
                    act.wait_ge(at_g[h], 32 * B * (t + 1))
                    stage_at(b + 2, h)
            act.wait_ge(sq_ask, 3)
            S.activation(cols[:, C_E0:C_E0 + 4], cols[:, C_T0:C_T0 + 4], ACT.Exp).then_inc(sq_given, 1)

            def scale_msg(q, k, d):
                q, k = ahead(q, k, d)
                b = 4 * q + k
                act.wait_ge(gr_den, 3 * b + 3)
                if not (isinstance(b, int) and b < 4):
                    act.wait_ge(gr_t, 2 * (b - 3))
                for i in range(B):
                    S.activation(cat[k][:, i * P + D:i * P + P], msg_g[k][:, i * (D + 1):i * (D + 1) + D], ACT.Copy,
                                 scale=recip[k][:, i:i + 1]).then_inc(gr_u, 1)

            def features(q, k, d):
                q, k = ahead(q, k, d)
                b = 4 * q + k
                if not (isinstance(b, int) and b < 2):
                    act.wait_ge(gr_m, 7 * (b - 1))
                act.wait_ge(gr_t, 2 * b + 1)
                S.copy(ftS[k % 2][:, 0:512], psT[0][:, :]).then_inc(gr_c, 1)
                act.wait_ge(gr_t, 2 * b + 2)
                S.copy(ftS[k % 2][:, 512:B * P], psT[1][:, 0:B * P - 512]).then_inc(gr_c, 1)

            def gru_step(q, k, first, last):
                if last < 2:
                    scale_msg(q, k, 1)
                if not first:
                    q1, k1 = ahead(q, k, -1)
                    n = parts(k1)[2]
                    act.wait_ge(gr_n, 2 * (4 * q1 + k1) + 2)
                    S.activation(n, n, ACT.Tanh).then_inc(gr_tanh, 1)
                if last < 2:
                    features(q, k, 1)
                if last < 3:
                    rz = gates[k][:, :, 0:2 * D]
                    act.wait_ge(gr_p, 7 * (4 * q + k) + 14)
                    S.activation(rz, rz, ACT.Sigmoid).then_inc(gr_sig, 1)

            scale_msg(0, 0, 0)
            features(0, 0, 0)
            gru_loop(act, gru_step)


        @block.tensor
        def _(pe):
            T = nc.tensor
            turn = [0]

            def asked():
                turn[0] += 1
                pe.wait_ge(ask, turn[0])

            pe.wait_ge(consts, 6)
            asked()
            T.transpose(psC[0:1, 0:P], tile_d[:, J - 1:J], ident[:, :])
            T.transpose(psC[0:1, P:2 * P], col(C_C), ident[:, :]).then_inc(given, 1)
            asked()
            T.transpose(psC[:, 2 * P:2 * P + 1], row1[0:1, 0:P], ident[0:1, 0:1]).then_inc(given, 1)
            asked()
            T.transpose(psC[0:D + 1, 0:P], cbc[:, :], ident[:, :]).then_inc(given, 1)
            for k in range(14):
                asked()
                for c in range(4):
                    mm = T.transpose(psC[:, c * P:(c + 1) * P], sx[k % 2][:, c * P:(c + 1) * P], ident[:, :])
                mm.then_inc(given, 1)

            pe.wait_ge(ld_w, 16 * 18)
            pe.wait_ge(pads, 5)
            T.transpose(psH[0][:, 0:P], wcat[:, 0, :], ident[:, :])
            T.transpose(psH[0][:, P:H1], wcat[0:H1 - P, 1, :], ident[0:H1 - P, 0:H1 - P])
            T.transpose(psH[1][0:ED, 0:P], wea[:, 0, :], ident[:, :])
            T.transpose(psH[1][0:ED, P:H1], wea[0:H1 - P, 1, :], ident[0:H1 - P, 0:H1 - P])
            T.transpose(psH[2][0:D, 0:P], whh[:, 0, :], ident[:, :])
            T.transpose(psH[2][0:D, P:3 * D], whh[0:D, 1, :], ident[0:D, 0:D])
            T.transpose(psE[0:D, 0:P], wih[:, 0, :], ident[:, :])
            T.transpose(psE[0:D, P:3 * D], wih[0:D, 1, :], ident[0:D, 0:D]).then_inc(w_step, 1)
            pe.wait_ge(w_copied, 5)
            T.matmul(psH[0][:, 0:3 * D], wlin[:, :], whhT[:, :], start=True, stop=True)
            T.matmul(psH[1][:, 0:D], wlin[:, :], ident[0:D, 0:D], start=True, stop=True)
            T.matmul(psH[2][0:1, 0:3 * D], bcol[:, :], whhT[:, :], start=True, stop=True).then_inc(w_step, 1)

            for k in range(3):
                asked()
                T.transpose(psC[0:D, 0:P], R[1][:, (B - 1) * D:B * D], ident[:, :]).then_inc(given, 1)
                asked()
                T.transpose(psC[:, P:P + D], co[0:D, 0:P], ident[0:D, 0:D]).then_inc(given, 1)

            pe.wait_ge(w_copied, 9)
            pe.wait_ge(e_placed, 16 * B)
            with pe.Fori(0, IT) as t:
                for h in range(2):
                    b = 2 * t + h
                    pe.wait_ge(at_g[h], 32 * B * (t + 1))
                    pe.wait_ge(at_c, 3 * b)
                    for i in range(B):
                        mm = T.transpose(psT[i // 4][:, (i % 4) * P:(i % 4 + 1) * P], G[h][:, i * P:(i + 1) * P],
                                         ident[:, :])
                        if i in (3, B - 1):
                            mm.then_inc(at_t, 1)
                    pe.wait_ge(at_ea, b + 1)
                    T.transpose(psE[0:B * ED, 0:P], ea7[h][:, :], ident[:, :]).then_inc(at_t, 1)
                    pe.wait_ge(at_c, 3 * b + 3)
                    for i in range(B):
                        o = psH[i // 3][:, (i % 3) * H1:(i % 3 + 1) * H1]
                        if i % 3 == 0:
                            pe.wait_ge(at_sc, 7 * b + min(i + 3, B))
                        T.matmul(o, ftS[h][:, i * P:(i + 1) * P], rhs1[:, :], start=True, stop=False)
                        T.matmul(o, eaT[h][:, :], rhs_e[:, i * H1:(i + 1) * H1], start=False, stop=False)
                        T.matmul(o, ones[0:1, :], b1row[:, :], start=False, stop=True).then_inc(at_h, 1)
            asked()
            T.transpose(psC[0:1, 0:P], m_all[:, J:J + 1], ident[:, :])
            T.transpose(psC[0:1, P:2 * P], col(C_NBC), ident[:, :]).then_inc(given, 1)
            asked()
            T.transpose(psC[:, 2 * P:2 * P + 1], row1[0:1, 0:P], ident[0:1, 0:1])
            T.transpose(psC[:, 2 * P + 1:2 * P + 2], row1[0:1, 1:P + 1], ident[0:1, 0:1]).then_inc(given, 1)
            asked()
            T.transpose(psC[0:D + 1, 0:P], V[0][:, 0:D + 1], ident[:, :])
            T.transpose(psC[0:D + 1, P:2 * P], cbc[:, :], ident[:, :]).then_inc(given, 1)
            asked()
            T.transpose(psC[:, 2 * P:2 * P + D + 1], co[:, 0:P], ident[0:D + 1, 0:D + 1]).then_inc(given, 1)

            def transposes(q, k, d):
                q, k = ahead(q, k, d)
                b = 4 * q + k
                pe.wait_ge(gr_lc[k], 32 * (q + 1))
                pe.wait_ge(gr_u, 7 * b + 7)
                if not (isinstance(b, int) and b < 1):
                    pe.wait_ge(gr_c, 2 * b)
                for i in range(B):
                    mm = T.transpose(psT[i // 4][:, (i % 4) * P:(i % 4 + 1) * P], cat[k][:, i * P:(i + 1) * P],
                                     ident[:, :])
                    if i in (3, B - 1):
                        mm.then_inc(gr_t, 1)

            def gru_step(q, k, first, last):
                if last < 3:
                    b = 4 * q + k
                    for i in range(B):
                        if i in (0, 4):
                            pe.wait_ge(gr_c, 2 * b + 1 + i // 4)
                        pe.wait_ge(gr_p, 7 * b + (7, 2, 3, 4, 5, 6, 8)[i])
                        T.matmul(banks[i % 6][:, 0:5 * D], ftS[k % 2][:, i * P:(i + 1) * P], rhs_n[:, :],
                                 start=True, stop=True).then_inc(gr_m, 1)
                if last < 2:
                    transposes(q, k, 1)

            transposes(0, 0, 0)
            gru_loop(pe, gru_step)


        @block.vector
        def _(dve):
            v = nc.vector
            steps = [0]
            turn = [0]

            def link(ins):
                steps[0] += 1
                ins.then_inc(dv, 1)
                dve.wait_ge(dv, steps[0])

            def exchange():
                turn[0] += 1
                dve.sem_inc(ask, 1)
                dve.wait_ge(given, turn[0])

            ta, tb, tc, td = tile_a[:, 0:J], tile_b[:, 0:J], tile_c[:, 0:J], tile_d[:, 0:J]

            v.memset(key_d[:, :], PAD_KEY).then_inc(pads, 1)
            v.memset(ew[:, :], 0.0).then_inc(pads, 1)
            v.memset(src_i[:, :], 0).then_inc(pads, 1)
            v.memset(kx[:, :], PAD_KEY).then_inc(pads, 1)
            pl = place_v[:, :].rearrange("p (j w) -> p j w", w=2)
            link(v.memset(pl[:, :, 1:2], 0.0))
            v.memset(pl[:, :, 0:1], float(ROW_ZERO)).then_inc(place_pads, 1)
            v.memset(zrow[:, :], 0.0).then_inc(zset, 1)
            v.memset(wlin[:, :], 0.0).then_inc(zset, 1)
            link(v.memset(rhs_n[:, :], 0.0))
            v.memset(rhs_e[:, :], 0.0).then_inc(rhs_zero, 1)
            for lst in (row_i, srcs_i, dsts_i, perm_i, scat_i):
                link(v.memset(lst[:, J:J + 2 * B], 0))
            link(v.memset(row1[:, 0:1], 0.0))
            link(v.memset(co[:, 0:1], 0.0))
            dve.sem_inc(pads, 1)

            def runs(key, end):
                link(v.tensor_tensor(ta, key[:, 1:J + 1], key[:, 0:J], ALU.not_equal))
                link(v.tensor_tensor(tb, key[:, 1:J + 1], key[:, 2:J + 2], ALU.not_equal))
                link(v.tensor_copy(tc[:, 1:J], ta[:, 1:J]))
                link(v.memset(tc[:, 0:1], 0.0))
                link(v.tensor_tensor_scan(td, tc, tc, 0.0, ALU.max, ALU.max))
                link(v.tensor_scalar(tc, td, -1.0, 1.0, ALU.mult, ALU.add))
                link(v.tensor_tensor(end, tc, tb, ALU.mult))

            dve.wait_ge(ld_dst, 80)
            dve.wait_ge(consts, 6)
            runs(key_d, end_d[:, :])
            link(v.tensor_scalar(keep_d[:, :], ta, -1.0, 1.0, ALU.mult, ALU.add))
            link(v.tensor_tensor(col(C_C), tc[:, J - 1:J], keep_d[:, 0:1], ALU.mult))
            link(v.tensor_scalar(td, tb, -OOB, OOB, ALU.mult, ALU.add))
            link(v.tensor_tensor(place_i[:, 0:J], td, key_d[:, 1:J + 1], ALU.add))
            dve.wait_ge(place_set, 16)
            link(v.tensor_scalar(td, pos[:, :], fixrow[:, 0:1], None, ALU.subtract))
            link(v.tensor_tensor(td, td, end_d[:, :], ALU.mult))
            link(v.tensor_tensor(pl[:, :, 0], pos[:, :], td, ALU.subtract))
            dve.wait_ge(ld_ew, 48)
            link(v.tensor_tensor_scan(td, keep_d[:, :], ew[:, :], 0.0, ALU.mult, ALU.add))
            exchange()
            link(v.tensor_copy(row2[0:1, 0:P], psC[0:1, P:2 * P]))
            link(v.tensor_tensor_scan(row1[:, 1:P + 1], row2[0:1, 0:P], psC[0:1, 0:P], 0.0, ALU.mult, ALU.add))
            exchange()
            link(v.tensor_tensor(col(C_IN), psC[:, 2 * P:2 * P + 1], keep_d[:, 0:1], ALU.mult))
            link(v.scalar_tensor_tensor(out=pl[:, :, 1], in0=tc, scalar=col(C_IN), in1=td, op0=ALU.mult, op1=ALU.add))
            dve.sem_inc(place_ready, 1)
            link(v.tensor_scalar(tb, pl[:, :, 1], TINY, None, ALU.max))
            dve.sem_inc(sq_ask, 1)
            link(v.tensor_scalar(cbc[:, :], ones[:, 0:D + 1], col(C_C), None, ALU.mult))
            exchange()
            link(v.tensor_copy(cT[:, :], psC[0:D + 1, 0:P]))
            dve.wait_ge(sq_given, 1)
            link(v.reciprocal(ta, td))
            link(v.scalar_tensor_tensor(out=dinv[:, :], in0=pl[:, :, 1], scalar=0.0, in1=ta, op0=ALU.is_gt, op1=ALU.mult))
            link(v.scalar_tensor_tensor(out=ta, in0=end_d[:, :], scalar=1.0, in1=dinv[:, :], op0=ALU.mult, op1=ALU.mult,
                                        accum_out=col(C_DEND)))

            er = edge_s[:, :].rearrange("p (j w) -> p j w", w=ED + 1)
            dve.wait_ge(ld_ea, 48)
            dve.wait_ge(pool_pads, 2)
            link(v.tensor_copy(er[:, :, ED], key_d[:, 1:J + 1]))
            dve.sem_inc(edge_ready, 1)

            cur = [0]
            lin, u0, u1 = lin_i[:, :], sx[0][:, :].bitcast(U32), sx[1][:, :].bitcast(U32)
            dve.wait_ge(ld_key, 48)
            link(v.tensor_scalar(sx[1][:, :].bitcast(I32), kx[:, :], 32512.0, 256.0, ALU.is_ge, ALU.mult))
            link(v.scalar_tensor_tensor(out=sx[0][:, :].bitcast(I32), in0=kx[:, :], scalar=128.0,
                                        in1=sx[1][:, :].bitcast(I32), op0=ALU.add, op1=ALU.add))
            link(v.tensor_scalar(u1, u0, 16, None, ALU.logical_shift_left))
            link(v.tensor_tensor(u0, u1, lin, ALU.bitwise_or))
            link(v.tensor_scalar(mask[:, :], lin, 1, None, ALU.logical_shift_right))
            link(v.tensor_tensor(gray[:, :], lin, mask[:, :], ALU.bitwise_xor))

            def flip(k):
                s, d = (sx[cur[0]][:, :].bitcast(U32), sx[1 - cur[0]][:, :].bitcast(U32))
                link(v.tensor_scalar(mask[:, :], (gray if k else lin_i)[:, :], 31 - max(k, 1), 0x80000000,
                                     ALU.logical_shift_left, ALU.bitwise_and))
                link(v.tensor_tensor(d, s, mask[:, :], ALU.bitwise_xor))
                cur[0] ^= 1

            def compare(bit):
                a = sx[cur[0]][:, :].rearrange("p (a t s) -> p a t s", t=2, s=1 << bit)
                o = sx[1 - cur[0]][:, :].rearrange("p (a t s) -> p a t s", t=2, s=1 << bit)
                steps[0] += 2
                v.tensor_tensor(o[:, :, 0, :], a[:, :, 0, :], a[:, :, 1, :], ALU.min).then_inc(dv, 1)
                v.tensor_tensor(o[:, :, 1, :], a[:, :, 0, :], a[:, :, 1, :], ALU.max).then_inc(dv, 1)
                dve.wait_ge(dv, steps[0])
                cur[0] ^= 1

            swaps = [0]

            def swap():
                k = swaps[0] % 2
                if cur[0] != k:
                    link(v.tensor_copy(sx[k][:, :], sx[1 - k][:, :]))
                    cur[0] = k
                exchange()
                link(v.tensor_copy(sx[1 - k][:, :], psC[:, :]))
                cur[0] ^= 1
                swaps[0] += 1

            flip(0)
            for k in range(1, 17):
                low = k - 1
                if k >= 10:
                    swap()
                    for bit in range(k - 1, 6, -1):
                        compare(bit - 9 if bit >= 9 else bit)
                    swap()
                    low = 6
                for bit in range(low, -1, -1):
                    compare(bit)
                if k < 16:
                    flip(k)
            if cur[0]:
                link(v.tensor_copy(sx[0][:, :], sx[1][:, :]))
            link(v.memset(key_s[:, :], 0))
            dve.sem_inc(sort_done, 1)
            dve.wait_ge(ld_sorted, 64)
            packed = key_s[:, :].bitcast(U32)
            hi, lo = tile_a[:, :].bitcast(U32), tile_b[:, :].bitcast(U32)
            link(v.tensor_scalar(hi, packed, 16, None, ALU.logical_shift_right))
            link(v.tensor_scalar(lo, packed, 0xFFFF, None, ALU.bitwise_and))
            link(v.tensor_scalar(perm_i[:, 0:J], lo[:, 1:J + 1], float(E), None, ALU.min))
            link(v.tensor_scalar(tile_c[:, :], hi, 32768.0, -256.0, ALU.is_ge, ALU.mult))
            link(v.scalar_tensor_tensor(out=key_s[:, :], in0=hi, scalar=-128.0, in1=tile_c[:, :], op0=ALU.add, op1=ALU.add))
            link(v.tensor_scalar(srcs_i[:, 0:J], key_s[:, 1:J + 1], float(NP - 1), None, ALU.min))
            runs(key_s, end_s[:, :])
            link(v.tensor_scalar(start_s[:, :], ta, -BIG, None, ALU.mult))
            link(v.tensor_scalar(col(C_G0S), ta[:, 0:1], -1.0, 1.0, ALU.mult, ALU.add))
            link(v.tensor_tensor(col(C_CS), tc[:, J - 1:J], col(C_G0S), ALU.mult))
            link(v.tensor_scalar(col(C_NBC), col(C_CS), BIG, -BIG, ALU.mult, ALU.add))
            link(v.tensor_scalar(col(C_NBG), col(C_G0S), BIG, -BIG, ALU.mult, ALU.add))
            link(v.tensor_tensor(tb, tb, end_s[:, :], ALU.subtract))
            link(v.tensor_scalar(td, tb, -OOB, OOB, ALU.mult, ALU.add))
            link(v.tensor_tensor(scat_i[:, 0:J], td, key_s[:, 1:J + 1], ALU.add))
            link(v.scalar_tensor_tensor(out=ta, in0=end_s[:, :], scalar=1.0, in1=key_s[:, 1:J + 1], op0=ALU.mult,
                                        op1=ALU.mult, accum_out=col(C_X0)))
            link(v.scalar_tensor_tensor(out=ta, in0=end_s[:, :], scalar=1.0, in1=end_s[:, :], op0=ALU.mult,
                                        op1=ALU.mult, accum_out=col(C_X1)))
            link(v.tensor_scalar(col(C_X1), col(C_X1), -OOB, OOB, ALU.mult, ALU.add))
            link(v.tensor_tensor(fix_i[:, :], col(C_X0), col(C_X1), ALU.add))

            dve.wait_ge(ld_x, 48)
            with dve.Fori(0, NB) as b:
                for i in range(B):
                    c = b * B + i
                    v.bn_stats(stats[:, bass.ds(c * 6, 6)], big[:, bass.ds(c * D, D)]).then_inc(bn, 1)
            dve.wait_ge(bn, J)

            def norm(s6, s, d, q, var, between):
                between(v.tensor_tensor(s, s6[:, :, 1], s6[:, :, 4], ALU.add))
                between(v.tensor_tensor(d, s6[:, :, 1], s6[:, :, 4], ALU.subtract))
                between(v.tensor_tensor(q, s6[:, :, 2], s6[:, :, 5], ALU.add))
                between(v.tensor_tensor(d, d, d, ALU.mult))
                between(v.tensor_scalar(q, q, 1.0 / D, EPS, ALU.mult, ALU.add))
                between(v.scalar_tensor_tensor(out=var, in0=d, scalar=0.25, in1=q, op0=ALU.mult, op1=ALU.add))

            norm(stats.rearrange("p (j w) -> p j w", w=6), ta, tb, tc, tb, link)
            dve.sem_inc(sq_ask, 1)
            dve.wait_ge(sq_given, 2)
            link(v.reciprocal(rstd[:, :], td))
            link(v.scalar_tensor_tensor(out=shift[:, 0:J], in0=ta, scalar=-0.5, in1=rstd[:, :], op0=ALU.mult, op1=ALU.mult))

            dve.wait_ge(w_copied, 9)
            for i in range(B):
                pass
            link(v.tensor_tensor(nrow[0:1, 0:3 * D], brow[0:1, 0:3 * D], brow[0:1, 0:3 * D], ALU.max))
            link(v.tensor_tensor(hrow[0:1, :], hrow[0:1, :], brow[0:1, 3 * D:6 * D], ALU.add))
            link(v.tensor_tensor(nrow[0:1, 0:2 * D], nrow[0:1, 0:2 * D], hrow[0:1, 0:2 * D], ALU.add))
            link(v.tensor_copy(nrow[0:1, 3 * D:4 * D], hrow[0:1, 2 * D:3 * D]))
            link(v.tensor_copy(nrow[0:1, 4 * D:5 * D], brow[0:1, 6 * D:7 * D]))
            dve.sem_inc(w_bias, 1)

            dve.wait_ge(ld_node, 16)
            dve.wait_ge(w_done, 3)
            dve.sem_inc(node_ready, 1)

            def node_row(t, h):
                b = 2 * t + h
                rows_h = O[h][:, :].rearrange("p (i w) -> p i w", w=D + 2)
                dve.wait_ge(tw_s[h], 32 * t)
                v.tensor_copy(rows_h[:, :, D:D + 2], at(node_v, b, 2).rearrange("p (i w) -> p i w", w=2)).then_inc(tw_p, 1)
                dve.wait_ge(tw_h, 7 * b + 7)
                v.scalar_tensor_tensor(out=O2[h][:, :].rearrange("p (i w) -> p i w", w=D), in0=rows_h[:, :, 0:D],
                                       scalar=0.25, in1=at(big, b, D).rearrange("p (i w) -> p i w", w=D),
                                       op0=ALU.mult, op1=ALU.add).then_inc(tw_x, 1)

            def edge_row(b, h, more):
                dve.wait_ge(ed_g[h], 8 * B * (b + 2 - h))
                v.tensor_copy(at(edge_s, b, ED + 1), G[h][:, 0:B * (ED + 1)]).then_inc(ed_c, 1)
                if more:
                    dve.wait_ge(ed_c, b + 1)
                    v.tensor_copy(st[h][:, 0:B], at(perm_i, b + 2)).then_inc(ed_staged, 1)

            n0 = ED_PARTS[0][1]
            for h in range(2):
                v.tensor_copy(st[h][:, 0:B], perm_i[:, h * B:(h + 1) * B]).then_inc(ed_staged, 1)
            with dve.Fori(0, n0 - 1) as t:
                for e in range(2):
                    for h in range(2):
                        node_row(2 * t + e, h)
                    edge_row(2 * t + e, e, True)
            for e in range(2):
                for h in range(2):
                    node_row(2 * n0 - 2 + e, h)
                edge_row(2 * n0 - 2 + e, e, False)

            for k in range(3):
                s = SW[k]
                w = D + 2 if k == 0 else D
                if k == 1:
                    dve.wait_ge(zeroed, 16 * (NB + 3))
                if k:
                    dve.wait_ge(SW[k - 1].x, 14 + J)
                else:
                    dve.wait_ge(tw_x, NB)
                v.memset(R[1][:, (B - 1) * D:B * D], 0.0).then_inc(s.r, 1)
                v.memset(F[:, :], 0.0).then_inc(s.f, 1)
                with dve.Fori(0, IT) as t:
                    for h in range(2):
                        b = 2 * t + h
                        dve.wait_ge(s.g[h], 16 * B * (t + 1))
                        if k == 0:
                            gv = G[h][:, 0:B * w].rearrange("p (i w) -> p i w", w=w)
                            v.tensor_scalar(q7[h][0][:, :], gv[:, :, D + 1], TINY, None, ALU.max).then_inc(sw_small, 1)
                            v.tensor_copy(at(row_i, b), gv[:, :, D]).then_inc(sw_small, 1)
                            v.scalar_tensor_tensor(out=q7[h][2][:, :], in0=gv[:, :, D + 1], scalar=0.0, in1=at(ew, b),
                                                   op0=ALU.is_gt, op1=ALU.mult).then_inc(sw_small, 1)
                            dve.wait_ge(sw_sq, b + 1)
                            v.reciprocal(q7[h][3][:, :], q7[h][1][:, :]).then_inc(sw_small, 1)
                            dve.wait_ge(sw_small, 4 * b + 4)
                            v.tensor_tensor(at(w_e, b), q7[h][2][:, :], q7[h][3][:, :], ALU.mult).then_inc(sw_w, 1)
                        else:
                            wb = at(w_e, b).unsqueeze(2).to_broadcast([P, B, D])
                            vv = V[h][:, 0:B * D].rearrange("p (i w) -> p i w", w=D)
                            v.tensor_tensor(vv, G[h][:, 0:B * D].rearrange("p (i w) -> p i w", w=D), wb,
                                            ALU.mult).then_inc(sw_small, 1)
                            dve.wait_ge(sw_small, 4 * NB + (k - 1) * NB + b + 1)
                            v.tensor_tensor(V[h][:, 0:B * D], V[h][:, 0:B * D], at(big, b, D), ALU.add).then_inc(s.v, B)
                        dve.wait_ge(s.x, 14 * t + 7 * h + 7)

                        def finish(i):
                            c = b * B + i
                            dve.wait_ge(s.r, c + 2)
                            dve.wait_ge(s.f, c + 1)
                            v.scalar_tensor_tensor(out=F[:, 0:D], in0=R[h][:, i * D:(i + 1) * D],
                                                   scalar=end_d[:, bass.ds(c, 1)], in1=F[:, 0:D], op0=ALU.mult,
                                                   op1=ALU.add).then_inc(s.f, 1)

                        for i in range(B):
                            c = b * B + i
                            prev = R[h][:, (i - 1) * D:i * D] if i else R[1 - h][:, (B - 1) * D:B * D]
                            new = V[h][:, i * D:(i + 1) * D] if k else big[:, bass.ds(c * D, D)]
                            dve.wait_ge(s.v, c + 1 if k == 0 else 7 * b + 7)
                            dve.wait_ge(s.r, c + 1)
                            v.scalar_tensor_tensor(out=R[h][:, i * D:(i + 1) * D], in0=prev,
                                                   scalar=keep_d[:, bass.ds(c, 1)], in1=new, op0=ALU.mult,
                                                   op1=ALU.add).then_inc(s.r, 1)
                            if i:
                                finish(i - 1)
                        finish(B - 1)
                dve.wait_ge(s.r, J + 1)
                dve.wait_ge(s.f, J + 1)
                exchange()
                link(v.tensor_tensor_scan(co[0:D, 1:P + 1], cT[0:D, :], psC[0:D, 0:P], 0.0, ALU.mult, ALU.add))
                exchange()
                if k:
                    dve.wait_ge(fix_stored[k - 1], 16)
                link(v.scalar_tensor_tensor(out=fixr[:, 0:D], in0=psC[:, P:P + D], scalar=keep_d[:, 0:1], in1=F[:, 0:D],
                                            op0=ALU.mult, op1=ALU.add))
                link(v.tensor_scalar(fixr[:, 0:D], fixr[:, 0:D], col(C_DEND), None, ALU.mult))
                dve.sem_inc(fix_ready[k], 1)

            dve.wait_ge(SW[2].x, 14 + J)
            nv = node_v[:, :].rearrange("p (j w) -> p j w", w=2)
            link(v.tensor_copy(node_i[:, 0:J], nv[:, :, 0]))
            dve.sem_inc(nodes_listed, 1)
            dve.sem_inc(nu_h, 14)
            with dve.Fori(0, IT) as t:
                for h in range(2):
                    b = 2 * t + h
                    dve.wait_ge(nu_g[h], 16 * B * (t + 1))
                    dve.wait_ge(nu_l[h], 16 * (t + 1))
                    dve.wait_ge(nu_s[h], 32 * t)
                    dve.wait_ge(nu_h, 14 * t + 7 * h + 7)
                    count = [0]

                    def step(ins):
                        count[0] += 1
                        ins.then_inc(nu_d, 1)
                        dve.wait_ge(nu_d, 16 * b + count[0])

                    step(v.scalar_tensor_tensor(out=V[h][:, 0:B * D], in0=G[h][:, 0:B * D], scalar=0.25,
                                                in1=O2[h][:, :], op0=ALU.mult, op1=ALU.add))
                    for i in range(B):
                        v.bn_stats(st6[h][:, i * 6:(i + 1) * 6], V[h][:, i * D:(i + 1) * D]).then_inc(nu_d, 1)
                    count[0] += B
                    dve.wait_ge(nu_d, 16 * b + count[0])
                    q = q7[h]
                    norm(st6[h][:, :].rearrange("p (i w) -> p i w", w=6), q[2][:, :], q[3][:, :], q[0][:, :], q[4][:, :], step)
                    dve.wait_ge(nu_q, b + 1)
                    step(v.reciprocal(q[0][:, :], q[5][:, :]))
                    step(v.scalar_tensor_tensor(out=q[1][:, :], in0=q[2][:, :], scalar=-0.5, in1=q[0][:, :],
                                                op0=ALU.mult, op1=ALU.mult))

            dve.wait_ge(ed_c, NB)
            dve.wait_ge(nu_h, 14 + J)
            for h in range(2):
                dve.wait_ge(nu_s[h], 32 * IT)
            link(v.memset(F[:, :], 0.0))
            link(v.memset(m_all[:, 0:1], -BIG))
            v.memset(R[1][:, (B - 1) * (D + 1):B * (D + 1)], 0.0).then_inc(at_r, 1)
            v.tensor_scalar(dsts_i[:, 0:J], er[:, :, ED], float(NP - 1), None, ALU.min).then_inc(at_d, 1)
            dve.sem_inc(at_sc, 7)
            dve.wait_ge(w_done, 2)
            dve.wait_ge(pads, 5)
            with dve.Fori(0, IT) as t:
                for h in range(2):
                    b = 2 * t + h
                    w = D + 1
                    for i in range(B):
                        if i % 3 == 0:
                            dve.wait_ge(at_h, 7 * b + min(i + 3, B))
                        v.scalar_tensor_tensor(out=hh[h][i], in0=psH[i // 3][:, (i % 3) * H1:(i % 3 + 1) * H1],
                                               scalar=0.0, in1=w2bc[:, :], op0=ALU.max, op1=ALU.mult,
                                               accum_out=score[h][:, i:i + 1]).then_inc(at_sc, 1)
                    dve.wait_ge(at_sc, 7 * b + 14)
                    count = [1]

                    def step(ins):
                        count[0] += 1
                        ins.then_inc(at_d, 1)
                        dve.wait_ge(at_d, 7 * b + count[0])

                    sc, mp = q7[h][0][:, :], q7[h][1][:, :]
                    m_new, m_old = m_all[:, bass.ds(b * B + 1, B)], at(m_all, b)
                    step(v.tensor_scalar(sc, score[h][:, :], b2c[:, 0:1], None, ALU.add))
                    step(v.tensor_tensor_scan(m_new, at(start_s, b), sc, m_all[:, bass.ds(b * B, 1)], ALU.add, ALU.max))
                    step(v.tensor_tensor(mp, at(start_s, b), m_old, ALU.add))
                    step(v.tensor_tensor(q14[h][:, 0:B], mp, m_new, ALU.subtract))
                    step(v.tensor_tensor(q14[h][:, B:2 * B], sc, m_new, ALU.subtract))
                    step(v.tensor_scalar(q14[h][:, :], q14[h][:, :], EXP_MIN, None, ALU.max))
                    dve.wait_ge(at_e, b + 1)
                    vv = V[h][:, :].rearrange("p (i w) -> p i w", w=w)
                    step(v.tensor_copy(vv[:, :, D], e14[h][:, B:2 * B]))
                    dve.wait_ge(at_s[h], 16 * B * t)

                    def finish(i):
                        c = b * B + i
                        dve.wait_ge(at_r, c + 2)
                        dve.wait_ge(at_f, c)
                        v.scalar_tensor_tensor(out=F[:, :], in0=R[h][:, i * w:(i + 1) * w],
                                               scalar=end_s[:, bass.ds(c, 1)], in1=F[:, :], op0=ALU.mult,
                                               op1=ALU.add).then_inc(at_f, 1)

                    for i in range(B):
                        c = b * B + i
                        prev = R[h][:, (i - 1) * w:i * w] if i else R[1 - h][:, (B - 1) * w:B * w]
                        dve.wait_ge(at_v, c + 1)
                        dve.wait_ge(at_r, c + 1)
                        v.scalar_tensor_tensor(out=R[h][:, i * w:(i + 1) * w], in0=prev, scalar=e14[h][:, i:i + 1],
                                               in1=V[h][:, i * w:(i + 1) * w], op0=ALU.mult,
                                               op1=ALU.add).then_inc(at_r, 1)
                        if i:
                            finish(i - 1)
                    finish(B - 1)
            dve.wait_ge(at_r, J + 1)
            dve.wait_ge(at_f, J)
            link(v.memset(row1[:, 0:1], -BIG))
            exchange()
            link(v.tensor_copy(row2[0:1, 0:P], psC[0:1, P:2 * P]))
            link(v.tensor_tensor_scan(row1[:, 1:P + 1], row2[0:1, 0:P], psC[0:1, 0:P], -BIG, ALU.add, ALU.max))
            exchange()
            link(v.tensor_copy(cols[:, C_MCI:C_MCI + 2], psC[:, 2 * P:2 * P + 2]))
            link(v.scalar_tensor_tensor(out=ta, in0=end_s[:, :], scalar=1.0, in1=m_all[:, 1:J + 1], op0=ALU.mult,
                                        op1=ALU.mult, accum_out=col(C_ME)))
            link(v.tensor_tensor(col(C_X0), col(C_MCI), col(C_NBG), ALU.add))
            link(v.tensor_tensor(col(C_X1), col(C_ME), col(C_X0), ALU.max))
            link(v.tensor_tensor(col(C_T0), col(C_MCI), col(C_MCO), ALU.subtract))
            link(v.tensor_tensor(col(C_T1), m_all[:, J:J + 1], col(C_MCO), ALU.subtract))
            link(v.tensor_tensor(col(C_T2), col(C_X0), col(C_X1), ALU.subtract))
            link(v.tensor_tensor(col(C_T3), col(C_ME), col(C_X1), ALU.subtract))
            link(v.tensor_scalar(cols[:, C_T0:C_T0 + 4], cols[:, C_T0:C_T0 + 4], EXP_MIN, 0.0, ALU.max, ALU.min))
            dve.sem_inc(sq_ask, 1)
            dve.wait_ge(sq_given, 3)
            link(v.tensor_tensor(col(C_X0), col(C_CS), col(C_E0), ALU.mult))
            link(v.tensor_scalar(cbc[:, :], ones[:, 0:D + 1], col(C_X0), None, ALU.mult))
            link(v.tensor_scalar(V[0][:, 0:D + 1], R[1][:, (B - 1) * (D + 1):B * (D + 1)], col(C_E0 + 1), None, ALU.mult))
            exchange()
            link(v.tensor_copy(cT[:, :], psC[0:D + 1, P:2 * P]))
            link(v.tensor_tensor_scan(co[:, 1:P + 1], cT[:, :], psC[0:D + 1, 0:P], 0.0, ALU.mult, ALU.add))
            exchange()
            dve.wait_ge(fix_stored[2], 16)
            link(v.tensor_scalar(F[:, :], F[:, :], col(C_E0 + 3), None, ALU.mult))
            v.scalar_tensor_tensor(out=fixr[:, :], in0=psC[:, 2 * P:2 * P + D + 1], scalar=col(C_E0 + 2), in1=F[:, :],
                                   op0=ALU.mult, op1=ALU.add).then_inc(fix_ready[3], 2)

            dve.wait_ge(w_done, 3)
            dve.sem_inc(gr_p, 7)

            def den_step(q, k, d):
                q, k = ahead(q, k, d)
                b = 4 * q + k
                dve.wait_ge(gr_lv[k], 16 * (q + 1))
                den = msg_g[k].rearrange("p (i w) -> p i w", w=D + 1)[:, :, D]
                if not (isinstance(b, int) and b < 4):
                    dve.wait_ge(gr_u, 7 * (b - 3))
                v.tensor_scalar(recip[k], den, 0.5, None, ALU.max).then_inc(gr_den, 1)
                v.tensor_scalar(flag[k], den, 0.0, None, ALU.is_gt).then_inc(gr_den, 1)
                dve.wait_ge(gr_den, 3 * b + 2)
                v.reciprocal(recip[k], recip[k]).then_inc(gr_den, 1)

            def evacuate(q, k):
                b = 4 * q + k
                if not (isinstance(b, int) and b < 4):
                    dve.wait_ge(gr_o, b - 3)
                for i in range(B):
                    dve.wait_ge(gr_m, 7 * b + i + 1)
                    v.tensor_tensor(gates[k][:, i, :], banks[i % 6][:, 0:5 * D], bias_n[:, :], ALU.add).then_inc(gr_p, 1)

            def reset_gate(q, k, d):
                q, k = ahead(q, k, d)
                b = 4 * q + k
                r, z, n, hn, m = parts(k)
                dve.wait_ge(gr_sig, b + 1)
                v.tensor_tensor(hn, hn, r, ALU.mult).then_inc(gr_n, 1)
                dve.wait_ge(gr_n, 2 * b + 1)
                v.tensor_tensor(n, n, hn, ALU.add).then_inc(gr_n, 1)

            def mix(q, k, d):
                q, k = ahead(q, k, d)
                b = 4 * q + k
                r, z, n, hn, m = parts(k)
                dve.wait_ge(gr_tanh, b + 1)
                v.tensor_tensor(m, m, n, ALU.subtract).then_inc(gr_mix, 1)
                dve.wait_ge(gr_mix, 4 * b + 1)
                v.tensor_tensor(m, m, z, ALU.mult).then_inc(gr_mix, 1)
                dve.wait_ge(gr_mix, 4 * b + 2)
                dve.wait_ge(gr_nh, b + 1)
                v.tensor_tensor(m, m, hn, ALU.add).then_inc(gr_mix, 1)
                dve.wait_ge(gr_mix, 4 * b + 3)
                v.tensor_tensor(m, m, flag[k].unsqueeze(2).to_broadcast([P, B, D]), ALU.mult).then_inc(gr_mix, 1)

            def gru_step(q, k, first, last):
                if not first:
                    reset_gate(q, k, -1)
                if last < 3:
                    evacuate(q, k)
                if last < 1:
                    den_step(q, k, 2)
                if not first:
                    mix(q, k, -1)

            den_step(0, 0, 0)
            den_step(0, 0, 1)
            gru_loop(dve, gru_step)


_INS = ["x", "src", "dst", "edge_attr_16", "edge_weight", "L1_gnn_W_att1", "L1_gnn_b_att1", "L1_gnn_W_att2",
        "L1_gnn_b_att2", "L1_gnn_W_lin", "L1_gnn_b_lin", "L1_gnn_W_ih", "L1_gnn_b_ih", "L1_gnn_W_hh", "L1_gnn_b_hh"]


def kernel(**inputs):
    import numpy as _np
    import concourse.bacc as _bacc
    from concourse import mybir as _mybir
    from concourse.bass_utils import run_bass_kernel_spmd as _run

    nc = _bacc.Bacc("TRN2", target_bir_lowering=False, num_devices=1)
    arrays, args = {}, []
    for name in _INS:
        a = _np.ascontiguousarray(inputs[name])
        arrays[f"in_{name}_dram"] = a
        args.append(nc.dram_tensor(f"in_{name}_dram", a.shape, _mybir.dt.from_np(a.dtype), kind="ExternalInput").ap())
    out = nc.dram_tensor("out_0_dram", (N, D), F32, kind="ExternalOutput").ap()
    build(nc, *args, out)
    r = _run(nc, [arrays], core_ids=[0])
    return r.results[0]["out_0_dram"]
```

```python
from contextlib import ExitStack

import concourse.bass as bass
from concourse import mybir

F32 = mybir.dt.float32
BF16 = mybir.dt.bfloat16
I32 = mybir.dt.int32
U32 = mybir.dt.uint32
ALU = mybir.AluOpType
ACT = mybir.ActivationFunctionType

P = 128
N = 50000
E = 50000
D = 64
ED = 16
H1 = 2 * D + ED
J = 392
MID = J // 2
NP = P * J
B = 7
NB = J // B
LN_ACT = 4
IT = NB // 2
FULL = N // J
REST = N - FULL * J
ROW_FIX = NP
ROW_ZERO = NP + P
ROWS = NP + 2 * P
PAD_KEY = 60000
OOB = 1000000.0
BIG = 1.0e30
TINY = 2.0 ** -116
EXP_MIN = -200.0
EPS = 1e-5
SORT = P * 512
SORT0 = SORT - NP


def build(nc, x, src, dst, edge_attr, edge_weight, W_att1, b_att1, W_att2, b_att2, W_lin, b_lin,
          W_ih, b_ih, W_hh, b_hh, out):
    with ExitStack() as ctx:
        def sb(name, shape, dt=F32):
            return ctx.enter_context(nc.sbuf_tensor(name, shape, dt))

        def sem(name):
            return ctx.enter_context(nc.semaphore(name))

        def dram(name, shape, dt=F32):
            return nc.dram_tensor(name, shape, dt, kind="Internal").ap()

        t_h = dram("t_h", [NP, D + 2])
        t_xa = dram("t_xa", [NP, D])
        t_u = [dram(f"t_u{k}", [ROWS, D]) for k in range(3)]
        t_sorted = dram("t_sorted", [SORT, 1], I32)
        t_edge = dram("t_edge", [NP, ED + 1])
        t_xh = dram("t_xh", [NP, P])
        t_h2 = dram("t_h2", [NP, D])
        t_last = dram("t_last", [1, J * D])

        def rows(t):
            return t[0:NP, :].rearrange("(p j) f -> p (j f)", j=J)

        big = sb("big", [P, J * D])
        edge_s = sb("edge_s", [P, J * (ED + 1)])
        key_d = sb("key_d", [P, J + 2], I32)
        src_i = sb("src_i", [P, J + 2 * B], I32)
        ew = sb("ew", [P, J])
        keep_d = sb("keep_d", [P, J])
        end_d = sb("end_d", [P, J])
        dinv = sb("dinv", [P, J])
        w_e = sb("w_e", [P, J])
        row_i = sb("row_i", [P, J + 2 * B], I32)
        place_v = sb("place_v", [P, J * 2])
        node_i = src_i
        start_s = sb("start_s", [P, J])
        end_s = sb("end_s", [P, J])
        srcs_i = sb("srcs_i", [P, J + 2 * B], I32)
        dsts_i = sb("dsts_i", [P, J + 2 * B], I32)
        p_e = dsts_i[:, 0:J].bitcast(F32)
        j_e = row_i[:, 0:J].bitcast(F32)
        perm_i = sb("perm_i", [P, J + 2 * B], I32)
        scat_i = sb("scat_i", [P, J + 2 * B], I32)
        key_s = scat_i[:, 0:J + 2]
        m_all = sb("m_all", [P, 1 + J])
        tile_a = sb("tile_a", [P, J + 2])
        tile_b = sb("tile_b", [P, J + 2])
        tile_c = sb("tile_c", [P, J + 2])
        tile_d = sb("tile_d", [P, J + 2])
        rstd, shift = w_e, m_all
        work = sb("work", [P, 6 * 512])
        sx = [work[:, k * 512:(k + 1) * 512] for k in range(2)]
        kx = work[:, 1024:1536].bitcast(I32)
        mask = work[:, 1536:2048].bitcast(U32)
        gray = work[:, 2048:2560].bitcast(U32)
        lin_i = work[:, 2560:3072].bitcast(U32)
        stats = work[:, 0:6 * J]
        ident = sb("ident", [P, P])
        ones = sb("ones", [P, P])
        cols = sb("cols", [P, 40])
        iota_b = tile_d[:, :].bitcast(BF16)[:, 0:J]
        fix_i = sb("fix_i", [P, 1], I32)
        fix_idx = sb("fix_idx", [P, 1], I32)
        st = [sb(f"st{h}", [P, 2 * B], I32) for h in range(2)]
        sst = [sb(f"sst{h}", [P, B], I32) for h in range(2)]
        ea7 = [work[:, 1792 + h * B * ED:1792 + (h + 1) * B * ED] for h in range(2)]
        eaT = [work[0:B * ED, 2016 + h * P:2016 + (h + 1) * P] for h in range(2)]
        ftS = [work[:, h * B * P:(h + 1) * B * P] for h in range(2)]
        q14 = [sb(f"q14_{h}", [P, 2 * B]) for h in range(2)]
        e14 = [sb(f"e14_{h}", [P, 2 * B]) for h in range(2)]
        score = [sb(f"score{h}", [P, B]) for h in range(2)]
        G = [sb(f"G{h}", [P, B * 128]) for h in range(2)]
        V = [sb(f"V{h}", [P, B * (D + 1)]) for h in range(2)]
        zrow = V[1][:, :]
        R = [sb(f"R{h}", [P, B * (D + 1)]) for h in range(2)]
        O = [sb(f"O{h}", [P, B * (D + 2)]) for h in range(2)]
        O2 = [sb(f"O2{h}", [P, B * D]) for h in range(2)]
        F = sb("F", [P, D + 1])
        q7 = [[sb(f"q7_{h}_{k}", [P, B]) for k in range(6)] for h in range(2)]
        st6 = [sb(f"st6_{h}", [P, B * 6]) for h in range(2)]
        row1 = sb("row1", [1, 3 * (P + 1)])
        row2 = sb("row2", [1, 2 * P])
        cT = sb("cT", [D + 1, P])
        co = sb("co", [D + 1, P + 1])
        fixr = sb("fixr", [P, D + 1])
        cbc = sb("cbc", [P, D + 1])
        wcat = G[1][:, 0:256].rearrange("p (k w) -> p k w", k=2)
        wea = G[1][:, 256:288].rearrange("p (k w) -> p k w", k=2)
        wih = G[1][:, 288:416].rearrange("p (k w) -> p k w", k=2)
        whh = G[1][:, 416:544].rearrange("p (k w) -> p k w", k=2)
        wlin = G[1][0:D, 544:672]
        whhT = G[1][0:D, 672:864]
        bcol = sb("bcol", [D, 1])
        rhs1 = sb("rhs1", [P, H1])
        rhs_e = sb("rhs_e", [B * ED, B * H1])
        w1e = sb("w1e", [ED, H1])
        b1row = sb("b1row", [1, H1])
        w2bc = sb("w2bc", [P, H1])
        bias_n = sb("bias_n", [P, 5 * D])
        brow = O2[1][0:1, :]
        nrow = O2[0][0:1, 0:5 * D]
        rowt = O[0][0:1, 3 * D:3 * D + H1]
        hrow = O[0][0:1, 0:3 * D]
        rhs_n = sb("rhs_n", [P, 5 * D])
        b2c = sb("b2c", [P, 1])

        ps = [ctx.enter_context(nc.psum_tensor(f"ps{k}", [P, 512], F32)) for k in range(8)]
        psT, psH, psE, psC = ps[0:2], ps[2:5], ps[5], ps[6]
        hist = [psT[0], psT[1], ps[7], psH[2]]
        hot = [t[:, :].bitcast(BF16) for t in (V[0], V[1], R[0], R[1])]
        hot_j = [t[:, 0:J] for t in hot]
        w1, w2, w3 = place_v[:, 0:J], place_v[:, J:2 * J], tile_c[:, 0:J]
        hot_p = [[t[:, J + n * P:J + (n + 1) * P] for n in range(4)] for t in hot]
        row4 = [O[0][:, :], O[1][:, :]] + [G[h][:, P:P + B * (D + 2)] for h in range(2)]
        xa4 = [O2[0][:, :], O2[1][:, :]] + [V[h][:, 0:B * D] for h in range(2)]

        pads = sem("pads")
        pool_pads = sem("pool_pads")
        consts = sem("consts")
        ld_dst, ld_src, ld_ew, ld_x = sem("ld_dst"), sem("ld_src"), sem("ld_ew"), sem("ld_x")
        ld_ea, ld_key, ld_w, ld_sorted = sem("ld_ea"), sem("ld_key"), sem("ld_w"), sem("ld_sorted")
        zeroed = sem("zeroed")
        hist_hot = sem("hist_hot")
        hist_scaled = sem("hist_scaled")
        hist_used = sem("hist_used")
        edge_ready = sem("edge_ready")
        edge_stored = sem("edge_stored")
        dv = sem("dv")
        ask = sem("ask")
        given = sem("given")
        sq_ask, sq_given = sem("sq_ask"), sem("sq_given")
        sort_done = sem("sort_done")
        node_ready = sem("node_ready")
        fix_ready = [sem(f"fix_ready{k}") for k in range(4)]
        fix_stored = [sem(f"fix_stored{k}") for k in range(4)]
        w_step = sem("w_step")
        w_copied = sem("w_copied")
        w_bias = sem("w_bias")
        w_done = sem("w_done")
        zset = sem("zset")
        nodes_listed = sem("nodes_listed")
        rhs_zero, e_placed = sem("rhs_zero"), sem("e_placed")
        bn = sem("bn")
        order_sp = sem("order_sp")
        order = sem("order")
        tw_l = sem("tw_l")
        tw_h, tw_p, tw_x, tw_s = sem("tw_h"), sem("tw_p"), sem("tw_x"), [sem(f"tw_s{k}") for k in range(4)]
        ed_staged, ed_g, ed_c = sem("ed_staged"), [sem(f"ed_g{h}") for h in range(2)], sem("ed_c")

        class Sweep:
            def __init__(self, name):
                self.staged = sem(name + "_staged")
                self.g = [sem(f"{name}_g{h}") for h in range(2)]
                self.v = sem(name + "_v")
                self.r = sem(name + "_r")
                self.f = sem(name + "_f")
                self.x = sem(name + "_x")
                self.s = [sem(f"{name}_s{h}") for h in range(2)]

        SW = [Sweep(f"l{k}") for k in range(3)]
        sw_small = sem("sw_small")
        sw_sq = sem("sw_sq")
        sw_w = sem("sw_w")
        nu_staged, nu_g, nu_l = sem("nu_staged"), [sem(f"nu_g{h}") for h in range(2)], [sem(f"nu_l{h}") for h in range(2)]
        nu_d, nu_q, nu_h, nu_s = sem("nu_d"), sem("nu_q"), sem("nu_h"), [sem(f"nu_s{h}") for h in range(2)]
        at_staged, at_g = sem("at_staged"), [sem(f"at_g{h}") for h in range(2)]
        at_ea, at_t, at_c, at_h, at_sc = sem("at_ea"), sem("at_t"), sem("at_c"), sem("at_h"), sem("at_sc")
        at_d, at_e, at_v, at_r, at_f, at_s = sem("at_d"), sem("at_e"), sem("at_v"), sem("at_r"), sem("at_f"), [sem(f"at_s{h}") for h in range(2)]
        nu_o = sem("nu_o")
        fix_listed, fix_g = sem("fix_listed"), sem("fix_g")
        at_den = sem("at_den")
        gr_den = sem("gr_den")
        gr_u = sem("gr_u")
        gr_t, gr_c = sem("gr_t"), sem("gr_c")
        gr_m, gr_p = sem("gr_m"), sem("gr_p")
        gr_sig, gr_n, gr_tanh = sem("gr_sig"), sem("gr_n"), sem("gr_tanh")
        gr_mix, gr_o = sem("gr_mix"), sem("gr_o")
        at_ss = sem("at_ss")
        last_out = sem("last_out")

        C_C, C_IN, C_DEND, C_G0S, C_CS, C_NBC, C_NBG, C_MCI, C_MCO, C_ME, C_X0, C_X1, C_T0, C_T1, C_T2, C_T3, C_E0 = range(17)

        def col(k):
            return cols[:, k:k + 1]

        def at(tile, b, w=1, n=B):
            return tile[:, bass.ds(b * (n * w), n * w)]

        def early(b, n):
            return isinstance(b, int) and b < n

        spot = [0]

        def tiles(count, width):
            first = spot[0]
            spot[0] += count * width
            return [big[:, first + k * width:first + (k + 1) * width] for k in range(count)]

        G4 = tiles(4, 3 * D * B)
        ftG = tiles(2, B * P)
        gates = [g.rearrange("p (i w) -> p i w", w=5 * D) for g in tiles(2, B * 5 * D)]
        hh = [[t[:, i * H1:(i + 1) * H1] for i in range(B)] for t in tiles(2, B * H1)]
        XH = tiles(2, B * P)
        fix_in, fix_cat, fix_out = tiles(1, P)[0], tiles(1, P)[0], tiles(1, D)[0]
        banks = [psE, ps[7], psC]
        psG = [psE, psC]

        def parts(k):
            return [gates[k % 2][:, :, g * D:(g + 1) * D] for g in range(5)]

        def attention_loop(engine, step):
            for s in range(4):
                step(s, s, True, True, s > 0)
            with engine.Fori(1, NB // 4 - 1) as t:
                for k in range(4):
                    step(4 * t + k, k, True, True, True)
            for s in range(NB - 4, NB + 1):
                step(s, s % 4, s < NB - 1, s < NB, True)

        block = ctx.enter_context(nc.Block())

        @block.sync
        def _(sp):
            def load(tile, c0, src_flat, w, s):
                for a, b in ((0, 112), (112, FULL)):
                    sp.dma_start(tile[a:b, c0:c0 + J * w],
                                 src_flat[a * J * w:b * J * w].rearrange("(p j) -> p j", j=J * w)).then_inc(s, 16)
                sp.dma_start(tile[FULL:P, c0:c0 + REST * w],
                             src_flat[FULL * J * w:].rearrange("(p j) -> p j", j=REST * w)).then_inc(s, 16)

            sp.wait_ge(pads, 4)
            sp.dma_start(kx[0:96, :], src[0:96 * 512].rearrange("(p j) -> p j", j=512)).then_inc(ld_key, 16)
            sp.dma_start(kx[96:97, :], src[96 * 512:97 * 512].rearrange("(p j) -> p j", j=512)).then_inc(ld_key, 16)
            sp.dma_start(kx[97:98, 0:E - 97 * 512], src[97 * 512:].rearrange("(p j) -> p j", j=E - 97 * 512)).then_inc(ld_key, 16)
            load(key_d, 1, dst, 1, ld_dst)
            sp.dma_start(key_d[1:P, 0:1], dst[J - 1:FULL * J:J].rearrange("(p a) -> p a", a=1), allow_slow_non_contiguous=True).then_inc(ld_dst, 16)
            sp.dma_start(key_d[0:FULL, J + 1:J + 2], dst[J:FULL * J + 1:J].rearrange("(p a) -> p a", a=1), allow_slow_non_contiguous=True).then_inc(ld_dst, 16)
            load(ew, 0, edge_weight, 1, ld_ew)
            load(src_i, 0, src, 1, ld_src)
            sp.wait_ge(zset, 2)
            for k, (a, b) in enumerate(((0, P), (P, H1))):
                sp.dma_start(wcat[0:b - a, k, 0:D], W_att1[a:b, 0:D]).then_inc(ld_w, 16)
                sp.dma_start(wcat[0:b - a, k, D:P], W_att1[a:b, D + ED:H1]).then_inc(ld_w, 16)
                sp.dma_start(wea[0:b - a, k, :], W_att1[a:b, D:D + ED]).then_inc(ld_w, 16)
            for k, (a, b) in enumerate(((0, P), (P, 3 * D))):
                sp.dma_start(wih[0:b - a, k, :], W_ih[a:b, :]).then_inc(ld_w, 16)
                sp.dma_start(whh[0:b - a, k, :], W_hh[a:b, :]).then_inc(ld_w, 16)
            sp.dma_start(wlin[:, D:P], W_lin).then_inc(ld_w, 16)
            sp.dma_start(bcol[:, :], b_lin.rearrange("(p a) -> p a", a=1)).then_inc(ld_w, 16)
            for t, c, v, n in ((brow, 0, b_ih, 3 * D), (brow, 3 * D, b_hh, 3 * D), (brow, 6 * D, b_lin, D),
                               (b1row, 0, b_att1, H1), (rowt, 0, W_att2.rearrange("a b -> (a b)"), H1),
                               (row2, 2 * P - 1, b_att2, 1)):
                sp.dma_start(t[0:1, c:c + n], v.rearrange("(a n) -> a n", a=1)).then_inc(ld_w, 16)
            sp.wait_ge(pool_pads, 2)
            load(big, 0, x.rearrange("n f -> (n f)"), D, ld_x)
            er = edge_s[:, :].rearrange("p (j w) -> p j w", w=ED + 1)
            for a, b, n in ((0, 112, J), (112, FULL, J), (FULL, P, REST)):
                sp.dma_start(er[a:b, 0:n, 0:ED],
                             edge_attr[a * J:a * J + (b - a) * n, :].rearrange("(p j) f -> p j f", j=n)).then_inc(ld_ea, 16)
            for k in range(3):
                sp.dma_start(t_u[k][ROW_ZERO:ROWS, :], zrow[:, 0:D]).then_inc(zeroed, 16)
            sp.wait_ge(edge_ready, 1)
            sp.dma_start(rows(t_edge), edge_s[:, :]).then_inc(edge_stored, 16)
            sp.wait_ge(sort_done, 1)
            flat = t_sorted.rearrange("n a -> (n a)")
            sp.dma_start(flat.rearrange("(p j) -> p j", j=512), sx[0][:, :].bitcast(I32)).then_inc(ld_sorted, 16)
            sp.wait_ge(ld_sorted, 16)
            sp.dma_start(key_s[:, 1:J + 1], flat[SORT0:].rearrange("(p j) -> p j", j=J)).then_inc(ld_sorted, 16)
            sp.dma_start(key_s[1:P, 0:1], t_sorted[SORT0 + J - 1:SORT - 1:J, :], allow_slow_non_contiguous=True).then_inc(ld_sorted, 16)
            sp.dma_start(key_s[0:P - 1, J + 1:J + 2], t_sorted[SORT0 + J:SORT:J, :], allow_slow_non_contiguous=True).then_inc(ld_sorted, 16)
            sp.wait_ge(w_copied, 3)
            sp.wait_ge(rhs_zero, 1)
            for i in range(B):
                sp.dma_start(rhs_e[i * ED:(i + 1) * ED, i * H1:(i + 1) * H1], w1e[:, :]).then_inc(e_placed, 16)
            h_rows, xa_rows = rows(t_h), rows(t_xa)
            with sp.Fori(0, NB // 4) as t:
                for k in range(4):
                    b = 4 * t + k
                    sp.wait_ge(tw_h, LN_ACT * (b + 1))
                    sp.sem_inc(order_sp, 1)
                    sp.wait_ge(tw_p, b + 1)
                    sp.sem_inc(order_sp, 1)
                    sp.dma_start(at(h_rows, b, D + 2), row4[k]).then_inc(tw_s[k], 16)
                    sp.wait_ge(tw_x, b + 1)
                    sp.sem_inc(order_sp, 1)
                    sp.dma_start(at(xa_rows, b, D), xa4[k]).then_inc(tw_s[k], 16)
            for k in range(3):
                s, u_rows = SW[k], rows(t_u[k])
                with sp.Fori(0, IT) as t:
                    for h in range(2):
                        sp.wait_ge(s.x, 14 + 14 * t + 7 * h + 7)
                        sp.sem_inc(order_sp, 1)
                        sp.dma_start(at(u_rows, 2 * t + h, D), O[h][:, 0:B * D]).then_inc(s.s[h], 16)
                sp.wait_ge(fix_ready[k], 1)
                sp.dma_start(t_u[k][ROW_FIX:ROW_FIX + P, :], fixr[:, 0:D]).then_inc(fix_stored[k], 16)
            xh_rows, h2_rows = rows(t_xh), rows(t_h2)
            out_rows = out[0:FULL * J, :].rearrange("(p j) f -> p (j f)", j=J)
            for h in range(2):
                sp.dma_start(O2[h][:, :], xa_rows[:, h * B * D:(h + 1) * B * D]).then_inc(nu_l[h], 16)

            def nu_store(b, h, last):
                sp.wait_ge(nu_d, 16 * b + 1)
                sp.sem_inc(order_sp, 1)
                if not last:
                    sp.dma_start(O2[h][:, :], at(xa_rows, b + 2, D)).then_inc(nu_l[h], 16)
                sp.wait_ge(nu_h, 7 * b + 7)
                sp.sem_inc(order_sp, 1)
                sp.dma_start(at(xh_rows, b, P), XH[h][:, :]).then_inc(nu_s[h], 16)
                sp.dma_start(at(h2_rows, b, D).rearrange("p (j w) -> p j w", w=D),
                             XH[h][:, :].rearrange("p (j w) -> p j w", w=P)[:, :, D:P]).then_inc(nu_s[h], 16)
                sp.wait_ge(nu_o, b + 1)
                sp.sem_inc(order_sp, 1)
                sp.dma_start(at(out_rows[0:112, :], b, D), O[h][0:112, 0:B * D]).then_inc(nu_s[h], 16)
                sp.dma_start(at(out_rows[112:FULL, :], b, D), O[h][112:FULL, 0:B * D]).then_inc(nu_s[h], 16)
                sp.dma_start(at(t_last, b, D), O[h][FULL:P, 0:B * D]).then_inc(nu_s[h], 16)

            with sp.Fori(0, IT - 1) as t:
                for h in range(2):
                    nu_store(2 * t + h, h, False)
            for h in range(2):
                nu_store(NB - 2 + h, h, True)
            for h in range(2):
                sp.wait_ge(nu_s[h], 80 * IT)
            sp.dma_start(out[FULL * J:N, :].rearrange("(a j) f -> a (j f)", a=1), t_last[:, 0:REST * D]).then_inc(last_out, 16)
            for h in range(2):
                sp.wait_ge(at_s[h], 16 * B * IT)
            sp.wait_ge(fix_stored[3], 16)

        @block.gpsimd
        def _(pool):
            def gather(dst_ap, table, idx, bound, s):
                pool.indirect_dma_start(out=dst_ap, out_offset=None, in_=table,
                                        in_offset=bass.IndirectOffsetOnAxis(ap=idx, axis=0),
                                        bounds_check=bound, oob_is_err=False).then_inc(s, 16)

            def scatter(table, src_ap, idx, bound, s):
                pool.indirect_dma_start(out=table, out_offset=bass.IndirectOffsetOnAxis(ap=idx, axis=0), in_=src_ap,
                                        in_offset=None, bounds_check=bound, oob_is_err=False).then_inc(s, 16)

            pool.memset(ident[:, :], 0.0).then_inc(consts, 1)
            pool.iota(lin_i[:, :], pattern=[[1, 512]], base=0, channel_multiplier=512).then_inc(consts, 1)
            pool.iota(m_all[:, 0:J], pattern=[[1, J]], base=-MID, channel_multiplier=0,
                      allow_small_or_imprecise_dtypes=True).then_inc(consts, 1)
            pool.memset(ones[:, :], 1.0).then_inc(consts, 1)
            pool.wait_ge(consts, 4)
            pool.affine_select(out=ident[:, :], in_=ident[:, :], compare_op=ALU.not_equal, fill=1.0, base=0,
                               pattern=[[-1, P]], channel_multiplier=1).then_inc(consts, 1)
            pool.wait_ge(consts, 5)
            pool.memset(big[96:P, REST * D:J * D], 0.0).then_inc(pool_pads, 1)
            pool.wait_ge(pool_pads, 1)
            pool.memset(edge_s[96:P, REST * (ED + 1):J * (ED + 1)], 0.0).then_inc(pool_pads, 1)

            def edge_part(first, end):
                with pool.Fori(first, end) as t:
                    for h in range(2):
                        pool.wait_ge(ed_staged, 2 * t + h + 1)
                        pool.sem_inc(order, 1)
                        for i in range(B):
                            w = ED + 1
                            gather(G[h][:, w * i:w * i + w], t_edge, st[h][:, i:i + 1], NP - 1, ed_g[h])

            pool.wait_ge(edge_stored, 16)
            pool.wait_ge(w_copied, 9)
            edge_part(0, 10)
            pool.wait_ge(ld_w, 16 * 18)
            pool.partition_broadcast(w2bc[:, :], rowt[0:1, :]).then_inc(w_done, 1)
            pool.partition_broadcast(b2c[:, :], row2[0:1, 2 * P - 1:2 * P]).then_inc(w_done, 1)
            pool.wait_ge(w_bias, 1)
            pool.partition_broadcast(bias_n[:, :], nrow[0:1, :]).then_inc(w_done, 1)
            edge_part(10, IT)
            for k in range(4):
                pool.wait_ge(tw_s[k], 32 * (NB // 4) + 1)
            for k in range(3):
                s = SW[k]
                w = D + 2 if k == 0 else D
                if k:
                    for h in range(2):
                        pool.wait_ge(SW[k - 1].s[h], 16 * IT + 1)
                    pool.wait_ge(fix_stored[k - 1], 16)
                with pool.Fori(0, IT) as t:
                    for h in range(2):
                        pool.wait_ge(s.staged, 2 * t + h + 1)
                        pool.sem_inc(order, 1)
                        for i in range(B):
                            if k == 0:
                                gather(G[h][:, w * i:w * i + w], t_h, st[h][:, i:i + 1], NP - 1, s.g[h])
                            else:
                                gather(G[h][:, w * i:w * i + w], t_u[k - 1], st[h][:, i:i + 1], ROWS - 1, s.g[h])
            for h in range(2):
                pool.wait_ge(SW[2].s[h], 16 * IT + 1)
            pool.wait_ge(fix_stored[2], 16)
            with pool.Fori(0, IT) as t:
                for h in range(2):
                    pool.wait_ge(nu_staged, 2 * t + h + 1)
                    pool.sem_inc(order, 1)
                    for i in range(B):
                        gather(G[h][:, D * i:D * i + D], t_u[2], st[h][:, i:i + 1], ROWS - 1, nu_g[h])

            for h in range(2):
                pool.wait_ge(nu_s[h], 80 * IT)
            pool.wait_ge(last_out, 16)
            pool.wait_ge(fix_listed, 1)
            gather(fix_in[:, :], t_xh, fix_idx[:, :], NP - 1, fix_g)

            def at_gather(b, k):
                h = k % 2
                pool.wait_ge(at_staged, 2 * b + 2)
                pool.sem_inc(order, 1)
                for i in range(B):
                    c = 3 * D * i
                    gather(G4[k][:, c:c + 2 * D], t_xh, st[h][:, i:i + 1], NP - 1, at_g[h])
                    gather(G4[k][:, c + 2 * D:c + 3 * D], t_h2, st[h][:, B + i:B + i + 1], NP - 1, at_g[h])

            def out_scatter(b, k):
                h = k % 2
                pool.wait_ge(at_ss, b + 1)
                pool.sem_inc(order, 1)
                pool.wait_ge(gr_o, b + 1)
                pool.sem_inc(order, 1)
                for i in range(B):
                    scatter(out, O[h][:, i * D:(i + 1) * D], sst[h][:, i:i + 1], N - 1, at_s[h])

            for b in range(4):
                at_gather(b, b)
                if b >= 3:
                    out_scatter(b - 3, b - 3)
            with pool.Fori(1, NB // 4) as t:
                for k in range(4):
                    at_gather(4 * t + k, k)
                    out_scatter(4 * t + k - 3, (k - 3) % 4)
            for b in range(NB - 3, NB):
                out_scatter(b, b % 4)
            pool.wait_ge(fix_ready[3], 1)
            scatter(out, fix_out[:, :], fix_i[:, :], N - 1, fix_stored[3])

        @block.scalar
        def _(act):
            S = nc.scalar

            def stage(b, h, lists, s):
                for k, lst in enumerate(lists):
                    S.copy(st[h][:, k * B:k * B + B], at(lst, b)).then_inc(s, 1)

            act.wait_ge(w_step, 1)
            S.copy(rhs1[:, 0:P], psH[0][:, 0:P]).then_inc(w_copied, 1)
            S.copy(rhs1[:, P:H1], psH[0][:, P:H1]).then_inc(w_copied, 1)
            S.copy(w1e[:, :], psH[1][0:ED, 0:H1]).then_inc(w_copied, 1)
            S.copy(whhT[:, :], psH[2][0:D, 0:3 * D]).then_inc(w_copied, 1)
            S.copy(rhs_n[0:D, 0:3 * D], psE[0:D, 0:3 * D]).then_inc(w_copied, 1)
            act.wait_ge(w_step, 2)
            S.copy(rhs_n[D:P, 0:2 * D], psH[0][D:P, 0:2 * D]).then_inc(w_copied, 1)
            S.activation(rhs_n[D:P, 3 * D:4 * D], psH[0][D:P, 2 * D:3 * D], ACT.Copy, scale=0.5).then_inc(w_copied, 1)
            S.copy(rhs_n[D:P, 4 * D:5 * D], psH[1][D:P, 0:D]).then_inc(w_copied, 1)
            S.copy(hrow[0:1, :], psH[2][0:1, 0:3 * D]).then_inc(w_copied, 1)

            with act.Fori(0, J // 4) as t:
                for k in range(4):
                    c = 4 * t + k
                    act.wait_ge(hist_hot, 10 * t + (2, 5, 7, 10)[k])
                    for n, part in enumerate((w1, w2, w3)[0:2 + k % 2]):
                        S.activation(hot_p[k][1 + n], hot_p[k][0], ACT.Copy,
                                     scale=part[:, bass.ds(c, 1)]).then_inc(hist_scaled, 1)
            act.wait_ge(sq_ask, 1)
            S.activation(tile_d[:, 0:J], tile_b[:, 0:J], ACT.Sqrt).then_inc(sq_given, 1)

            act.wait_ge(node_ready, 1)
            with act.Fori(0, NB // 4) as t:
                for k in range(4):
                    act.wait_ge(tw_s[k], 32 * t + 1)
                    for i in range(LN_ACT):
                        c = (4 * t + k) * B + i
                        S.activation(row4[k][:, i * (D + 2):i * (D + 2) + D], big[:, bass.ds(c * D, D)], ACT.Relu,
                                     bias=shift[:, bass.ds(c, 1)], scale=rstd[:, bass.ds(c, 1)]).then_inc(tw_h, 1)

            act.wait_ge(sq_ask, 2)
            S.activation(tile_d[:, 0:J], tile_b[:, 0:J], ACT.Sqrt).then_inc(sq_given, 1)

            for k in range(3):
                s = SW[k]
                lst = src_i if k == 0 else row_i
                w = D + 2 if k == 0 else D
                if k == 0:
                    for h in range(2):
                        act.wait_ge(ed_g[h], 16 * B * IT)
                    act.wait_ge(ed_c, NB)
                    act.wait_ge(tw_x, NB)
                    act.wait_ge(ld_src, 48)
                S.copy(st[0][:, 0:B], lst[:, 0:B]).then_inc(s.staged, 1)
                S.copy(st[1][:, 0:B], lst[:, B:2 * B]).then_inc(s.staged, 1)
                for h in range(2):
                    act.sem_inc(s.s[h], 1)
                act.sem_inc(s.x, 14)
                with act.Fori(0, IT) as t:
                    for h in range(2):
                        b = 2 * t + h
                        if k == 0:
                            act.wait_ge(sw_small, 4 * b + 1)
                            S.activation(q7[h][1][:, :], q7[h][0][:, :], ACT.Sqrt).then_inc(sw_sq, 1)
                            act.wait_ge(sw_w, b + 1)
                            for i in range(B):
                                c = b * B + i
                                S.activation(big[:, bass.ds(c * D, D)], G[h][:, w * i:w * i + D], ACT.Copy,
                                             scale=w_e[:, bass.ds(c, 1)]).then_inc(s.v, 1)
                        act.wait_ge(s.v, 7 * b + 7)
                        act.wait_ge(s.g[h], 16 * B * (t + 1))
                        S.copy(st[h][:, 0:B], at(lst, b + 2)).then_inc(s.staged, 1)
                        act.wait_ge(s.s[h], 16 * t + 1)
                        for i in range(B):
                            c = b * B + i
                            act.wait_ge(s.r, 7 * b + i + 2)
                            S.activation(O[h][:, D * i:D * i + D], R[h][:, D * i:D * i + D], ACT.Copy,
                                         scale=dinv[:, bass.ds(c, 1)]).then_inc(s.x, 1)
                act.wait_ge(s.staged, NB + 2)

            act.wait_ge(nodes_listed, 1)
            S.copy(st[0][:, 0:B], node_i[:, 0:B]).then_inc(nu_staged, 1)
            S.copy(st[1][:, 0:B], node_i[:, B:2 * B]).then_inc(nu_staged, 1)
            with act.Fori(0, IT) as t:
                for h in range(2):
                    b = 2 * t + h
                    act.wait_ge(nu_d, 16 * b + 1)
                    act.wait_ge(nu_g[h], 16 * B * (t + 1))
                    S.copy(st[h][:, 0:B], at(node_i, b + 2)).then_inc(nu_staged, 1)
                    act.wait_ge(nu_d, 16 * b + 14)
                    S.activation(q7[h][5][:, :], q7[h][4][:, :], ACT.Sqrt).then_inc(nu_q, 1)
                    act.wait_ge(nu_d, 16 * b + 16)
                    for i in range(B):
                        S.activation(XH[h][:, P * i + D:P * i + P], XH[h][:, P * i:P * i + D], ACT.Relu,
                                     bias=q7[h][1][:, i:i + 1], scale=q7[h][0][:, i:i + 1]).then_inc(nu_h, 1)

            def stage_at(b, h):
                for k, lst in enumerate((srcs_i, dsts_i)):
                    S.copy(st[h][:, k * B:k * B + B], at(lst, b)).then_inc(at_staged, 1)

            act.wait_ge(at_d, 1)
            act.wait_ge(nu_staged, NB + 2)
            for h in range(2):
                act.wait_ge(nu_g[h], 16 * B * IT)
                stage_at(h, h)

            def messages(b, k):
                h, w = k % 2, D + 1
                act.wait_ge(gr_den, b + 1)
                for i in range(B):
                    S.activation(G4[k][:, i * 3 * D + 2 * D:(i + 1) * 3 * D], R[h][:, i * w:i * w + D], ACT.Copy,
                                 scale=q7[h][2][:, i:i + 1]).then_inc(gr_u, 1)
                act.wait_ge(gr_t, 2 * b + 1)
                S.copy(ftG[h][:, 0:512], psG[0][:, :]).then_inc(gr_c, 1)
                act.wait_ge(gr_t, 2 * b + 2)
                S.copy(ftG[h][:, 512:B * P], psG[1][:, 0:B * P - 512]).then_inc(gr_c, 1)

            def features(b, k):
                h = k % 2
                ea = at(edge_s, b, ED + 1).rearrange("p (j w) -> p j w", w=ED + 1)[:, :, 0:ED]
                S.copy(ea7[h][:, :].rearrange("p (j w) -> p j w", w=ED), ea).then_inc(at_ea, 1)
                act.wait_ge(at_t, 2 * b + 1)
                S.copy(ftS[h][:, 0:512], psT[0][:, :]).then_inc(at_c, 1)
                act.wait_ge(at_t, 2 * b + 2)
                S.copy(ftS[h][:, 512:B * P], psT[1][:, 0:B * P - 512]).then_inc(at_c, 1)
                S.copy(eaT[h][:, :], psT[1][0:B * ED, 3 * P:4 * P]).then_inc(at_c, 1)

            def factors(b, k):
                h = k % 2
                act.wait_ge(at_d, 6 * b + 7)
                S.activation(e14[h][:, :], q14[h][:, :], ACT.Exp).then_inc(at_e, 1)
                act.wait_ge(at_e, b + 1)
                for i in range(B):
                    S.activation(V[h][:, i * (D + 1):i * (D + 1) + D], G4[k][:, i * 3 * D + 2 * D:(i + 1) * 3 * D],
                                 ACT.Copy, scale=e14[h][:, B + i:B + i + 1]).then_inc(at_v, 1)

            def attention_step(s, k, after, now, before):
                kb = (k - 1) % 4
                if before:
                    messages(s - 1, kb)
                if now:
                    h = k % 2
                    act.wait_ge(at_g[h], 16 * B * (s + 2 - h))
                    if not early(s, 2):
                        act.wait_ge(gr_o, s - 1)
                    stage_at(s + 2, h)
                if before:
                    rz = gates[kb % 2][:, :, 0:2 * D]
                    act.wait_ge(gr_p, 7 * s + 7)
                    S.activation(rz, rz, ACT.Tanh, scale=0.5).then_inc(gr_sig, 1)
                if after:
                    features(s + 1, (k + 1) % 4)
                if now:
                    factors(s, k)
                if before:
                    n = parts(kb)[2]
                    act.wait_ge(gr_n, 2 * s)
                    S.activation(n, n, ACT.Tanh).then_inc(gr_tanh, 1)
                    hb = kb % 2
                    if not early(s, 3):
                        act.wait_ge(at_s[hb], 8 * B * (s - 1 - hb))
                    S.copy(sst[hb][:, :], at(scat_i, s - 1)).then_inc(at_ss, 1)

            features(0, 0)
            attention_loop(act, attention_step)
            act.wait_ge(sq_ask, 3)
            S.activation(cols[:, C_E0:C_E0 + 4], cols[:, C_T0:C_T0 + 4], ACT.Exp).then_inc(sq_given, 1)

            act.wait_ge(sq_ask, 4)
            S.activation(gates[0][:, 0, 0:2 * D], gates[0][:, 0, 0:2 * D], ACT.Tanh, scale=0.5).then_inc(sq_given, 1)
            act.wait_ge(sq_ask, 5)
            S.activation(gates[0][:, 0, 2 * D:3 * D], gates[0][:, 0, 2 * D:3 * D], ACT.Tanh).then_inc(sq_given, 1)

        @block.tensor
        def _(pe):
            T = nc.tensor
            turn = [0]

            def asked():
                turn[0] += 1
                pe.wait_ge(ask, turn[0])

            pe.wait_ge(consts, 5)
            pe.wait_ge(ld_w, 16 * 18)
            pe.wait_ge(pads, 5)
            T.transpose(psH[0][:, 0:P], wcat[:, 0, :], ident[:, :])
            T.transpose(psH[0][:, P:H1], wcat[0:H1 - P, 1, :], ident[0:H1 - P, 0:H1 - P])
            T.transpose(psH[1][0:ED, 0:P], wea[:, 0, :], ident[:, :])
            T.transpose(psH[1][0:ED, P:H1], wea[0:H1 - P, 1, :], ident[0:H1 - P, 0:H1 - P])
            T.transpose(psH[2][0:D, 0:P], whh[:, 0, :], ident[:, :])
            T.transpose(psH[2][0:D, P:3 * D], whh[0:D, 1, :], ident[0:D, 0:D])
            T.transpose(psE[0:D, 0:P], wih[:, 0, :], ident[:, :])
            T.transpose(psE[0:D, P:3 * D], wih[0:D, 1, :], ident[0:D, 0:D]).then_inc(w_step, 1)
            pe.wait_ge(w_copied, 5)
            T.matmul(psH[0][:, 0:3 * D], wlin[:, :], whhT[:, :], start=True, stop=True)
            T.matmul(psH[1][:, 0:D], wlin[:, :], ident[0:D, 0:D], start=True, stop=True)
            T.matmul(psH[2][0:1, 0:3 * D], bcol[:, :], whhT[:, :], start=True, stop=True).then_inc(w_step, 1)

            for k in range(14):
                asked()
                for c in range(4):
                    mm = T.transpose(psC[:, c * P:(c + 1) * P], sx[k % 2][:, c * P:(c + 1) * P], ident[:, :])
                mm.then_inc(given, 1)
            asked()
            T.transpose(psC[0:1, 0:P], tile_d[:, J - 1:J], ident[:, :])
            T.transpose(psC[0:1, P:2 * P], col(C_C), ident[:, :]).then_inc(given, 1)
            asked()
            T.transpose(psC[:, 2 * P:2 * P + 1], row1[0:1, 0:P], ident[0:1, 0:1]).then_inc(given, 1)
            asked()
            T.transpose(psC[0:D + 1, 0:P], cbc[:, :], ident[:, :]).then_inc(given, 1)

            pe.wait_ge(w_copied, 9)
            pe.sem_inc(hist_used, 4)

            def histogram(t, k):
                c = 4 * t + k
                pe.wait_ge(hist_hot, 10 * t + (3, 5, 8, 10)[k])
                pe.wait_ge(hist_scaled, 10 * t + (2, 5, 7, 10)[k])
                for n in range(4):
                    mm = T.matmul(hist[n][:, 0:J], hot_p[k][n], hot_j[k], start=isinstance(c, int) and c == 0,
                                  stop=isinstance(c, int) and c == J - 1)
                mm.then_inc(hist_used, 1)

            for k in range(4):
                histogram(0, k)
            with pe.Fori(1, J // 4 - 1) as t:
                for k in range(4):
                    histogram(t, k)
            for k in range(4):
                histogram(J // 4 - 1, k)
            asked()
            T.transpose(psC[0:1, 0:P], tile_d[:, J - 1:J], ident[:, :]).then_inc(given, 1)
            asked()
            T.transpose(psC[:, 2 * P:2 * P + 1], row1[0:1, 0:P], ident[0:1, 0:1]).then_inc(given, 1)

            for k in range(3):
                asked()
                T.transpose(psC[0:D, 0:P], R[1][:, (B - 1) * D:B * D], ident[:, :]).then_inc(given, 1)
                asked()
                T.transpose(psC[:, P:P + D], co[0:D, 0:P], ident[0:D, 0:D]).then_inc(given, 1)

            pe.wait_ge(w_copied, 9)
            pe.wait_ge(e_placed, 16 * B)

            def layer_one(b, k):
                h = k % 2
                pe.wait_ge(at_g[h], 16 * B * (b + 2 - h))
                if not early(b, 1):
                    pe.wait_ge(at_c, 3 * b)
                for i in range(B):
                    mm = T.transpose(psT[i // 4][:, (i % 4) * P:(i % 4 + 1) * P], G4[k][:, i * 3 * D + D:(i + 1) * 3 * D],
                                     ident[:, :])
                    if i == 3:
                        mm.then_inc(at_t, 1)
                pe.wait_ge(at_ea, b + 1)
                T.transpose(psT[1][0:B * ED, 3 * P:4 * P], ea7[h][:, :], ident[:, :]).then_inc(at_t, 1)
                pe.wait_ge(at_c, 3 * b + 3)
                for i in range(B):
                    o = psH[i // 3][:, (i % 3) * H1:(i % 3 + 1) * H1]
                    if i % 3 == 0:
                        pe.wait_ge(at_sc, 7 * b + min(i + 3, B))
                    T.matmul(o, ftS[h][:, i * P:(i + 1) * P], rhs1[:, :], start=True, stop=False)
                    T.matmul(o, eaT[h][:, :], rhs_e[:, i * H1:(i + 1) * H1], start=False, stop=False)
                    T.matmul(o, ones[0:1, :], b1row[:, :], start=False, stop=True).then_inc(at_h, 1)

            def gru_products(b, k):
                pe.wait_ge(gr_u, 7 * b + 7)
                pe.wait_ge(gr_p, 7 * b + 7)
                for i in range(B):
                    mm = T.transpose(psG[i // 4][:, (i % 4) * P:(i % 4 + 1) * P], G4[k][:, i * 3 * D + D:(i + 1) * 3 * D],
                                     ident[:, :])
                    if i in (3, B - 1):
                        mm.then_inc(gr_t, 1)
                for i in range(B):
                    if i in (0, 2):
                        pe.wait_ge(gr_c, 2 * b + 1 + i // 2)
                    if i >= 3:
                        pe.wait_ge(gr_p, 7 * b + i + 5)
                    T.matmul(banks[i % 3][:, 0:5 * D], ftG[k % 2][:, i * P:(i + 1) * P], rhs_n[:, :],
                             start=True, stop=True).then_inc(gr_m, 1)

            def attention_step(s, k, after, now, before):
                if before:
                    gru_products(s - 1, (k - 1) % 4)
                if after:
                    layer_one(s + 1, (k + 1) % 4)

            layer_one(0, 0)
            attention_loop(pe, attention_step)
            asked()
            T.transpose(psC[0:1, 0:P], m_all[:, J:J + 1], ident[:, :])
            T.transpose(psC[0:1, P:2 * P], col(C_NBC), ident[:, :]).then_inc(given, 1)
            asked()
            T.transpose(psC[:, 2 * P:2 * P + 1], row1[0:1, 0:P], ident[0:1, 0:1])
            T.transpose(psC[:, 2 * P + 1:2 * P + 2], row1[0:1, 1:P + 1], ident[0:1, 0:1]).then_inc(given, 1)
            asked()
            T.transpose(psC[0:D + 1, 0:P], V[0][:, 0:D + 1], ident[:, :])
            T.transpose(psC[0:D + 1, P:2 * P], cbc[:, :], ident[:, :]).then_inc(given, 1)
            asked()
            T.transpose(psC[:, 2 * P:2 * P + D + 1], co[:, 0:P], ident[0:D + 1, 0:D + 1]).then_inc(given, 1)

            asked()
            T.transpose(psC[:, 0:P], fix_cat[:, :], ident[:, :]).then_inc(given, 1)
            asked()
            T.matmul(psE[:, 0:5 * D], ftG[0][:, 0:P], rhs_n[:, :], start=True, stop=True).then_inc(given, 1)

        @block.vector
        def _(dve):
            v = nc.vector
            steps = [0]
            turn = [0]

            def link(ins):
                steps[0] += 1
                ins.then_inc(dv, 1)
                dve.wait_ge(dv, steps[0])

            def exchange():
                turn[0] += 1
                dve.sem_inc(ask, 1)
                dve.wait_ge(given, turn[0])

            ta, tb, tc, td = tile_a[:, 0:J], tile_b[:, 0:J], tile_c[:, 0:J], tile_d[:, 0:J]

            v.memset(kx[:, :], PAD_KEY).then_inc(pads, 1)
            v.memset(key_d[:, :], PAD_KEY).then_inc(pads, 1)
            v.memset(ew[:, :], 0.0).then_inc(pads, 1)
            v.memset(src_i[:, :], 0).then_inc(pads, 1)
            pl = place_v[:, :].rearrange("p (j w) -> p j w", w=2)
            v.memset(zrow[:, :], 0.0).then_inc(zset, 1)
            v.memset(wlin[:, :], 0.0).then_inc(zset, 1)
            link(v.memset(rhs_n[:, :], 0.0))
            v.memset(rhs_e[:, :], 0.0).then_inc(rhs_zero, 1)
            for lst in (row_i, srcs_i, dsts_i, perm_i, scat_i):
                link(v.memset(lst[:, J:J + 2 * B], 0))
            link(v.memset(row1[:, 0:1], 0.0))
            link(v.memset(co[:, 0:1], 0.0))
            dve.sem_inc(pads, 1)

            def runs(key, end):
                link(v.tensor_tensor(ta, key[:, 1:J + 1], key[:, 0:J], ALU.not_equal))
                link(v.tensor_tensor(tb, key[:, 1:J + 1], key[:, 2:J + 2], ALU.not_equal))
                link(v.tensor_copy(tc[:, 1:J], ta[:, 1:J]))
                link(v.memset(tc[:, 0:1], 0.0))
                link(v.tensor_tensor_scan(td, tc, tc, 0.0, ALU.max, ALU.max))
                link(v.tensor_scalar(tc, td, -1.0, 1.0, ALU.mult, ALU.add))
                link(v.tensor_tensor(end, tc, tb, ALU.mult))

            er = edge_s[:, :].rearrange("p (j w) -> p j w", w=ED + 1)

            def split(x, q, r, t, q_i):
                link(v.tensor_scalar(q_i, x, 1.0 / J, None, ALU.mult))
                link(v.tensor_copy(q, q_i))
                link(v.scalar_tensor_tensor(out=r, in0=q, scalar=-float(J), in1=x, op0=ALU.mult, op1=ALU.add))
                link(v.tensor_scalar(t, r, 0.0, None, ALU.is_lt))
                link(v.tensor_tensor(q, q, t, ALU.subtract))
                link(v.scalar_tensor_tensor(out=r, in0=t, scalar=float(J), in1=r, op0=ALU.mult, op1=ALU.add))
                link(v.tensor_scalar(t, r, float(J), None, ALU.is_ge))
                link(v.tensor_tensor(q, q, t, ALU.add))
                link(v.scalar_tensor_tensor(out=r, in0=t, scalar=-float(J), in1=r, op0=ALU.mult, op1=ALU.add))

            def edge_begin():
                for h in range(2):
                    v.tensor_copy(st[h][:, 0:B], perm_i[:, h * B:(h + 1) * B]).then_inc(ed_staged, 1)

            def edge_row(b, h, more):
                dve.wait_ge(ed_g[h], 8 * B * (b + 2 - h))
                v.tensor_copy(at(edge_s, b, ED + 1), G[h][:, 0:B * (ED + 1)]).then_inc(ed_c, 1)
                if more:
                    dve.wait_ge(ed_c, b + 1)
                    v.tensor_copy(st[h][:, 0:B], at(perm_i, b + 2)).then_inc(ed_staged, 1)

            cur = [0]
            lin, u0, u1 = lin_i[:, :], sx[0][:, :].bitcast(U32), sx[1][:, :].bitcast(U32)
            dve.wait_ge(ld_key, 48)
            dve.wait_ge(consts, 5)
            link(v.tensor_scalar(sx[1][:, :].bitcast(I32), kx[:, :], 32512.0, 256.0, ALU.is_ge, ALU.mult))
            link(v.scalar_tensor_tensor(out=sx[0][:, :].bitcast(I32), in0=kx[:, :], scalar=128.0,
                                        in1=sx[1][:, :].bitcast(I32), op0=ALU.add, op1=ALU.add))
            link(v.tensor_scalar(u1, u0, 16, None, ALU.logical_shift_left))
            link(v.tensor_tensor(u0, u1, lin, ALU.bitwise_or))
            link(v.tensor_scalar(mask[:, :], lin, 1, None, ALU.logical_shift_right))
            link(v.tensor_tensor(gray[:, :], lin, mask[:, :], ALU.bitwise_xor))

            def flip(k):
                s, d = (sx[cur[0]][:, :].bitcast(U32), sx[1 - cur[0]][:, :].bitcast(U32))
                link(v.tensor_scalar(mask[:, :], (gray if k else lin_i)[:, :], 31 - max(k, 1), 0x80000000,
                                     ALU.logical_shift_left, ALU.bitwise_and))
                link(v.tensor_tensor(d, s, mask[:, :], ALU.bitwise_xor))
                cur[0] ^= 1

            def compare(bit):
                a = sx[cur[0]][:, :].rearrange("p (a t s) -> p a t s", t=2, s=1 << bit)
                o = sx[1 - cur[0]][:, :].rearrange("p (a t s) -> p a t s", t=2, s=1 << bit)
                steps[0] += 2
                v.tensor_tensor(o[:, :, 0, :], a[:, :, 0, :], a[:, :, 1, :], ALU.min).then_inc(dv, 1)
                v.tensor_tensor(o[:, :, 1, :], a[:, :, 0, :], a[:, :, 1, :], ALU.max).then_inc(dv, 1)
                dve.wait_ge(dv, steps[0])
                cur[0] ^= 1

            swaps = [0]

            def swap():
                k = swaps[0] % 2
                if cur[0] != k:
                    link(v.tensor_copy(sx[k][:, :], sx[1 - k][:, :]))
                    cur[0] = k
                exchange()
                link(v.tensor_copy(sx[1 - k][:, :], psC[:, :]))
                cur[0] ^= 1
                swaps[0] += 1

            flip(0)
            for k in range(1, 17):
                low = k - 1
                if k == 12:
                    dve.wait_ge(ld_ea, 48)
                    dve.wait_ge(pool_pads, 2)
                    dve.wait_ge(ld_dst, 80)
                    link(v.tensor_copy(er[:, :, ED], key_d[:, 1:J + 1]))
                    dve.sem_inc(edge_ready, 1)
                if k >= 10:
                    swap()
                    for bit in range(k - 1, 6, -1):
                        compare(bit - 9 if bit >= 9 else bit)
                    swap()
                    low = 6
                for bit in range(low, -1, -1):
                    compare(bit)
                if k < 16:
                    flip(k)
            if cur[0]:
                link(v.tensor_copy(sx[0][:, :], sx[1][:, :]))
            link(v.memset(key_s[:, :], 0))
            dve.sem_inc(sort_done, 1)

            dve.wait_ge(ld_dst, 80)
            dve.wait_ge(consts, 5)
            runs(key_d, end_d[:, :])
            link(v.tensor_scalar(keep_d[:, :], ta, -1.0, 1.0, ALU.mult, ALU.add))
            link(v.tensor_tensor(col(C_C), tc[:, J - 1:J], keep_d[:, 0:1], ALU.mult))
            dve.wait_ge(ld_sorted, 64)
            packed = key_s[:, :].bitcast(U32)
            hi, lo = tile_a[:, :].bitcast(U32), tile_b[:, :].bitcast(U32)
            link(v.tensor_scalar(hi, packed, 16, None, ALU.logical_shift_right))
            link(v.tensor_scalar(lo, packed, 0xFFFF, None, ALU.bitwise_and))
            link(v.tensor_scalar(perm_i[:, 0:J], lo[:, 1:J + 1], float(E), None, ALU.min))
            edge_begin()
            link(v.tensor_scalar(tile_d[:, :], hi, 32768.0, -256.0, ALU.is_ge, ALU.mult))
            link(v.scalar_tensor_tensor(out=key_s[:, :], in0=hi, scalar=-128.0, in1=tile_d[:, :], op0=ALU.add, op1=ALU.add))
            dve.wait_ge(ld_ew, 48)
            link(v.tensor_tensor_scan(td, keep_d[:, :], ew[:, :], 0.0, ALU.mult, ALU.add))
            exchange()
            link(v.tensor_copy(row2[0:1, 0:P], psC[0:1, P:2 * P]))
            link(v.tensor_tensor_scan(row1[:, 1:P + 1], row2[0:1, 0:P], psC[0:1, 0:P], 0.0, ALU.mult, ALU.add))
            exchange()
            link(v.tensor_tensor(col(C_IN), psC[:, 2 * P:2 * P + 1], keep_d[:, 0:1], ALU.mult))
            link(v.scalar_tensor_tensor(out=dinv[:, :], in0=tc, scalar=col(C_IN), in1=td, op0=ALU.mult, op1=ALU.add))
            link(v.tensor_scalar(cbc[:, :], ones[:, 0:D + 1], col(C_C), None, ALU.mult))
            exchange()
            link(v.tensor_copy(cT[:, :], psC[0:D + 1, 0:P]))

            link(v.tensor_copy(ta, key_d[:, 1:J + 1]))
            split(ta, tb, tc, td, srcs_i[:, 0:J])
            link(v.tensor_scalar(p_e, tb, -float(MID), None, ALU.add))
            link(v.tensor_scalar(j_e, tc, -float(MID), None, ALU.add))

            dve.wait_ge(w_copied, 9)
            link(v.tensor_copy(nrow[0:1, 0:3 * D], brow[0:1, 0:3 * D]))
            link(v.tensor_tensor(hrow[0:1, :], hrow[0:1, :], brow[0:1, 3 * D:6 * D], ALU.add))
            link(v.tensor_tensor(nrow[0:1, 0:2 * D], nrow[0:1, 0:2 * D], hrow[0:1, 0:2 * D], ALU.add))
            link(v.tensor_scalar(nrow[0:1, 3 * D:4 * D], hrow[0:1, 2 * D:3 * D], 0.5, None, ALU.mult))
            link(v.tensor_copy(nrow[0:1, 4 * D:5 * D], brow[0:1, 6 * D:7 * D]))
            dve.sem_inc(w_bias, 1)

            bf = tile_a[:, :].bitcast(BF16)[:, 0:J]
            link(v.tensor_copy(bf, ew[:, :]))
            link(v.tensor_copy(w1, bf))
            link(v.tensor_tensor(tb, ew[:, :], w1, ALU.subtract))
            link(v.tensor_copy(bf, tb))
            link(v.tensor_copy(w2, bf))
            link(v.tensor_tensor(w3, tb, w2, ALU.subtract))
            link(v.tensor_copy(iota_b, m_all[:, 0:J]))
            dve.wait_ge(ld_x, 48)
            dve.wait_ge(zeroed, 48)
            with dve.Fori(0, J // 56) as t:
                for e in range(6):
                    for i in range(e * 56 // 6, (e + 1) * 56 // 6):
                        c, k = 56 * t + i, i % 4
                        dve.wait_ge(hist_used, c + 1)
                        p_c, j_c = p_e[:, bass.ds(c, 1)], j_e[:, bass.ds(c, 1)]
                        v.tensor_scalar(hot_j[k], iota_b, j_c, None, ALU.is_equal).then_inc(hist_hot, 1)
                        v.tensor_scalar(hot_p[k][0], iota_b[:, 0:P], p_c, None, ALU.is_equal).then_inc(hist_hot, 1)
                        if k % 2 == 0:
                            v.tensor_scalar(hot_p[k][3], iota_b[:, 0:P], p_c, w3[:, bass.ds(c, 1)], ALU.is_equal,
                                            ALU.mult).then_inc(hist_hot, 1)
                        v.bn_stats(stats[:, bass.ds(c * 6, 6)], big[:, bass.ds(c * D, D)]).then_inc(bn, 1)
                    edge_row(6 * t + e, e % 2, True)
            dve.wait_ge(hist_used, J + 4)
            dve.wait_ge(bn, J)
            link(v.tensor_copy(tb, hist[0][:, 0:J]))
            link(v.tensor_copy(tc, hist[3][:, 0:J]))
            link(v.tensor_tensor(tc, tc, hist[2][:, 0:J], ALU.add))
            link(v.tensor_tensor(pl[:, :, 1], tc, hist[1][:, 0:J], ALU.add))
            edge_row(NB - 14, 0, True)
            link(v.tensor_tensor_scan(td, tb, tb, 0.0, ALU.add, ALU.max))
            exchange()
            link(v.tensor_copy(row2[0:1, 0:P], psC[0:1, 0:P]))
            link(v.tensor_tensor_scan(row1[:, 1:P + 1], row2[0:1, 0:P], row2[0:1, 0:P], 0.0, ALU.add, ALU.max))
            exchange()
            link(v.tensor_copy(col(C_IN), psC[:, 2 * P:2 * P + 1]))
            link(v.tensor_scalar(ta, td, col(C_IN), -1.0, ALU.add, ALU.add))
            split(ta, j_e, tc, td, dsts_i[:, 0:J])
            edge_row(NB - 13, 1, True)
            link(v.tensor_tensor(tc, tb, tc, ALU.subtract))
            link(v.tensor_scalar(tc, tc, 1.0, None, ALU.is_gt))
            link(v.tensor_tensor(td, j_e, ta, ALU.subtract))
            link(v.tensor_scalar(td, td, float(ROW_FIX), None, ALU.add))
            link(v.tensor_tensor(td, td, tc, ALU.mult))
            link(v.tensor_tensor(ta, ta, td, ALU.add))
            link(v.tensor_scalar(tb, tb, 0.0, None, ALU.is_gt))
            link(v.tensor_scalar(ta, ta, -float(ROW_ZERO), None, ALU.add))
            link(v.tensor_tensor(ta, ta, tb, ALU.mult))
            link(v.tensor_scalar(pl[:, :, 0], ta, float(ROW_ZERO), None, ALU.add))

            def norm(s6, s, d, q, var, between):
                between(v.tensor_tensor(s, s6[:, :, 1], s6[:, :, 4], ALU.add))
                between(v.tensor_tensor(d, s6[:, :, 1], s6[:, :, 4], ALU.subtract))
                between(v.tensor_tensor(q, s6[:, :, 2], s6[:, :, 5], ALU.add))
                between(v.tensor_tensor(d, d, d, ALU.mult))
                between(v.tensor_scalar(q, q, 1.0 / D, EPS, ALU.mult, ALU.add))
                between(v.scalar_tensor_tensor(out=var, in0=d, scalar=0.25, in1=q, op0=ALU.mult, op1=ALU.add))

            edge_row(NB - 12, 0, True)
            norm(stats.rearrange("p (j w) -> p j w", w=6), ta, tb, tc, tb, link)
            dve.sem_inc(sq_ask, 1)
            dve.wait_ge(sq_given, 1)
            link(v.reciprocal(rstd[:, :], td))
            link(v.scalar_tensor_tensor(out=shift[:, 0:J], in0=ta, scalar=-0.5, in1=rstd[:, :], op0=ALU.mult, op1=ALU.mult))

            edge_row(NB - 11, 1, True)

            dve.wait_ge(w_done, 3)
            for k in range(4):
                dve.sem_inc(tw_s[k], 1)
            dve.sem_inc(node_ready, 1)

            def node_share(q, k):
                b = 4 * q + k
                rows_h = row4[k].rearrange("p (i w) -> p i w", w=D + 2)
                dve.wait_ge(tw_s[k], 32 * q + 1)
                v.tensor_copy(rows_h[:, :, D:D + 2], at(place_v, b, 2).rearrange("p (i w) -> p i w", w=2)).then_inc(tw_l, 1)
                for i in range(LN_ACT, B):
                    c = b * B + i
                    v.tensor_scalar(rows_h[:, i, 0:D], big[:, bass.ds(c * D, D)], rstd[:, bass.ds(c, 1)],
                                    shift[:, bass.ds(c, 1)], ALU.mult, ALU.add).then_inc(tw_l, 1)
                dve.wait_ge(tw_l, (1 + B - LN_ACT) * (b + 1))
                v.tensor_scalar(rows_h[:, LN_ACT:B, 0:D], rows_h[:, LN_ACT:B, 0:D], 0.0, None, ALU.max).then_inc(tw_p, 1)

            def node_xa(q, k):
                b = 4 * q + k
                rows_h = row4[k].rearrange("p (i w) -> p i w", w=D + 2)
                dve.wait_ge(tw_p, b + 1)
                dve.wait_ge(tw_h, LN_ACT * (b + 1))
                v.scalar_tensor_tensor(out=xa4[k].rearrange("p (i w) -> p i w", w=D), in0=rows_h[:, :, 0:D],
                                       scalar=0.25, in1=at(big, b, D).rearrange("p (i w) -> p i w", w=D),
                                       op0=ALU.mult, op1=ALU.add).then_inc(tw_x, 1)

            def node_rows(t, edges, more, last=False):
                for e in range(2):
                    for k in range(4):
                        if not (last and e == 1 and k == 3):
                            node_share(2 * t + e + (k + 1) // 4, (k + 1) % 4)
                        node_xa(2 * t + e, k)
                    if edges:
                        edge_row(NB - 10 + 2 * t + e, e, more)

            node_share(0, 0)
            with dve.Fori(0, 4) as t:
                node_rows(t, True, True)
            node_rows(4, True, False)
            with dve.Fori(5, NB // 8 - 1) as t:
                node_rows(t, False, False)
            node_rows(NB // 8 - 1, False, False, last=True)

            link(v.tensor_scalar(tb, dinv[:, :], TINY, None, ALU.max))
            dve.sem_inc(sq_ask, 1)
            dve.wait_ge(sq_given, 2)
            link(v.reciprocal(ta, td))
            link(v.scalar_tensor_tensor(out=dinv[:, :], in0=dinv[:, :], scalar=0.0, in1=ta, op0=ALU.is_gt, op1=ALU.mult))
            link(v.scalar_tensor_tensor(out=ta, in0=end_d[:, :], scalar=1.0, in1=dinv[:, :], op0=ALU.mult, op1=ALU.mult,
                                        accum_out=col(C_DEND)))

            def src_lists():
                link(v.tensor_scalar(srcs_i[:, 0:J], key_s[:, 1:J + 1], float(NP - 1), None, ALU.min))
                runs(key_s, end_s[:, :])
                link(v.tensor_scalar(start_s[:, :], ta, -BIG, None, ALU.mult))
                link(v.tensor_scalar(col(C_G0S), ta[:, 0:1], -1.0, 1.0, ALU.mult, ALU.add))
                link(v.tensor_tensor(col(C_CS), tc[:, J - 1:J], col(C_G0S), ALU.mult))
                link(v.tensor_scalar(col(C_NBC), col(C_CS), BIG, -BIG, ALU.mult, ALU.add))
                link(v.tensor_scalar(col(C_NBG), col(C_G0S), BIG, -BIG, ALU.mult, ALU.add))
                link(v.tensor_tensor(tb, tb, end_s[:, :], ALU.subtract))
                link(v.tensor_scalar(td, tb, -OOB, OOB, ALU.mult, ALU.add))
                link(v.tensor_tensor(td, td, key_s[:, 1:J + 1], ALU.add))
                link(v.scalar_tensor_tensor(out=ta, in0=end_s[:, :], scalar=1.0, in1=key_s[:, 1:J + 1], op0=ALU.mult,
                                            op1=ALU.mult, accum_out=col(C_X0)))
                link(v.scalar_tensor_tensor(out=ta, in0=end_s[:, :], scalar=1.0, in1=end_s[:, :], op0=ALU.mult,
                                            op1=ALU.mult, accum_out=col(C_X1)))
                link(v.tensor_scalar(col(C_X1), col(C_X1), -OOB, OOB, ALU.mult, ALU.add))
                link(v.tensor_tensor(fix_i[:, :], col(C_X0), col(C_X1), ALU.add))
                link(v.tensor_copy(scat_i[:, 0:J], td))

            for k in range(3):
                s = SW[k]
                w = D + 2 if k == 0 else D
                if k == 1:
                    dve.wait_ge(zeroed, 48)
                if k:
                    dve.wait_ge(SW[k - 1].x, 14 + J)
                else:
                    dve.wait_ge(tw_x, NB)
                v.memset(R[1][:, (B - 1) * D:B * D], 0.0).then_inc(s.r, 1)
                v.memset(F[:, :], 0.0).then_inc(s.f, 1)
                with dve.Fori(0, IT) as t:
                    for h in range(2):
                        b = 2 * t + h
                        dve.wait_ge(s.g[h], 16 * B * (t + 1))
                        if k == 0:
                            gv = G[h][:, 0:B * w].rearrange("p (i w) -> p i w", w=w)
                            v.tensor_scalar(q7[h][0][:, :], gv[:, :, D + 1], TINY, None, ALU.max).then_inc(sw_small, 1)
                            v.tensor_copy(at(row_i, b), gv[:, :, D]).then_inc(sw_small, 1)
                            v.scalar_tensor_tensor(out=q7[h][2][:, :], in0=gv[:, :, D + 1], scalar=0.0, in1=at(ew, b),
                                                   op0=ALU.is_gt, op1=ALU.mult).then_inc(sw_small, 1)
                            dve.wait_ge(sw_sq, b + 1)
                            v.reciprocal(q7[h][3][:, :], q7[h][1][:, :]).then_inc(sw_small, 1)
                            dve.wait_ge(sw_small, 4 * b + 4)
                            v.tensor_tensor(at(w_e, b), q7[h][2][:, :], q7[h][3][:, :], ALU.mult).then_inc(sw_w, 1)
                        else:
                            wb = at(w_e, b).unsqueeze(2).to_broadcast([P, B, D])
                            vv = V[h][:, 0:B * D].rearrange("p (i w) -> p i w", w=D)
                            v.tensor_tensor(vv, G[h][:, 0:B * D].rearrange("p (i w) -> p i w", w=D), wb,
                                            ALU.mult).then_inc(sw_small, 1)
                            dve.wait_ge(sw_small, 4 * NB + (k - 1) * NB + b + 1)
                            v.tensor_tensor(V[h][:, 0:B * D], V[h][:, 0:B * D], at(big, b, D), ALU.add).then_inc(s.v, B)
                        dve.wait_ge(s.x, 14 * t + 7 * h + 7)

                        def finish(i):
                            c = b * B + i
                            dve.wait_ge(s.r, c + 2)
                            dve.wait_ge(s.f, c + 1)
                            v.scalar_tensor_tensor(out=F[:, 0:D], in0=R[h][:, i * D:(i + 1) * D],
                                                   scalar=end_d[:, bass.ds(c, 1)], in1=F[:, 0:D], op0=ALU.mult,
                                                   op1=ALU.add).then_inc(s.f, 1)

                        for i in range(B):
                            c = b * B + i
                            prev = R[h][:, (i - 1) * D:i * D] if i else R[1 - h][:, (B - 1) * D:B * D]
                            new = V[h][:, i * D:(i + 1) * D] if k else big[:, bass.ds(c * D, D)]
                            dve.wait_ge(s.v, c + 1 if k == 0 else 7 * b + 7)
                            dve.wait_ge(s.r, c + 1)
                            v.scalar_tensor_tensor(out=R[h][:, i * D:(i + 1) * D], in0=prev,
                                                   scalar=keep_d[:, bass.ds(c, 1)], in1=new, op0=ALU.mult,
                                                   op1=ALU.add).then_inc(s.r, 1)
                            if i:
                                finish(i - 1)
                        finish(B - 1)
                dve.wait_ge(s.r, J + 1)
                dve.wait_ge(s.f, J + 1)
                exchange()
                link(v.tensor_tensor_scan(co[0:D, 1:P + 1], cT[0:D, :], psC[0:D, 0:P], 0.0, ALU.mult, ALU.add))
                exchange()
                if k:
                    dve.wait_ge(fix_stored[k - 1], 16)
                link(v.scalar_tensor_tensor(out=fixr[:, 0:D], in0=psC[:, P:P + D], scalar=keep_d[:, 0:1], in1=F[:, 0:D],
                                            op0=ALU.mult, op1=ALU.add))
                link(v.tensor_scalar(fixr[:, 0:D], fixr[:, 0:D], col(C_DEND), None, ALU.mult))
                dve.sem_inc(fix_ready[k], 1)
                if k == 0:
                    src_lists()

            dve.wait_ge(SW[2].x, 14 + J)
            nv = place_v[:, :].rearrange("p (j w) -> p j w", w=2)
            link(v.tensor_copy(node_i[:, 0:J], nv[:, :, 0]))
            dve.sem_inc(nodes_listed, 1)
            v.tensor_scalar(fix_idx[:, :], fix_i[:, :], float(NP - 1), None, ALU.min).then_inc(fix_listed, 1)

            def defaults(b, h):
                dve.wait_ge(nu_h, 7 * b + 7)
                xh = XH[h][:, :].rearrange("p (i w) -> p i w", w=P)
                v.tensor_tensor(O[h][:, 0:B * D].rearrange("p (i w) -> p i w", w=D), xh[:, :, 0:D], xh[:, :, D:P],
                                ALU.add).then_inc(nu_o, 1)

            def nu_step(b, h, first):
                dve.wait_ge(nu_g[h], 8 * B * (b + 2 - h))
                dve.wait_ge(nu_l[h], 8 * (b + 2 - h))
                if not early(b, 2):
                    dve.wait_ge(nu_s[h], 40 * (b - h))
                count = [0]

                def step(ins):
                    count[0] += 1
                    ins.then_inc(nu_d, 1)
                    dve.wait_ge(nu_d, 16 * b + count[0])

                x2 = XH[h][:, :].rearrange("p (i w) -> p i w", w=P)[:, :, 0:D]
                step(v.scalar_tensor_tensor(out=x2, in0=G[h][:, 0:B * D].rearrange("p (i w) -> p i w", w=D), scalar=0.25,
                                            in1=O2[h][:, :].rearrange("p (i w) -> p i w", w=D), op0=ALU.mult, op1=ALU.add))
                for i in range(B):
                    v.bn_stats(st6[h][:, i * 6:(i + 1) * 6], XH[h][:, i * P:i * P + D]).then_inc(nu_d, 1)
                count[0] += B
                dve.wait_ge(nu_d, 16 * b + count[0])
                q = q7[h]
                norm(st6[h][:, :].rearrange("p (i w) -> p i w", w=6), q[2][:, :], q[3][:, :], q[0][:, :], q[4][:, :], step)
                if not first:
                    defaults(b - 1, 1 - h)
                dve.wait_ge(nu_q, b + 1)
                step(v.reciprocal(q[0][:, :], q[5][:, :]))
                step(v.scalar_tensor_tensor(out=q[1][:, :], in0=q[2][:, :], scalar=-0.5, in1=q[0][:, :],
                                            op0=ALU.mult, op1=ALU.mult))

            for h in range(2):
                nu_step(h, h, h == 0)
            with dve.Fori(1, IT) as t:
                for h in range(2):
                    nu_step(2 * t + h, h, False)
            defaults(NB - 1, 1)

            dve.wait_ge(ed_c, NB)
            dve.wait_ge(nu_o, NB)
            for h in range(2):
                dve.wait_ge(nu_s[h], 80 * IT)
            link(v.memset(F[:, :], 0.0))
            link(v.memset(m_all[:, 0:1], -BIG))
            v.memset(R[1][:, (B - 1) * (D + 1):B * (D + 1)], 0.0).then_inc(at_r, 1)
            v.tensor_scalar(dsts_i[:, 0:J], er[:, :, ED], float(NP - 1), None, ALU.min).then_inc(at_d, 1)
            dve.sem_inc(at_sc, 7)
            dve.wait_ge(w_done, 2)
            dve.wait_ge(pads, 5)

            def scores(b, k):
                h = k % 2
                for i in range(B):
                    if i % 3 == 0:
                        dve.wait_ge(at_h, 7 * b + min(i + 3, B))
                    v.scalar_tensor_tensor(out=hh[h][i], in0=psH[i // 3][:, (i % 3) * H1:(i % 3 + 1) * H1],
                                           scalar=0.0, in1=w2bc[:, :], op0=ALU.max, op1=ALU.mult,
                                           accum_out=score[h][:, i:i + 1]).then_inc(at_sc, 1)

            def maxima(b, k):
                h = k % 2
                dve.wait_ge(at_sc, 7 * b + 14)
                count = [1]

                def step(ins):
                    count[0] += 1
                    ins.then_inc(at_d, 1)
                    dve.wait_ge(at_d, 6 * b + count[0])

                sc, mp = q7[h][0][:, :], q7[h][1][:, :]
                m_new, m_old = m_all[:, bass.ds(b * B + 1, B)], at(m_all, b)
                step(v.tensor_scalar(sc, score[h][:, :], b2c[:, 0:1], None, ALU.add))
                step(v.tensor_tensor_scan(m_new, at(start_s, b), sc, m_all[:, bass.ds(b * B, 1)], ALU.add, ALU.max))
                step(v.tensor_tensor(mp, at(start_s, b), m_old, ALU.add))
                step(v.tensor_tensor(q14[h][:, 0:B], mp, m_new, ALU.subtract))
                step(v.tensor_tensor(q14[h][:, B:2 * B], sc, m_new, ALU.subtract))
                step(v.tensor_scalar(q14[h][:, :], q14[h][:, :], EXP_MIN, None, ALU.max))

            def running_sums(b, k):
                h, w = k % 2, D + 1
                dve.wait_ge(at_e, b + 1)
                vv = V[h][:, :].rearrange("p (i w) -> p i w", w=w)
                v.tensor_copy(vv[:, :, D], e14[h][:, B:2 * B]).then_inc(at_den, 1)
                dve.wait_ge(at_den, b + 1)
                if not early(b, 2):
                    dve.wait_ge(gr_u, 7 * (b - 1))

                def finish(i):
                    c = b * B + i
                    dve.wait_ge(at_r, c + 2)
                    if not early(c, 1):
                        dve.wait_ge(at_f, c)
                    v.scalar_tensor_tensor(out=F[:, :], in0=R[h][:, i * w:(i + 1) * w],
                                           scalar=end_s[:, bass.ds(c, 1)], in1=F[:, :], op0=ALU.mult,
                                           op1=ALU.add).then_inc(at_f, 1)

                for i in range(B):
                    c = b * B + i
                    prev = R[h][:, (i - 1) * w:i * w] if i else R[1 - h][:, (B - 1) * w:B * w]
                    dve.wait_ge(at_v, c + 1)
                    dve.wait_ge(at_r, c + 1)
                    v.scalar_tensor_tensor(out=R[h][:, i * w:(i + 1) * w], in0=prev, scalar=e14[h][:, i:i + 1],
                                           in1=V[h][:, i * w:(i + 1) * w], op0=ALU.mult,
                                           op1=ALU.add).then_inc(at_r, 1)
                    if i:
                        finish(i - 1)
                finish(B - 1)
                den = R[h][:, :].rearrange("p (i w) -> p i w", w=w)[:, :, D]
                v.reciprocal(q7[h][2][:, :], den).then_inc(gr_den, 1)

            def evacuate(b, k):
                for i in range(B):
                    dve.wait_ge(gr_m, 7 * b + i + 1)
                    v.tensor_tensor(gates[k % 2][:, i, :], banks[i % 3][:, 0:5 * D], bias_n[:, :],
                                    ALU.add).then_inc(gr_p, 1)

            def reset_gate(b, k):
                r, z, n, hn, m = parts(k)
                dve.wait_ge(gr_sig, b + 1)
                v.scalar_tensor_tensor(out=hn, in0=r, scalar=1.0, in1=hn, op0=ALU.add, op1=ALU.mult).then_inc(gr_n, 1)
                dve.wait_ge(gr_n, 2 * b + 1)
                v.tensor_tensor(n, n, hn, ALU.add).then_inc(gr_n, 1)

            def new_rows(b, k):
                r, z, n, hn, m = parts(k)
                x2 = G4[k][:, :].rearrange("p (i w) -> p i w", w=3 * D)[:, :, 0:D]
                dve.wait_ge(gr_tanh, b + 1)
                v.tensor_tensor(m, m, n, ALU.subtract).then_inc(gr_mix, 1)
                dve.wait_ge(gr_mix, 3 * b + 1)
                v.scalar_tensor_tensor(out=m, in0=z, scalar=1.0, in1=m, op0=ALU.add, op1=ALU.mult).then_inc(gr_mix, 1)
                v.tensor_tensor(n, n, x2, ALU.add).then_inc(gr_mix, 1)
                dve.wait_ge(gr_mix, 3 * b + 3)
                if not early(b, 2):
                    dve.wait_ge(at_s[k % 2], 8 * B * (b - k % 2))
                v.scalar_tensor_tensor(out=O[k % 2][:, 0:B * D].rearrange("p (i w) -> p i w", w=D), in0=m, scalar=0.5,
                                       in1=n, op0=ALU.mult, op1=ALU.add).then_inc(gr_o, 1)

            def attention_step(s, k, after, now, before):
                kb = (k - 1) % 4
                if now:
                    scores(s, k)
                if before:
                    evacuate(s - 1, kb)
                if now:
                    maxima(s, k)
                if before:
                    reset_gate(s - 1, kb)
                if now:
                    running_sums(s, k)
                if before:
                    new_rows(s - 1, kb)

            dve.wait_ge(w_done, 3)
            dve.sem_inc(gr_p, 7)
            attention_loop(dve, attention_step)
            dve.wait_ge(at_r, J + 1)
            dve.wait_ge(at_f, J)
            link(v.memset(row1[:, 0:1], -BIG))
            exchange()
            link(v.tensor_copy(row2[0:1, 0:P], psC[0:1, P:2 * P]))
            link(v.tensor_tensor_scan(row1[:, 1:P + 1], row2[0:1, 0:P], psC[0:1, 0:P], -BIG, ALU.add, ALU.max))
            exchange()
            link(v.tensor_copy(cols[:, C_MCI:C_MCI + 2], psC[:, 2 * P:2 * P + 2]))
            link(v.scalar_tensor_tensor(out=ta, in0=end_s[:, :], scalar=1.0, in1=m_all[:, 1:J + 1], op0=ALU.mult,
                                        op1=ALU.mult, accum_out=col(C_ME)))
            link(v.tensor_tensor(col(C_X0), col(C_MCI), col(C_NBG), ALU.add))
            link(v.tensor_tensor(col(C_X1), col(C_ME), col(C_X0), ALU.max))
            link(v.tensor_tensor(col(C_T0), col(C_MCI), col(C_MCO), ALU.subtract))
            link(v.tensor_tensor(col(C_T1), m_all[:, J:J + 1], col(C_MCO), ALU.subtract))
            link(v.tensor_tensor(col(C_T2), col(C_X0), col(C_X1), ALU.subtract))
            link(v.tensor_tensor(col(C_T3), col(C_ME), col(C_X1), ALU.subtract))
            link(v.tensor_scalar(cols[:, C_T0:C_T0 + 4], cols[:, C_T0:C_T0 + 4], EXP_MIN, 0.0, ALU.max, ALU.min))
            dve.sem_inc(sq_ask, 1)
            dve.wait_ge(sq_given, 3)
            link(v.tensor_tensor(col(C_X0), col(C_CS), col(C_E0), ALU.mult))
            link(v.tensor_scalar(cbc[:, :], ones[:, 0:D + 1], col(C_X0), None, ALU.mult))
            link(v.tensor_scalar(V[0][:, 0:D + 1], R[1][:, (B - 1) * (D + 1):B * (D + 1)], col(C_E0 + 1), None, ALU.mult))
            exchange()
            link(v.tensor_copy(cT[:, :], psC[0:D + 1, P:2 * P]))
            link(v.tensor_tensor_scan(co[:, 1:P + 1], cT[:, :], psC[0:D + 1, 0:P], 0.0, ALU.mult, ALU.add))
            exchange()
            dve.wait_ge(fix_stored[2], 16)
            link(v.tensor_scalar(F[:, :], F[:, :], col(C_E0 + 3), None, ALU.mult))
            link(v.scalar_tensor_tensor(out=fixr[:, :], in0=psC[:, 2 * P:2 * P + D + 1], scalar=col(C_E0 + 2),
                                        in1=F[:, :], op0=ALU.mult, op1=ALU.add))

            dve.wait_ge(fix_g, 16)
            link(v.tensor_copy(fix_cat[:, 0:D], fix_in[:, D:P]))
            link(v.tensor_scalar(col(C_X0), fixr[:, D:D + 1], 0.5, None, ALU.max))
            link(v.reciprocal(col(C_X1), col(C_X0)))
            link(v.tensor_scalar(fix_cat[:, D:P], fixr[:, 0:D], col(C_X1), None, ALU.mult))
            exchange()
            link(v.tensor_copy(ftG[0][:, 0:P], psC[:, 0:P]))
            exchange()
            g = gates[0][:, 0, :]
            link(v.tensor_tensor(g, psE[:, 0:5 * D], bias_n[:, :], ALU.add))
            dve.sem_inc(sq_ask, 1)
            dve.wait_ge(sq_given, 4)
            r, z, n, hn, m = (g[:, c * D:(c + 1) * D] for c in range(5))
            link(v.scalar_tensor_tensor(out=hn, in0=r, scalar=1.0, in1=hn, op0=ALU.add, op1=ALU.mult))
            link(v.tensor_tensor(n, n, hn, ALU.add))
            dve.sem_inc(sq_ask, 1)
            dve.wait_ge(sq_given, 5)
            link(v.tensor_tensor(m, m, n, ALU.subtract))
            link(v.scalar_tensor_tensor(out=m, in0=z, scalar=1.0, in1=m, op0=ALU.add, op1=ALU.mult))
            link(v.tensor_tensor(n, n, fix_in[:, 0:D], ALU.add))
            v.scalar_tensor_tensor(out=fix_out[:, :], in0=m, scalar=0.5, in1=n, op0=ALU.mult,
                                   op1=ALU.add).then_inc(fix_ready[3], 1)


_INS = ["x", "src", "dst", "edge_attr_16", "edge_weight", "L1_gnn_W_att1", "L1_gnn_b_att1", "L1_gnn_W_att2",
        "L1_gnn_b_att2", "L1_gnn_W_lin", "L1_gnn_b_lin", "L1_gnn_W_ih", "L1_gnn_b_ih", "L1_gnn_W_hh", "L1_gnn_b_hh"]


def kernel(**inputs):
    import numpy as _np
    import concourse.bacc as _bacc
    from concourse import mybir as _mybir
    from concourse.bass_utils import run_bass_kernel_spmd as _run

    nc = _bacc.Bacc("TRN2", target_bir_lowering=False, num_devices=1)
    arrays, args = {}, []
    for name in _INS:
        a = _np.ascontiguousarray(inputs[name])
        arrays[f"in_{name}_dram"] = a
        args.append(nc.dram_tensor(f"in_{name}_dram", a.shape, _mybir.dt.from_np(a.dtype), kind="ExternalInput").ap())
    out = nc.dram_tensor("out_0_dram", (N, D), F32, kind="ExternalOutput").ap()
    build(nc, *args, out)
    r = _run(nc, [arrays], core_ids=[0])
    return r.results[0]["out_0_dram"]
```
